# Optimizing a Trainium2 kernel written in Bass

```python
import numpy as np
import jax
import jax.numpy as jnp

def _softmax(x, axis=-1):
    return jax.nn.softmax(x, axis=axis)

def _gelu(x):
    return jax.nn.gelu(x, approximate=True)

def _silu(x):
    return jax.nn.silu(x)

def _sigmoid(x):
    return jax.nn.sigmoid(x)

def _layernorm(x, axis=-1, eps=1e-05):
    m = jnp.mean(x, axis=axis, keepdims=True)
    v = jnp.var(x, axis=axis, keepdims=True)
    return (x - m) / jnp.sqrt(v + eps)

def _scatter_add(tgt, idx, src, axis=0):
    return tgt.at[idx].add(src)

def _segment_sum(src, seg, n):
    return jax.ops.segment_sum(src, seg, n)
kernel_name = 'mk_vit_tower_d1_tok_img256_r4_15c676'

def setup_inputs(seed: int=0):
    np.random.seed(seed)
    _w = jnp.asarray

    def _rec_inputs():
        import jax
        import jax.numpy as jnp
        _rk = jax.random.key(seed)
        x = -0.000125008 + 0.999885 * jax.random.normal(jax.random.fold_in(_rk, 1), (32, 64, 64, 64), jnp.float32)
        return x
    x = _rec_inputs()

    def _L0_tok_setup():
        import jax, jax.numpy as jnp
        import numpy as np
        B, C, H, W = (32, 64, 64, 64)
        STRIDE, HEADS = (4, 8)

        def _ln(x, w, b):
            mu = x.mean(-1, keepdims=True)
            var = ((x - mu) ** 2).mean(-1, keepdims=True)
            return (x - mu) * jax.lax.rsqrt(var + 1e-05) * w + b
        key = jax.random.key(seed)
        ks = jax.random.split(key, 4)
        return {'features': jax.random.normal(ks[0], (B, C, H, W), dtype=jnp.float32), 'ln_q_w': jnp.ones((C,), jnp.float32), 'ln_q_b': jnp.zeros((C,), jnp.float32), 'Wq': jax.random.normal(ks[1], (C, C), dtype=jnp.float32) * 0.02, 'ln_kv_w': jnp.ones((C,), jnp.float32), 'ln_kv_b': jnp.zeros((C,), jnp.float32), 'Wkv': jax.random.normal(ks[2], (2 * C, C), dtype=jnp.float32) * 0.02, 'proj_w': jax.random.normal(ks[3], (C, C), dtype=jnp.float32) * 0.02, 'proj_b': jnp.zeros((C,), jnp.float32), 'conv_stride': STRIDE, 'num_heads': HEADS}
    _L0_tok_all = _L0_tok_setup()
    _L0_tok_in = {k: v for k, v in _L0_tok_all.items() if k in ('ln_q_w', 'ln_q_b', 'Wq', 'ln_kv_w', 'ln_kv_b', 'Wkv', 'proj_w', 'proj_b')}
    del _L0_tok_all

    def _L0_attn_setup():
        import jax, jax.numpy as jnp
        import numpy as np
        B_, L_, D_ = (4, 1024, 64)
        EXPAND = 2
        DI_ = EXPAND * D_
        H_ = 8
        P_ = DI_ // H_
        N_ = 16
        K_ = 3

        def _layernorm(x, w, b):
            m = x.mean(-1, keepdims=True)
            v = ((x - m) ** 2).mean(-1, keepdims=True)
            return (x - m) * jax.lax.rsqrt(v + 1e-05) * w + b

        def _mh_ssm(x, in_w, in_b, xp_w, xp_b, dt_b, A_log, D_skip, out_w, out_b):
            Bsz, L, _ = x.shape
            xz = x @ in_w.T + in_b
            xi, z = jnp.split(xz, 2, axis=-1)
            xi = jax.nn.silu(xi)
            proj = xi @ xp_w.T + xp_b
            dt = jax.nn.softplus(proj[..., :DI_] + dt_b)
            Bm = proj[..., DI_:DI_ + H_ * N_].reshape(Bsz, L, H_, N_)
            Cm = proj[..., DI_ + H_ * N_:].reshape(Bsz, L, H_, N_)
            A = -jnp.exp(A_log).reshape(H_, P_, N_)
            x4 = xi.reshape(Bsz, L, H_, P_)
            dt4 = dt.reshape(Bsz, L, H_, P_)

            def step(h, t):
                xt, dtt, Bt, Ct = t
                dA = jnp.exp(dtt[..., None] * A)
                h = h * dA + dtt[..., None] * Bt[:, :, None, :] * xt[..., None]
                y = jnp.einsum('bhpn,bhn->bhp', h, Ct)
                return (h, y)
            xs = (x4.transpose(1, 0, 2, 3), dt4.transpose(1, 0, 2, 3), Bm.transpose(1, 0, 2, 3), Cm.transpose(1, 0, 2, 3))
            h0 = jnp.zeros((Bsz, H_, P_, N_), x.dtype)
            _, ys = jax.lax.scan(step, h0, xs)
            y = ys.transpose(1, 0, 2, 3).reshape(Bsz, L, DI_) + xi * D_skip
            y = y * jax.nn.silu(z)
            return y @ out_w.T + out_b
        key = jax.random.key(seed)
        ks = jax.random.split(key, 32)

        def n(i, shape, s=0.02):
            return jax.random.normal(ks[i], shape, jnp.float32) * s
        inp = {'inputs': jax.random.normal(ks[0], (B_, L_, D_), jnp.float32)}
        i = 1
        for pre in ('f_', 'b_'):
            inp[pre + 'in_proj_w'] = n(i, (2 * DI_, D_))
            i += 1
            inp[pre + 'in_proj_b'] = jnp.zeros((2 * DI_,), jnp.float32)
            inp[pre + 'x_proj_w'] = n(i, (DI_ + 2 * H_ * N_, DI_))
            i += 1
            inp[pre + 'x_proj_b'] = jnp.zeros((DI_ + 2 * H_ * N_,), jnp.float32)
            inp[pre + 'dt_bias'] = jnp.full((DI_,), -4.0, jnp.float32)
            inp[pre + 'A_log'] = jnp.log(jnp.tile(jnp.arange(1, N_ + 1, dtype=jnp.float32), (DI_, 1)))
            inp[pre + 'D_skip'] = jnp.ones((DI_,), jnp.float32)
            inp[pre + 'out_proj_w'] = n(i, (D_, DI_))
            i += 1
            inp[pre + 'out_proj_b'] = jnp.zeros((D_,), jnp.float32)
        inp['norm_w'] = jnp.ones((D_,), jnp.float32)
        inp['norm_b'] = jnp.zeros((D_,), jnp.float32)
        inp['conv_w'] = n(20, (D_, 1, K_), 0.1)
        inp['conv_b'] = jnp.zeros((D_,), jnp.float32)
        return inp
    _L0_attn_all = _L0_attn_setup()
    _L0_attn_in = {k: v for k, v in _L0_attn_all.items() if k in ('f_in_proj_w', 'f_in_proj_b', 'f_x_proj_w', 'f_x_proj_b', 'f_dt_bias', 'f_A_log', 'f_D_skip', 'f_out_proj_w', 'f_out_proj_b', 'b_in_proj_w', 'b_in_proj_b', 'b_x_proj_w', 'b_x_proj_b', 'b_dt_bias', 'b_A_log', 'b_D_skip', 'b_out_proj_w', 'b_out_proj_b', 'norm_w', 'norm_b', 'conv_w', 'conv_b')}
    del _L0_attn_all

    def _L0_ffn_setup():
        import jax, jax.numpy as jnp
        import numpy as np
        D_MODEL = 64
        N_EXPERTS = 16
        HIDDEN = 128
        SCALE = 0.02
        key = jax.random.key(seed)
        ks = jax.random.split(key, 5)
        x = jax.random.normal(ks[0], (4, 2048, D_MODEL), dtype=jnp.float32)
        gate_w = jax.random.normal(ks[1], (D_MODEL, N_EXPERTS), dtype=jnp.float32) * SCALE
        gate_b = jnp.zeros((N_EXPERTS,), dtype=jnp.float32)
        w1 = jax.random.normal(ks[2], (N_EXPERTS, D_MODEL, HIDDEN), dtype=jnp.float32) * SCALE
        w2 = jax.random.normal(ks[3], (N_EXPERTS, D_MODEL, HIDDEN), dtype=jnp.float32) * SCALE
        w3 = jax.random.normal(ks[4], (N_EXPERTS, HIDDEN, D_MODEL), dtype=jnp.float32) * SCALE
        return {'x': x, 'gate_w': gate_w, 'gate_b': gate_b, 'w1': w1, 'w2': w2, 'w3': w3}
    _L0_ffn_all = _L0_ffn_setup()
    _L0_ffn_in = {k: v for k, v in _L0_ffn_all.items() if k in ('gate_w', 'gate_b', 'w1', 'w2', 'w3')}
    del _L0_ffn_all
    return {'x': x, 'L0_tok_ln_q_w': _L0_tok_in['ln_q_w'], 'L0_tok_ln_q_b': _L0_tok_in['ln_q_b'], 'L0_tok_Wq': _L0_tok_in['Wq'], 'L0_tok_ln_kv_w': _L0_tok_in['ln_kv_w'], 'L0_tok_ln_kv_b': _L0_tok_in['ln_kv_b'], 'L0_tok_Wkv': _L0_tok_in['Wkv'], 'L0_tok_proj_w': _L0_tok_in['proj_w'], 'L0_tok_proj_b': _L0_tok_in['proj_b'], 'L0_attn_f_in_proj_w': _L0_attn_in['f_in_proj_w'], 'L0_attn_f_in_proj_b': _L0_attn_in['f_in_proj_b'], 'L0_attn_f_x_proj_w': _L0_attn_in['f_x_proj_w'], 'L0_attn_f_x_proj_b': _L0_attn_in['f_x_proj_b'], 'L0_attn_f_dt_bias': _L0_attn_in['f_dt_bias'], 'L0_attn_f_A_log': _L0_attn_in['f_A_log'], 'L0_attn_f_D_skip': _L0_attn_in['f_D_skip'], 'L0_attn_f_out_proj_w': _L0_attn_in['f_out_proj_w'], 'L0_attn_f_out_proj_b': _L0_attn_in['f_out_proj_b'], 'L0_attn_b_in_proj_w': _L0_attn_in['b_in_proj_w'], 'L0_attn_b_in_proj_b': _L0_attn_in['b_in_proj_b'], 'L0_attn_b_x_proj_w': _L0_attn_in['b_x_proj_w'], 'L0_attn_b_x_proj_b': _L0_attn_in['b_x_proj_b'], 'L0_attn_b_dt_bias': _L0_attn_in['b_dt_bias'], 'L0_attn_b_A_log': _L0_attn_in['b_A_log'], 'L0_attn_b_D_skip': _L0_attn_in['b_D_skip'], 'L0_attn_b_out_proj_w': _L0_attn_in['b_out_proj_w'], 'L0_attn_b_out_proj_b': _L0_attn_in['b_out_proj_b'], 'L0_attn_norm_w': _L0_attn_in['norm_w'], 'L0_attn_norm_b': _L0_attn_in['norm_b'], 'L0_attn_conv_w': _L0_attn_in['conv_w'], 'L0_attn_conv_b': _L0_attn_in['conv_b'], 'L0_ffn_gate_w': _L0_ffn_in['gate_w'], 'L0_ffn_gate_b': _L0_ffn_in['gate_b'], 'L0_ffn_w1': _L0_ffn_in['w1'], 'L0_ffn_w2': _L0_ffn_in['w2'], 'L0_ffn_w3': _L0_ffn_in['w3']}

def reference(x, L0_tok_ln_q_w, L0_tok_ln_q_b, L0_tok_Wq, L0_tok_ln_kv_w, L0_tok_ln_kv_b, L0_tok_Wkv, L0_tok_proj_w, L0_tok_proj_b, L0_attn_f_in_proj_w, L0_attn_f_in_proj_b, L0_attn_f_x_proj_w, L0_attn_f_x_proj_b, L0_attn_f_dt_bias, L0_attn_f_A_log, L0_attn_f_D_skip, L0_attn_f_out_proj_w, L0_attn_f_out_proj_b, L0_attn_b_in_proj_w, L0_attn_b_in_proj_b, L0_attn_b_x_proj_w, L0_attn_b_x_proj_b, L0_attn_b_dt_bias, L0_attn_b_A_log, L0_attn_b_D_skip, L0_attn_b_out_proj_w, L0_attn_b_out_proj_b, L0_attn_norm_w, L0_attn_norm_b, L0_attn_conv_w, L0_attn_conv_b, L0_ffn_gate_w, L0_ffn_gate_b, L0_ffn_w1, L0_ffn_w2, L0_ffn_w3):
    import jax
    import jax.numpy as jnp

    def _L0_tok_ref(features, ln_q_w, ln_q_b, Wq, ln_kv_w, ln_kv_b, Wkv, proj_w, proj_b, conv_stride, num_heads):
        import jax, jax.numpy as jnp
        import numpy as np
        B, C, H, W = (32, 64, 64, 64)
        STRIDE, HEADS = (4, 8)

        def _ln(x, w, b):
            mu = x.mean(-1, keepdims=True)
            var = ((x - mu) ** 2).mean(-1, keepdims=True)
            return (x - mu) * jax.lax.rsqrt(var + 1e-05) * w + b
        s = conv_stride
        b, c, hh, ww = features.shape
        h, w = (hh // s, ww // s)
        hw, n, d = (h * w, s * s, c // num_heads)
        scale = c ** (-0.5)
        x = features.reshape(b, c, h, s, w, s)
        reduce_feats = x.mean((3, 5)).reshape(b, c, hw).transpose(0, 2, 1)
        unf = x.transpose(0, 1, 2, 4, 3, 5).reshape(b, c, hw, n).transpose(0, 2, 3, 1)
        q = _ln(reduce_feats, ln_q_w, ln_q_b) @ Wq.T
        q = q.reshape(b, hw, num_heads, d).transpose(0, 2, 1, 3)
        kv = _ln(unf, ln_kv_w, ln_kv_b) @ Wkv.T
        kv = kv.reshape(b, hw, n, 2, num_heads, d).transpose(3, 0, 4, 1, 2, 5)
        k, v = (kv[0], kv[1])
        attn = jax.nn.softmax(jnp.einsum('bhpd,bhpnd->bhpn', q * scale, k), axis=-1)
        aggre = jnp.einsum('bhpn,bhpnd->bhpd', attn, v)
        aggre = aggre.transpose(0, 2, 1, 3).reshape(b, hw, c)
        return reduce_feats + aggre @ proj_w.T + proj_b

    def _L0_attn_ref(inputs, f_in_proj_w, f_in_proj_b, f_x_proj_w, f_x_proj_b, f_dt_bias, f_A_log, f_D_skip, f_out_proj_w, f_out_proj_b, b_in_proj_w, b_in_proj_b, b_x_proj_w, b_x_proj_b, b_dt_bias, b_A_log, b_D_skip, b_out_proj_w, b_out_proj_b, norm_w, norm_b, conv_w, conv_b):
        import jax, jax.numpy as jnp
        import numpy as np
        B_, L_, D_ = (4, 1024, 64)
        EXPAND = 2
        DI_ = EXPAND * D_
        H_ = 8
        P_ = DI_ // H_
        N_ = 16
        K_ = 3

        def _layernorm(x, w, b):
            m = x.mean(-1, keepdims=True)
            v = ((x - m) ** 2).mean(-1, keepdims=True)
            return (x - m) * jax.lax.rsqrt(v + 1e-05) * w + b

        def _mh_ssm(x, in_w, in_b, xp_w, xp_b, dt_b, A_log, D_skip, out_w, out_b):
            Bsz, L, _ = x.shape
            xz = x @ in_w.T + in_b
            xi, z = jnp.split(xz, 2, axis=-1)
            xi = jax.nn.silu(xi)
            proj = xi @ xp_w.T + xp_b
            dt = jax.nn.softplus(proj[..., :DI_] + dt_b)
            Bm = proj[..., DI_:DI_ + H_ * N_].reshape(Bsz, L, H_, N_)
            Cm = proj[..., DI_ + H_ * N_:].reshape(Bsz, L, H_, N_)
            A = -jnp.exp(A_log).reshape(H_, P_, N_)
            x4 = xi.reshape(Bsz, L, H_, P_)
            dt4 = dt.reshape(Bsz, L, H_, P_)

            def step(h, t):
                xt, dtt, Bt, Ct = t
                dA = jnp.exp(dtt[..., None] * A)
                h = h * dA + dtt[..., None] * Bt[:, :, None, :] * xt[..., None]
                y = jnp.einsum('bhpn,bhn->bhp', h, Ct)
                return (h, y)
            xs = (x4.transpose(1, 0, 2, 3), dt4.transpose(1, 0, 2, 3), Bm.transpose(1, 0, 2, 3), Cm.transpose(1, 0, 2, 3))
            h0 = jnp.zeros((Bsz, H_, P_, N_), x.dtype)
            _, ys = jax.lax.scan(step, h0, xs)
            y = ys.transpose(1, 0, 2, 3).reshape(Bsz, L, DI_) + xi * D_skip
            y = y * jax.nn.silu(z)
            return y @ out_w.T + out_b
        y1 = _mh_ssm(inputs, f_in_proj_w, f_in_proj_b, f_x_proj_w, f_x_proj_b, f_dt_bias, f_A_log, f_D_skip, f_out_proj_w, f_out_proj_b)
        y1n = jnp.flip(_layernorm(y1, norm_w, norm_b), axis=1)
        y2 = _mh_ssm(y1n, b_in_proj_w, b_in_proj_b, b_x_proj_w, b_x_proj_b, b_dt_bias, b_A_log, b_D_skip, b_out_proj_w, b_out_proj_b)
        out = jnp.flip(y2, axis=1)
        xt = inputs.transpose(0, 2, 1)
        c = jax.lax.conv_general_dilated(xt, conv_w, window_strides=(1,), padding=[(1, 1)], dimension_numbers=('NCH', 'OIH', 'NCH'), feature_group_count=D_)
        c = jax.nn.gelu(c + conv_b[None, :, None], approximate=False)
        return out + c.transpose(0, 2, 1)

    def _L0_ffn_ref(x, gate_w, gate_b, w1, w2, w3):
        import jax, jax.numpy as jnp
        import numpy as np
        D_MODEL = 64
        N_EXPERTS = 16
        HIDDEN = 128
        SCALE = 0.02
        n_experts = w1.shape[0]
        logits = jnp.einsum('bsd,de->bse', x, gate_w) + gate_b
        probs = jax.nn.softmax(logits, axis=-1)
        top_probs, top_idx = jax.lax.top_k(probs, 2)
        top_probs = top_probs / jnp.sum(top_probs, axis=-1, keepdims=True)
        dispatch = jnp.sum(jax.nn.one_hot(top_idx, n_experts, dtype=x.dtype) * top_probs[..., None], axis=-2)
        h1 = jnp.einsum('bsd,edh->bseh', x, w1)
        h2 = jnp.einsum('bsd,edh->bseh', x, w2)
        hidden = jax.nn.silu(h1) * h2
        expert_out = jnp.einsum('bseh,eho->bseo', hidden, w3)
        return jnp.einsum('bseo,bse->bso', expert_out, dispatch)
    h = _L0_tok_ref(x, L0_tok_ln_q_w, L0_tok_ln_q_b, L0_tok_Wq, L0_tok_ln_kv_w, L0_tok_ln_kv_b, L0_tok_Wkv, L0_tok_proj_w, L0_tok_proj_b, 4, 8)
    h = h + _L0_attn_ref(_layernorm(h, axis=-1), L0_attn_f_in_proj_w, L0_attn_f_in_proj_b, L0_attn_f_x_proj_w, L0_attn_f_x_proj_b, L0_attn_f_dt_bias, L0_attn_f_A_log, L0_attn_f_D_skip, L0_attn_f_out_proj_w, L0_attn_f_out_proj_b, L0_attn_b_in_proj_w, L0_attn_b_in_proj_b, L0_attn_b_x_proj_w, L0_attn_b_x_proj_b, L0_attn_b_dt_bias, L0_attn_b_A_log, L0_attn_b_D_skip, L0_attn_b_out_proj_w, L0_attn_b_out_proj_b, L0_attn_norm_w, L0_attn_norm_b, L0_attn_conv_w, L0_attn_conv_b)
    h = h + _L0_ffn_ref(_layernorm(h, axis=-1), L0_ffn_gate_w, L0_ffn_gate_b, L0_ffn_w1, L0_ffn_w2, L0_ffn_w3)
    return h

_drawn_inputs = setup_inputs


def setup_inputs(seed=0):
    import zlib

    import numpy as np

    out = dict(_drawn_inputs(seed))
    spreads = {'L0_tok_ln_q_w': (1.0, 0.6),
     'L0_tok_ln_q_b': (0.0, 2.0),
     'L0_tok_ln_kv_w': (1.0, 0.6),
     'L0_tok_ln_kv_b': (0.0, 0.759),
     'L0_tok_proj_b': (0.0, 0.1),
     'L0_attn_f_in_proj_b': (0.0, 0.8),
     'L0_attn_f_x_proj_b': (0.0, 0.8),
     'L0_attn_f_dt_bias': (-4.0, 0.6),
     'L0_attn_f_D_skip': (1.0, 0.6),
     'L0_attn_f_out_proj_b': (0.0, 0.8),
     'L0_attn_b_in_proj_b': (0.0, 0.8),
     'L0_attn_b_x_proj_b': (0.0, 0.8),
     'L0_attn_b_dt_bias': (-4.0, 0.6),
     'L0_attn_b_D_skip': (1.0, 0.6),
     'L0_attn_b_out_proj_b': (0.0, 2.0),
     'L0_attn_norm_w': (1.0, 0.6),
     'L0_attn_norm_b': (0.0, 0.8),
     'L0_attn_conv_b': (0.0, 2.0),
     'L0_ffn_gate_b': (0.0, 2.0)}
    factors = {'L0_tok_Wq': 8.0,
     'L0_attn_f_in_proj_w': 8.0,
     'L0_attn_f_x_proj_w': 8.0,
     'L0_attn_f_A_log': 8.0,
     'L0_attn_f_out_proj_w': 8.0,
     'L0_attn_b_in_proj_w': 7.985,
     'L0_attn_b_x_proj_w': 8.0,
     'L0_attn_b_A_log': 8.0,
     'L0_attn_b_out_proj_w': 8.0,
     'L0_ffn_gate_w': 22.528,
     'L0_ffn_w1': 8.0,
     'L0_ffn_w2': 8.0,
     'L0_ffn_w3': 8.0,
     'L0_attn_conv_w': 32.046}
    for name, (base, spread) in spreads.items():
        noise = np.random.default_rng([zlib.crc32(name.encode()), seed]).standard_normal(out[name].shape)
        drawn = base * np.exp(spread * noise) if base else spread * noise
        out[name] = jnp.asarray(drawn.astype(out[name].dtype))
    for name, factor in factors.items():
        out[name] = (out[name] * factor).astype(out[name].dtype)
    return out
```

```python
from contextlib import contextmanager

import concourse.bass as bass
from concourse import mybir

F32 = mybir.dt.float32
F16 = mybir.dt.float16
BF16 = mybir.dt.bfloat16
ALU = mybir.AluOpType
ACT = mybir.ActivationFunctionType
AX = mybir.AxisListType

BATCH, C, SIDE, STRIDE, HEADS = 32, 64, 64, 4, 8
D = C // HEADS
T = (SIDE // STRIDE) ** 2
N = STRIDE * STRIDE
PIX = N * T
HALVES = 2
STEPS = BATCH // HALVES
GROUPS = STEPS // 2
COLS = STEPS * T
GC = COLS // GROUPS
GT = HALVES * GC
DI, SN = 128, 16
SP = DI // HEADS
EXPERTS, HID = 16, 128
EPS = 1e-5
BANK = 512
CH = 2 * BANK
KCH = PIX // CH
TQ = T // 4

PARTS = [("mean", 128), ("sum_c", 32), ("sum_d", 32), ("center", 128), ("ysel", 128), ("dup", 1),
         ("wq", 128), ("wk", 128), ("wv", 128), ("proj", 128),
         ("lnq_w", 1), ("lnq_b", 1), ("lnkv_w", 1), ("lnkv_b", 1), ("proj_b", 1)]
for _d in "fb":
    PARTS += [(_d + "_win", 512), (_d + "_wx", 384), (_d + "_wo", 64), (_d + "_alog", 16), (_d + "_bxi", 1),
              (_d + "_bz", 1), (_d + "_bdt", 1), (_d + "_dtb", 1), (_d + "_bB", 1), (_d + "_bC", 1),
              (_d + "_D", 1), (_d + "_bo", 1)]
PARTS += [("norm_w", 1), ("norm_b", 1), ("conv_w", 3), ("conv_b", 1), ("gate", 32), ("gate_b", 16), ("rank", 16)]
AT, _n = {}, 0
for _name, _w in PARTS:
    AT[_name] = (_n, _w)
    _n += _w
PACKED = _n


class Core:

    def __init__(self, nc):
        self.nc = nc
        self.sems = {}
        self.pack = nc.alloc_sbuf_tensor("pack", [128, PACKED], F32)
        self.bsel = nc.alloc_sbuf_tensor("bsel", [128, 4 * 128], F16)
        self.rsel = nc.alloc_sbuf_tensor("rsel", [96, 4 * 128], BF16)
        self.wq = nc.alloc_sbuf_tensor("wq_folded", [128, 128], F32)
        self.wk = nc.alloc_sbuf_tensor("wk_folded", [128, 128], F32)
        self.wv = nc.alloc_sbuf_tensor("wv_folded", [128, 128], F32)
        self.cols = nc.alloc_sbuf_tensor("cols", [128, 16], F32)
        self.neg_a = nc.alloc_sbuf_tensor("neg_a", [128, 2 * SP], F32)
        self.h = nc.alloc_sbuf_tensor("h", [128, COLS], F32)
        self.x = nc.alloc_sbuf_tensor("x_norm", [128, COLS], F32)
        self.arena_words = 38900
        self.arena = nc.alloc_sbuf_tensor("arena", [128, self.arena_words], F32)
        self.psum = nc.alloc_psum_tensor("psum", [128, 8 * BANK], F32)
        self.used = 0

    def p(self, name, i=0, w=None):
        at, width = AT[name]
        return self.pack[:, at + i:at + i + (width if w is None else w)]

    def sem(self, name):
        if name not in self.sems:
            self.sems[name] = self.nc.alloc_semaphore(name)
        return self.sems[name]

    @contextmanager
    def stage(self):
        self.used, self.sems = 0, {}
        yield
        self.nc.all_engine_barrier()
        self.nc.clear_and_free_semaphores(list(self.sems.values()))
        self.nc.all_engine_barrier()

    def take(self, words, dtype=F32):
        at, self.used = self.used, self.used + words
        assert self.used <= self.arena_words, self.used
        view = self.arena[:, at:at + words]
        return view if dtype == F32 else view.bitcast(dtype)

    def bank(self, b, n=1):
        return self.psum[:, b * BANK:(b + n) * BANK]


def setup(core, params, bsel, rsel):
    nc, p, S = core.nc, core.p, core.sem
    t = core.take(512)
    with nc.Block() as block:
        @block.sync
        def _(sp):
            sp.dma_start(core.pack[:, :], params).then_inc(S("params_in"), 16)
            sp.dma_start(core.bsel[:, :], bsel).then_inc(S("params_in"), 16)
            sp.dma_start(core.rsel[:, :], rsel).then_inc(S("params_in"), 16)
            sp.wait_ge(S("params_in"), 48)

        @block.vector
        def _(dve):
            dve.wait_ge(S("params_in"), 48)
            dve.tensor_scalar(t[:, 0:128], p("wq"), p("lnq_w"), None, ALU.mult)
            dve.tensor_scalar(t[:, 128:256], p("wk"), p("lnkv_w"), None, ALU.mult)
            dve.tensor_scalar(t[:, 256:384], p("wv"), p("lnkv_w"), None, ALU.mult).then_inc(S("fold_scaled"), 1)
            for i, d in enumerate("fb"):
                dve.tensor_scalar(core.cols[:, 4 + 4 * i:5 + 4 * i], p(d + "_bxi"), -1.0, None, ALU.mult)
                dve.tensor_scalar(core.cols[:, 5 + 4 * i:6 + 4 * i], p(d + "_bz"), -1.0, None, ALU.mult)
                dve.tensor_tensor(core.cols[:, 6 + 4 * i:7 + 4 * i], p(d + "_bdt"), p(d + "_dtb"), ALU.add)
            dve.wait_ge(S("fold_mm"), 1)
            dve.tensor_scalar(core.wq[:, :], core.bank(0)[:, 0:128], C ** -0.5 / N, None, ALU.mult)
            dve.tensor_copy(core.wk[:, :], core.bank(0)[:, 128:256])
            dve.tensor_copy(core.wv[:, :], core.bank(0)[:, 256:384])
            dve.tensor_scalar(core.cols[:, 0:1], core.bank(1)[:, 0:1], C ** -0.5, None, ALU.mult)
            dve.tensor_copy(core.cols[:, 1:2], core.bank(1)[:, 1:2]).then_inc(S("bias_v"), 1)
            dve.wait_ge(S("bias_o_mm"), 1)
            dve.tensor_tensor(core.cols[:, 2:3], core.bank(2)[:, 0:1], p("proj_b"), ALU.add)
            dve.wait_ge(S("a_exp"), 1)
            dve.tensor_scalar(core.neg_a[:, :], core.neg_a[:, :], -1.0, None, ALU.mult)

        @block.tensor
        def _(pe):
            pe.wait_ge(S("fold_scaled"), 1)
            for i in range(3):
                pe.matmul(core.bank(0)[:, 128 * i:128 * (i + 1)], p("center"), t[:, 128 * i:128 * (i + 1)],
                          start=True, stop=True)
            pe.matmul(core.bank(1)[:, 0:1], p("wq"), p("lnq_b"), start=True, stop=True)
            pe.matmul(core.bank(1)[:, 1:2], p("wv"), p("lnkv_b"), start=True, stop=True).then_inc(S("fold_mm"), 1)
            pe.wait_ge(S("bias_v"), 1)
            pe.matmul(core.bank(2)[:, 0:1], p("proj"), core.cols[:, 1:2], start=True, stop=True)\
              .then_inc(S("bias_o_mm"), 1)

        @block.scalar
        def _(act):
            act.preload_act_table_set("natural_log_exp_and_others")
            act.wait_ge(S("params_in"), 48)
            act.activation(core.neg_a[:, 0:SP], p("f_alog"), ACT.Exp)
            act.activation(core.neg_a[:, SP:2 * SP], p("b_alog"), ACT.Exp).then_inc(S("a_exp"), 1)


def attention(core, xin):
    nc, p, S = core.nc, core.p, core.sem
    xt = [core.take(PIX) for _ in range(2)]
    xsq = core.take(PIX)
    kq = core.take(PIX)
    v = [core.take(PIX) for _ in range(2)]
    mean_t = core.take(8 * T)
    rf, rf_sq, q_musq, q_rstd, q, av_sum = (core.take(T) for _ in range(6))
    musq = core.take(CH)
    rstd = [core.take(CH) for _ in range(2)]
    prob = core.take(CH)
    gain = core.take(CH)
    hi = core.take(CH // 2, F16)
    prob16 = core.take(CH // 2, F16)
    top, den, rden = (core.take(TQ) for _ in range(3))
    slot = [core.bank(0, 2), core.bank(2, 2)]
    rows = core.bank(4, 2)
    small = core.bank(6)
    qb = core.bank(7)
    q_bias, o_bias = core.cols[:, 0:1], core.cols[:, 2:3]

    def bcast_n(view, n):
        return view.unsqueeze(1).to_broadcast([128, n, view.shape[-1]])

    def by_n(view):
        return view.rearrange("p (n t) -> p n t", n=N)

    def schedule(emit, loop):
        emit(0, 0, front=True, back=False, pre=True)
        emit(1, 1, front=True, back=True, pre=True)
        with loop(1, STEPS // 2 - 1) as k:
            emit(2 * k, 0, front=True, back=True, pre=True)
            emit(2 * k + 1, 1, front=True, back=True, pre=True)
        emit(STEPS - 2, 0, front=True, back=True, pre=True)
        emit(STEPS - 1, 1, front=True, back=True, pre=False)
        emit(STEPS, 0, front=False, back=True, pre=False)

    def later(s, n):
        return not isinstance(s, int) or s >= n

    with nc.Block() as block:
        @block.sync
        def _(sp):
            def load(s, par):
                if later(s, 2):
                    sp.wait_ge(S("v_mm"), KCH * (s - 1))
                sp.dma_start(xt[par], xin[s]).then_inc(S(f"x_in{par}"), 16)

            load(0, 0)
            load(1, 1)
            with sp.Fori(1, STEPS // 2) as k:
                load(2 * k, 0)
                load(2 * k + 1, 1)

        @block.gpsimd
        def _(pool):
            def pre(s, par):
                pool.wait_ge(S(f"x_in{par}"), 8 * (s - par) + 16)
                if later(s, 1):
                    pool.wait_ge(S("rf_sum"), s)
                x = xt[par]
                pool.tensor_tensor(mean_t, x[:, 0:8 * T], x[:, 8 * T:16 * T], ALU.add).then_inc(S("mean_part"), 1)
                for i, n in enumerate((4, 2)):
                    pool.wait_ge(S("mean_part"), 3 * s + i + 1)
                    pool.tensor_tensor(mean_t[:, 0:n * T], mean_t[:, 0:n * T], mean_t[:, n * T:2 * n * T], ALU.add)\
                        .then_inc(S("mean_part"), 1)
                pool.wait_ge(S("mean_part"), 3 * s + 3)
                if later(s, 1):
                    pool.wait_ge(S("q_mm"), s)
                    pool.wait_ge(S("h_base"), s)
                pool.tensor_tensor(rf, mean_t[:, 0:T], mean_t[:, T:2 * T], ALU.add).then_inc(S("rf_sum"), 1)

            def step(s, par, front, back, pre):
                if pre:
                    pre_(s + 1, 1 - par)
                if front:
                    pool.wait_ge(S("s_max"), s + 1)
                    pool.tensor_tensor(by_n(prob), by_n(prob), bcast_n(top, N), ALU.subtract)\
                        .then_inc(S("s_centred"), 1)
                    pool.wait_ge(S("inv_den"), s + 1)
                    pool.tensor_tensor(by_n(gain), by_n(rstd[par]), bcast_n(rden, N), ALU.mult)\
                        .then_inc(S("gain"), 1)
                    pool.wait_ge(S("gain"), s + 1)
                    pool.tensor_tensor(prob, prob, gain, ALU.mult).then_inc(S("prob"), 1)

            pre_ = pre
            pre_(0, 0)
            schedule(step, pool.Fori)

        @block.scalar
        def _(act):
            def pre_x(s, par):
                act.wait_ge(S(f"x_in{par}"), 8 * (s - par) + 16)
                if later(s, 1):
                    act.wait_ge(S("sum_x2"), s)
                act.activation(xsq, xt[par], ACT.Square).then_inc(S("x_sq"), 1)

            def pre_rf(s):
                act.wait_ge(S("rf_sum"), s + 1)
                act.activation(rf_sq, rf, ACT.Square, scale=1.0 / N).then_inc(S("rf_sq"), 1)
                act.activation(core.h[:, bass.ds(s * T, T)], rf, ACT.Identity, bias=o_bias, scale=1.0 / N)\
                   .then_inc(S("h_base"), 1)

            def pre_stats(s, par):
                act.wait_ge(S("q_stats"), s + 1)
                act.activation(q_musq, small[:, 0:T], ACT.Square, scale=1.0 / N).then_inc(S("q_musq"), 1)
                act.wait_ge(S("sum_x"), s + 1)
                act.activation(musq, rows, ACT.Square).then_inc(S("x_musq"), 1)
                act.wait_ge(S("q_var"), s + 1)
                act.activation(q_rstd, q_rstd, ACT.Ln, bias=EPS).then_inc(S("q_ln"), 1)
                act.wait_ge(S("q_ln"), s + 1)
                act.activation(q_rstd, q_rstd, ACT.Exp, scale=-0.5).then_inc(S("q_rstd"), 1)
                act.wait_ge(S("x_var"), s + 1)
                act.activation(rstd[par], rstd[par], ACT.Ln, bias=EPS).then_inc(S("x_ln"), 1)
                act.wait_ge(S("x_ln"), s + 1)
                act.activation(rstd[par], rstd[par], ACT.Exp, scale=-0.5).then_inc(S("x_rstd"), 1)

            def step(s, par, front, back, pre):
                if pre:
                    pre_x(s + 1, 1 - par)
                if front:
                    for c in range(KCH):
                        act.wait_ge(S("v_mm"), KCH * s + c + 1)
                        if c == 0 and later(s, 2):
                            act.wait_ge(S("av_sum"), s - 1)
                        act.activation(v[par][:, c * CH:(c + 1) * CH], slot[c % 2], ACT.Copy).then_inc(S("v_out"), 1)
                if pre:
                    pre_rf(s + 1)
                if front:
                    act.wait_ge(S("s_centred"), s + 1)
                    act.activation(prob, prob, ACT.Exp).then_inc(S("s_exp"), 1)
                if pre:
                    pre_stats(s + 1, 1 - par)
                if front:
                    act.wait_ge(S("prob"), s + 1)
                    act.activation(hi, prob, ACT.Copy).then_inc(S("prob_hi"), 1)

            act.preload_act_table_set("natural_log_exp_and_others")
            pre_x(0, 0)
            pre_rf(0)
            pre_stats(0, 0)
            schedule(step, act.Fori)

        @block.vector
        def _(dve):
            def pre(s, par):
                dve.wait_ge(S("q_musq"), s + 1)
                dve.tensor_tensor(q_rstd, small[:, T:2 * T], q_musq, ALU.subtract).then_inc(S("q_var"), 1)
                dve.wait_ge(S("sum_x2"), s + 1)
                dve.tensor_tensor(rstd[par], rows, musq, ALU.subtract).then_inc(S("x_var"), 1)
                dve.wait_ge(S("q_rstd"), s + 1)
                dve.tensor_tensor(q, qb[:, 0:T], q_rstd, ALU.mult).then_inc(S("q_scaled"), 1)
                dve.wait_ge(S("q_scaled"), s + 1)
                dve.tensor_scalar(q, q, q_bias, None, ALU.add).then_inc(S("q_out"), 1)

            def halve(view, n, s, i):
                dve.tensor_tensor(view[:, 0:n * T], view[:, 0:n * T], view[:, n * T:2 * n * T], ALU.add)\
                   .then_inc(S("av_part"), 1)
                dve.wait_ge(S("av_part"), 3 * (s - 1) + i + 1)

            def step(s, par, front, back, pre_next):
                for c in range(KCH):
                    if back:
                        dve.wait_ge(S("a_mm"), KCH * (s - 1) + c + 1)
                        if c == 0:
                            dve.wait_ge(S("v_out"), KCH * s)
                        quarter = by_n(v[1 - par])[:, :, c * TQ:(c + 1) * TQ]
                        dve.tensor_tensor(quarter, by_n(slot[0]), quarter, ALU.mult).then_inc(S("av"), 1)
                    if front:
                        dve.wait_ge(S("k_mm"), KCH * s + c + 1)
                        if c == 0:
                            dve.wait_ge(S("q_out"), s + 1)
                            if later(s, 1):
                                dve.wait_ge(S("scores"), s)
                        dve.tensor_tensor(kq[:, c * CH:(c + 1) * CH].rearrange("p (n t) -> p n t", t=T),
                                          slot[1].rearrange("p (n t) -> p n t", t=T), bcast_n(q, CH // T), ALU.mult)\
                           .then_inc(S("kq"), 1)
                if back:
                    dve.wait_ge(S("av"), KCH * s)
                    halve(v[1 - par], 8, s, 0)
                if front:
                    dve.wait_ge(S("scores"), s + 1)
                    dve.wait_ge(S("x_rstd"), s + 1)
                    dve.tensor_tensor(prob, rows, rstd[par], ALU.mult).then_inc(S("s_scaled"), 1)
                    dve.wait_ge(S("s_scaled"), s + 1)
                    dve.tensor_reduce(top, prob.rearrange("p (n t) -> p t n", n=N), AX.X, ALU.max)\
                       .then_inc(S("s_max"), 1)
                if back:
                    halve(v[1 - par], 4, s, 1)
                    halve(v[1 - par], 2, s, 2)
                    if later(s, 2):
                        dve.wait_ge(S("o_mm"), s - 1)
                    w = v[1 - par]
                    dve.tensor_tensor(av_sum, w[:, 0:T], w[:, T:2 * T], ALU.add).then_inc(S("av_sum"), 1)
                if front:
                    dve.wait_ge(S("s_exp"), s + 1)
                    dve.tensor_reduce(den, prob.rearrange("p (n t) -> p t n", n=N), AX.X, ALU.add)\
                       .then_inc(S("s_den"), 1)
                    dve.wait_ge(S("s_den"), s + 1)
                    dve.reciprocal(rden, den).then_inc(S("inv_den"), 1)
                if pre_next:
                    pre(s + 1, 1 - par)
                if front:
                    dve.wait_ge(S("prob_hi"), s + 1)
                    dve.scalar_tensor_tensor(prob16, hi, p("dup"), prob, ALU.mult, ALU.add).then_inc(S("prob16"), 1)
                if back:
                    dve.wait_ge(S("o_mm"), s)
                    cols = core.h[:, bass.ds((s - 1) * T, T)]
                    dve.tensor_tensor(cols, qb[:, T:2 * T], cols, ALU.add).then_inc(S("h_out"), 1)

            pre(0, 0)
            schedule(lambda s, par, front, back, pre: step(s, par, front, back, pre), dve.Fori)

        @block.tensor
        def _(pe):
            def quarters(weights, source, start_wait):
                for half in range(2):
                    for g in range(4):
                        view = by_n(source)[:, half * 8:half * 8 + 8, g * TQ:(g + 1) * TQ]
                        mm = pe.matmul(rows[32 * g:32 * g + 32, half * BANK:(half + 1) * BANK], weights, view,
                                       start=True, stop=True)
                return mm

            def pre(s, par):
                pe.wait_ge(S("rf_sq"), s + 1)
                if later(s, 1):
                    pe.wait_ge(S("q_var"), s)
                    pe.wait_ge(S("q_scaled"), s)
                pe.matmul(small[:, 0:T], p("mean"), rf, start=True, stop=True)
                pe.matmul(small[:, T:2 * T], p("mean"), rf_sq, start=True, stop=True).then_inc(S("q_stats"), 1)
                pe.matmul(qb[:, 0:T], core.wq[:, :], rf, start=True, stop=True).then_inc(S("q_mm"), 1)
                pe.wait_ge(S(f"x_in{par}"), 8 * (s - par) + 16)
                if later(s, 1):
                    pe.wait_ge(S("s_scaled"), s)
                quarters(p("sum_c"), xt[par], None).then_inc(S("sum_x"), 1)
                pe.wait_ge(S("x_sq"), s + 1)
                pe.wait_ge(S("x_musq"), s + 1)
                quarters(p("sum_c"), xsq, None).then_inc(S("sum_x2"), 1)

            def project(weights, source, dst):
                for b in range(2):
                    mm = pe.matmul(dst[:, b * BANK:(b + 1) * BANK], weights, source[:, b * BANK:(b + 1) * BANK],
                                   start=True, stop=True)
                return mm

            def step(s, par, front, back, pre_next):
                for c in range(KCH):
                    if back:
                        if c == 0:
                            pe.wait_ge(S("prob16"), s)
                            pe.wait_ge(S("v_out"), KCH * s - 1)
                        else:
                            pe.wait_ge(S("av"), KCH * (s - 1) + c)
                        project(core.bsel[:, c * 128:(c + 1) * 128], prob16, slot[0]).then_inc(S("a_mm"), 1)
                    if front:
                        if c > 0:
                            pe.wait_ge(S("kq"), KCH * s + c)
                        elif later(s, 1):
                            pe.wait_ge(S("v_out"), KCH * s)
                        project(core.wk[:, :], xt[par][:, c * CH:(c + 1) * CH], slot[1]).then_inc(S("k_mm"), 1)
                if front:
                    for c in range(KCH):
                        if c == 0 and back:
                            pe.wait_ge(S("av"), KCH * s)
                        if c == 1:
                            pe.wait_ge(S("kq"), KCH * (s + 1))
                        if c >= 2:
                            pe.wait_ge(S("v_out"), KCH * s + c - 1)
                        project(core.wv[:, :], xt[par][:, c * CH:(c + 1) * CH], slot[c % 2]).then_inc(S("v_mm"), 1)
                        if c == 0:
                            pe.wait_ge(S("kq"), KCH * (s + 1))
                            pe.wait_ge(S("x_var"), s + 1)
                            quarters(p("sum_d"), kq, None).then_inc(S("scores"), 1)
                if back:
                    pe.wait_ge(S("av_sum"), s)
                    if later(s, 2):
                        pe.wait_ge(S("h_out"), s - 1)
                    pe.matmul(qb[:, T:2 * T], p("proj"), av_sum, start=True, stop=True).then_inc(S("o_mm"), 1)
                if pre_next:
                    pre(s + 1, 1 - par)

            pre(0, 0)
            schedule(lambda s, par, front, back, pre: step(s, par, front, back, pre), pe.Fori)


def normalize(core, tag, src, write, extra=None):
    nc, p = core.nc, core.p
    S = lambda name: core.sem(f"{tag}_{name}")
    sq, musq, rstd, cen = ([core.take(CH) for _ in range(2)] for _ in range(4))
    extra = extra or {}
    chunks = COLS // CH

    with nc.Block() as block:
        @block.tensor
        def _(pe):
            for c in range(chunks):
                mean, square = core.bank(4 * (c % 2), 2), core.bank(4 * (c % 2) + 2, 2)
                if c >= 2:
                    pe.wait_ge(S("centred"), c - 1)
                    pe.wait_ge(S("var"), c - 1)
                for b in range(2):
                    cols = slice(b * BANK, (b + 1) * BANK)
                    mm = pe.matmul(mean[:, cols], p("mean"), src[:, c * CH:(c + 1) * CH][:, cols], start=True, stop=True)
                mm.then_inc(S("mean"), 1)
                pe.wait_ge(S("sq"), c + 1)
                for b in range(2):
                    cols = slice(b * BANK, (b + 1) * BANK)
                    mm = pe.matmul(square[:, cols], p("mean"), sq[c % 2][:, cols], start=True, stop=True)
                mm.then_inc(S("mean_sq"), 1)

        @block.scalar
        def _(act):
            act.preload_act_table_set("natural_log_exp_and_others")
            def square(c):
                if c >= 2:
                    act.wait_ge(S("mean_sq"), c - 1)
                act.activation(sq[c % 2], src[:, c * CH:(c + 1) * CH], ACT.Square).then_inc(S("sq"), 1)

            square(0)
            for c in range(chunks):
                if c + 1 < chunks:
                    square(c + 1)
                act.wait_ge(S("mean"), c + 1)
                if c >= 2:
                    act.wait_ge(S("var"), c - 1)
                act.activation(musq[c % 2], core.bank(4 * (c % 2), 2), ACT.Square).then_inc(S("musq"), 1)
                act.wait_ge(S("var"), c + 1)
                act.activation(rstd[c % 2], rstd[c % 2], ACT.Ln, bias=EPS).then_inc(S("ln"), 1)
                act.wait_ge(S("ln"), c + 1)
                act.activation(rstd[c % 2], rstd[c % 2], ACT.Exp, scale=-0.5).then_inc(S("rstd"), 1)
                act.wait_ge(S("scaled"), c + 1)
                write(act, c, cen[c % 2]).then_inc(S("written"), 1)
            if "act" in extra:
                extra["act"](act)

        @block.vector
        def _(dve):
            for c in range(chunks):
                if c >= 2:
                    dve.wait_ge(S("scaled"), c - 1)
                dve.wait_ge(S("mean_sq"), c + 1)
                dve.wait_ge(S("musq"), c + 1)
                dve.tensor_tensor(rstd[c % 2], core.bank(4 * (c % 2) + 2, 2), musq[c % 2], ALU.subtract)\
                   .then_inc(S("var"), 1)
                if c >= 2:
                    dve.wait_ge(S("written"), c - 1)
                dve.tensor_tensor(cen[c % 2], src[:, c * CH:(c + 1) * CH], core.bank(4 * (c % 2), 2), ALU.subtract)\
                   .then_inc(S("centred"), 1)
                dve.wait_ge(S("rstd"), c + 1)
                dve.wait_ge(S("centred"), c + 1)
                dve.tensor_tensor(cen[c % 2], cen[c % 2], rstd[c % 2], ALU.mult).then_inc(S("scaled"), 1)
            if "dve" in extra:
                extra["dve"](dve)


def by_seq(view):
    return view.rearrange("p (s t) -> p s t", t=T)


def mix_input(core):
    p, S = core.p, core.sem
    conv = core.take(COLS)
    x = core.x[:, :]

    def write(act, c, chunk):
        return act.activation(x[:, c * CH:(c + 1) * CH], chunk, ACT.Copy)

    def dve_conv(dve):
        dve.wait_ge(S("xn_written"), COLS // CH)
        dve.tensor_scalar(conv, x, p("conv_w", 1, 1), None, ALU.mult).then_inc(S("conv"), 1)
        dve.wait_ge(S("conv"), 1)
        after, before = by_seq(conv)[:, :, 1:T], by_seq(conv)[:, :, 0:T - 1]
        dve.scalar_tensor_tensor(after, by_seq(x)[:, :, 0:T - 1], p("conv_w", 0, 1), after, ALU.mult, ALU.add)\
           .then_inc(S("conv"), 1)
        dve.wait_ge(S("conv"), 2)
        dve.scalar_tensor_tensor(before, by_seq(x)[:, :, 1:T], p("conv_w", 2, 1), before, ALU.mult, ALU.add)\
           .then_inc(S("conv"), 1)
        dve.wait_ge(S("conv_gelu"), 1)
        dve.tensor_tensor(core.h[:, :], core.h[:, :], conv, ALU.add).then_inc(S("conv_added"), 1)

    def act_gelu(act):
        act.wait_ge(S("conv"), 3)
        act.activation(conv, conv, ACT.Gelu, bias=p("conv_b")).then_inc(S("conv_gelu"), 1)

    normalize(core, "xn", core.h[:, :], write, {"dve": dve_conv, "act": act_gelu})


def between_directions(core):
    p = core.p
    x = core.x[:, :]

    def write(act, c, chunk):
        return act.activation(by_seq(x[:, c * CH:(c + 1) * CH])[:, :, ::-1], by_seq(chunk), ACT.Identity,
                              bias=p("norm_b"), scale=p("norm_w"))

    normalize(core, "yn", x, write)


def add_backward(core):
    with core.nc.Block() as block:
        @block.vector
        def _(dve):
            dve.tensor_tensor(by_seq(core.h[:, :]), by_seq(core.h[:, :]), by_seq(core.x[:, :])[:, :, ::-1], ALU.add)


def mixer(core, d):
    nc, p = core.nc, core.p
    S = lambda name: core.sem(f"{d}_{name}")
    di = "fb".index(d)
    neg_bxi, neg_bz, b_dt = (core.cols[:, 4 + 4 * di + i:5 + 4 * di + i] for i in range(3))
    neg_a = core.neg_a[:, di * SP:(di + 1) * SP]
    decay = core.take(4 * CH)
    states = [core.take(4 * CH) for _ in range(2)]
    xi, zs, bm, cm = ([core.take(CH) for _ in range(2)] for _ in range(4))
    sig, dt, dx, rest, gate = (core.take(CH) for _ in range(5))
    dt_part = [core.take(CH // 2, BF16) for _ in range(3)]
    dx_part = [core.take(CH // 2, BF16) for _ in range(3)]
    dt_rows = [core.take(4 * CH // 2, BF16) for _ in range(2)]
    dx_rows = [core.take(4 * CH // 2, BF16) for _ in range(2)]
    ps_dt, ps_dx, ps_y, ps_p = (core.bank(b, 2) for b in (0, 2, 4, 6))

    def schedule(emit, loop):
        emit(0, 0, last=False)
        with loop(0, (GROUPS - 2) // 2) as k:
            emit(2 * k + 1, 1, last=False)
            emit(2 * k + 2, 0, last=False)
        emit(GROUPS - 1, 1, last=True)
        emit(GROUPS, 0, last=None)

    def has_post(g):
        return not isinstance(g, int) or g >= 1

    def has_old(g):
        return not isinstance(g, int) or g >= 2

    def rows_src(part, g):
        return part[32 * g:32 * g + 32, :]

    with nc.Block() as block:
        @block.sync
        def _(sp):
            def spread(g, par, name, parts, rows):
                for i in range(3):
                    sp.wait_ge(S(f"{name}_part"), 3 * g + i + 1)
                    for m in range(4):
                        sp.dma_start(rows[par][32 * i:32 * i + 32, m * CH:(m + 1) * CH],
                                     parts[i][32 * m:32 * m + 32, :]).then_inc(S(f"{name}_rows"), 16)

            def step(g, par, last):
                if last is False:
                    spread(g + 1, 1 - par, "dt", dt_part, dt_rows)
                    spread(g + 1, 1 - par, "dx", dx_part, dx_rows)

            spread(0, 0, "dt", dt_part, dt_rows)
            spread(0, 0, "dx", dx_part, dx_rows)
            schedule(step, sp.Fori)

        @block.tensor
        def _(pe):
            def two(out, weights, rhs):
                for b in range(2):
                    mm = pe.matmul(out[:, b * BANK:(b + 1) * BANK], weights[b] if isinstance(weights, list) else weights,
                                   rhs(b), start=True, stop=True)
                return mm

            def group_in(g):
                cols = core.x[:, bass.ds(g * GC, GC)]
                return lambda b: cols

            def pre_xi(g):
                if not isinstance(g, int) or g >= 1:
                    pe.wait_ge(S("c_out"), g)
                two(ps_p, [p(d + "_win", 0, 128), p(d + "_win", 128, 128)], group_in(g)).then_inc(S("xi_mm"), 1)

            def pre_z(g):
                pe.wait_ge(S("xi"), g + 1)
                two(ps_p, [p(d + "_win", 256, 128), p(d + "_win", 384, 128)], group_in(g)).then_inc(S("z_mm"), 1)

            def pre_x(g, par, i, name, freed, count):
                pe.wait_ge(S(freed), count)
                two(ps_p, p(d + "_wx", 128 * i, 128), lambda b: xi[par][:, b * BANK:(b + 1) * BANK])\
                    .then_inc(S(name), 1)

            def sum_states(quad, j, g):
                pe.wait_ge(S("ch"), 4 * quad + 4)
                if j == 0 and has_post(g):
                    pe.wait_ge(S("y_read"), g)
                for b in range(2):
                    for m in range(4):
                        mm = pe.matmul(ps_y[32 * m:32 * m + 32, b * BANK:(b + 1) * BANK], p("ysel", 32 * j, 32),
                                       states[j % 2][:, m * CH + b * BANK:m * CH + (b + 1) * BANK],
                                       start=(j == 0), stop=(j == 3))
                mm.then_inc(S("y_mm"), 1)

            def project_out(g):
                pe.wait_ge(S("gated"), g + 1)
                for b in range(2):
                    mm = pe.matmul(ps_p[64 * b:64 * b + 64, 0:BANK], p(d + "_wo"), gate[:, b * BANK:(b + 1) * BANK],
                                   start=True, stop=True)
                mm.then_inc(S("o_mm"), 1)

            def step(g, par, last):
                if last is None:
                    sum_states(4 * g - 1, 3, g)
                    project_out(g - 1)
                    return
                pe.wait_ge(S("dt_rows"), 16 * 12 * (g + 1))
                pe.wait_ge(S("dx_rows"), 16 * 12 * (g + 1))
                for k in range(16):
                    j, m = divmod(k, 4)
                    sel = core.rsel[:, 128 * j:128 * j + 128]
                    first = isinstance(g, int) and g == 0 and k == 0
                    if not first:
                        pe.wait_ge(S("decay"), 16 * g + k)
                    two(ps_dt, sel, lambda b: dt_rows[par][0:96, m * CH + b * BANK:m * CH + (b + 1) * BANK])\
                        .then_inc(S("dt_mm"), 1)
                    if not first:
                        pe.wait_ge(S("inject"), 16 * g + k)
                    two(ps_dx, sel, lambda b: dx_rows[par][0:96, m * CH + b * BANK:m * CH + (b + 1) * BANK])\
                        .then_inc(S("dx_mm"), 1)
                    if k == 0 and last is False:
                        pre_xi(g + 1)
                    if k == 1 and has_post(g):
                        sum_states(4 * g - 1, 3, g)
                    if k == 2 and last is False:
                        pre_z(g + 1)
                    if k == 6 and last is False:
                        pre_x(g + 1, 1 - par, 0, "dtp_mm", "zs", g + 2)
                    if k in (5, 9, 13):
                        sum_states(4 * g + k // 4 - 1, k // 4 - 1, g)
                    if k == 7 and has_post(g):
                        if last is False:
                            pe.wait_ge(S("dt_abs"), g + 2)
                            pe.wait_ge(S("dt_relu"), g + 2)
                        project_out(g - 1)
                    if k == 9 and last is False:
                        if has_post(g):
                            pre_x(g + 1, 1 - par, 1, "b_mm", "o_out", g)
                        else:
                            pe.wait_ge(S("dt_abs"), g + 2)
                            pre_x(g + 1, 1 - par, 1, "b_mm", "dt_relu", g + 2)
                    if k == 11 and last is False:
                        pre_x(g + 1, 1 - par, 2, "c_mm", "b_out", g + 2)

            pre_xi(0)
            pre_z(0)
            pre_x(0, 0, 0, "dtp_mm", "zs", 1)
            pe.wait_ge(S("dt_abs"), 1)
            pre_x(0, 0, 1, "b_mm", "dt_relu", 1)
            pre_x(0, 0, 2, "c_mm", "b_out", 1)
            schedule(step, pe.Fori)

        @block.scalar
        def _(act):
            def sigmoid(which, g):
                name, bias = (("xi", neg_bxi), ("z", neg_bz))[which]

                def first():
                    act.wait_ge(S(f"{name}_mm"), g + 1)
                    if which:
                        act.wait_ge(S("xi"), g + 1)
                    elif not (isinstance(g, int) and g == 0):
                        act.wait_ge(S("zs"), g)
                    act.activation(sig, ps_p, ACT.Exp, bias=bias, scale=-1.0).then_inc(S("sig"), 1)

                def second():
                    act.wait_ge(S("sig"), 6 * g + 3 * which + 1)
                    act.activation(sig, sig, ACT.Ln, bias=1.0).then_inc(S("sig"), 1)

                def third():
                    act.wait_ge(S("sig"), 6 * g + 3 * which + 2)
                    act.activation(sig, sig, ACT.Exp, scale=-1.0).then_inc(S("sig"), 1)
                return [first, second, third]

            def softplus(g):
                def absolute():
                    act.wait_ge(S("dtp_mm"), g + 1)
                    act.wait_ge(S("zs"), g + 1)
                    act.activation(sig, ps_p, ACT.Abs, bias=b_dt).then_inc(S("dt_abs"), 1)

                def relu():
                    if not (isinstance(g, int) and g == 0):
                        act.wait_ge(S("dt_part"), 3 * g)
                        act.wait_ge(S("dx_part"), 3 * g)
                    act.activation(dt, ps_p, ACT.Relu, bias=b_dt).then_inc(S("dt_relu"), 1)

                def exp():
                    act.wait_ge(S("dt_abs"), g + 1)
                    act.activation(sig, sig, ACT.Exp, scale=-1.0).then_inc(S("dt_exp"), 1)

                def log():
                    act.wait_ge(S("dt_exp"), g + 1)
                    act.activation(sig, sig, ACT.Ln, bias=1.0).then_inc(S("dt_ln"), 1)
                return [absolute, relu, exp, log]

            def high(name, src, ready, parts, g):
                def f():
                    act.wait_ge(S(ready), g + 1)
                    if not (isinstance(g, int) and g == 0):
                        act.wait_ge(S(f"{name}_rows"), 16 * 12 * g)
                    act.activation(parts[0], src, ACT.Copy).then_inc(S(f"{name}_part"), 1)
                return f

            def middle(name, parts, g):
                def f():
                    act.wait_ge(S(f"{name}_rest"), g + 1)
                    act.activation(parts[1], rest, ACT.Copy).then_inc(S(f"{name}_part"), 1)
                return f

            def plain(name, out, bias, g):
                def f():
                    act.wait_ge(S(f"{name}_mm"), g + 1)
                    if not (isinstance(g, int) and g <= 1):
                        act.wait_ge(S("ch"), 16 * (g - 1))
                    act.activation(out, ps_p, ACT.Identity, bias=bias).then_inc(S(f"{name}_out"), 1)
                return f

            def pre(g, par):
                a, z, s = sigmoid(0, g), sigmoid(1, g), softplus(g)
                return {0: [a[0]], 1: [a[1]], 2: [a[2]], 3: [z[0]], 4: [z[1]], 5: [z[2]], 6: [s[0], s[1]],
                        7: [s[2], s[3]], 9: [plain("b", bm[par], p(d + "_bB"), g)],
                        10: [high("dt", dt, "dt", dt_part, g)],
                        11: [middle("dt", dt_part, g), plain("c", cm[par], p(d + "_bC"), g)],
                        12: [high("dx", dx, "dx", dx_part, g)], 13: [middle("dx", dx_part, g)]}

            def output(g):
                act.wait_ge(S("o_mm"), g + 1)
                act.activation(core.x[:, bass.ds(g * GC, GC)], ps_p[:, 0:BANK], ACT.Identity, bias=p(d + "_bo"))\
                   .then_inc(S("o_out"), 1)

            def step(g, par, last):
                if last is None:
                    output(g - 1)
                    return
                todo = pre(g + 1, 1 - par) if last is False else {}
                for k in range(16):
                    n = 16 * g + k
                    m = k % 4
                    act.wait_ge(S("dt_mm"), n + 1)
                    if not (isinstance(n, int) and n < 4):
                        act.wait_ge(S("scan"), n - 3)
                    ring = by_seq(decay[:, m * CH:(m + 1) * CH])[:, :, 1:T]
                    act.activation(ring, by_seq(ps_dt)[:, :, 1:T], ACT.Exp, scale=neg_a[:, 4 * m + k // 4:4 * m + k // 4 + 1])\
                       .then_inc(S("decay"), 1)
                    for f in todo.get(k, []):
                        f()
                    if k == 8 and has_post(g):
                        output(g - 1)

            act.preload_act_table_set("natural_log_exp_and_others")
            first = pre(0, 0)
            for k in range(16):
                for f in first.get(k, []):
                    f()
            schedule(step, act.Fori)

        @block.gpsimd
        def _(pool):
            def add_dt(g):
                pool.wait_ge(S("dt_ln"), g + 1)
                pool.wait_ge(S("dt_relu"), g + 1)
                pool.tensor_tensor(dt, dt, sig, ALU.add).then_inc(S("dt"), 1)

            def mul_dx(g, par):
                pool.wait_ge(S("dt"), g + 1)
                pool.wait_ge(S("xi"), g + 1)
                pool.tensor_tensor(dx, dt, xi[par], ALU.mult).then_inc(S("dx"), 1)

            def gated(g, par):
                pool.wait_ge(S("y_read"), g + 1)
                pool.wait_ge(S("zs"), g + 1)
                pool.tensor_tensor(gate, gate, zs[par], ALU.mult).then_inc(S("gated"), 1)

            def step(g, par, last):
                if last is None:
                    gated(g - 1, 1 - par)
                    return
                for k in range(16):
                    j, m = divmod(k, 4)
                    pool.wait_ge(S("scan"), 16 * g + k + 1)
                    if k == 0:
                        pool.wait_ge(S("c_out"), g + 1)
                    part = states[j % 2][:, m * CH:(m + 1) * CH]
                    pool.tensor_tensor(part, part, cm[par], ALU.mult).then_inc(S("ch"), 1)
                    if k == 3 and has_post(g):
                        gated(g - 1, 1 - par)
                    if last is False:
                        if k == 7:
                            add_dt(g + 1)
                        if k == 8:
                            mul_dx(g + 1, 1 - par)

            add_dt(0)
            mul_dx(0, 0)
            schedule(step, pool.Fori)

        @block.vector
        def _(dve):
            def silu(name, out, g, bias):
                dve.wait_ge(S("sig"), 6 * g + (3 if name == "xi" else 6))
                if name == "xi" and not (isinstance(g, int) and g <= 1):
                    dve.wait_ge(S("y_read"), g - 1)
                dve.scalar_tensor_tensor(out, ps_p, bias, sig, ALU.add, ALU.mult).then_inc(S(name), 1)

            def split_rest(name, src, ready, parts, g):
                dve.wait_ge(S(f"{name}_part"), 3 * g + 1)
                if name == "dx":
                    dve.wait_ge(S("dt_part"), 3 * g + 3)
                elif not (isinstance(g, int) and g == 0):
                    dve.wait_ge(S("dx_part"), 3 * g)
                dve.tensor_tensor(rest, src, parts[0], ALU.subtract).then_inc(S(f"{name}_rest"), 1)

            def split_low(name, parts, g):
                dve.wait_ge(S(f"{name}_part"), 3 * g + 2)
                dve.tensor_tensor(parts[2], rest, parts[1], ALU.subtract).then_inc(S(f"{name}_part"), 1)

            def skip_add(g, par):
                dve.wait_ge(S("y_mm"), 4 * g + 4)
                if not (isinstance(g, int) and g == 0):
                    dve.wait_ge(S("o_mm"), g)
                dve.scalar_tensor_tensor(gate, xi[par], p(d + "_D"), ps_y, ALU.mult, ALU.add).then_inc(S("y_read"), 1)

            def pre(g, par, k):
                if k == 2:
                    silu("xi", xi[par], g, p(d + "_bxi"))
                if k == 5:
                    if not (isinstance(g, int) and g <= 1):
                        dve.wait_ge(S("gated"), g - 1)
                    silu("zs", zs[par], g, p(d + "_bz"))
                if k == 10:
                    split_rest("dt", dt, "dt", dt_part, g)
                if k == 11:
                    split_low("dt", dt_part, g)
                if k == 12:
                    split_rest("dx", dx, "dx", dx_part, g)
                if k == 13:
                    split_low("dx", dx_part, g)

            def step(g, par, last):
                if last is None:
                    skip_add(g - 1, 1 - par)
                    return
                for k in range(16):
                    j, m = divmod(k, 4)
                    n = 16 * g + k
                    part = states[j % 2][:, m * CH:(m + 1) * CH]
                    dve.wait_ge(S("dx_mm"), n + 1)
                    if k == 0:
                        dve.wait_ge(S("b_out"), g + 1)
                    if m == 0 and not (isinstance(g, int) and 4 * g + j < 2):
                        dve.wait_ge(S("y_mm"), 4 * g + j - 1)
                    dve.tensor_tensor(part, ps_dx, bm[par], ALU.mult).then_inc(S("inject"), 1)
                    dve.wait_ge(S("decay"), n + 1)
                    dve.wait_ge(S("inject"), n + 1)
                    dve.tensor_tensor_scan(part, decay[:, m * CH:(m + 1) * CH], part, 0.0, ALU.mult, ALU.add)\
                       .then_inc(S("scan"), 1)
                    if k == 2 and has_post(g):
                        skip_add(g - 1, 1 - par)
                    if last is False:
                        pre(g + 1, 1 - par, k)

            dve.memset(by_seq(decay)[:, :, 0:1], 0.0).then_inc(S("starts"), 1)
            for k in range(16):
                pre(0, 0, k)
            schedule(step, dve.Fori)


def route(core, ffn):
    nc, p, S = core.nc, core.p, core.sem
    x, tiles = core.x[:, :], COLS // 128
    wide = tiles * HALVES
    high, low = core.take(COLS // 2, F16), core.take(COLS // 2, F16)
    logits, first, second, key = (core.take(wide * EXPERTS) for _ in range(4))
    top, pick, second_top, ratio, weight = (core.take(wide) for _ in range(5))
    parts = core.take(wide * EXPERTS, F16)
    w_raw = core.take(2 * EXPERTS * HID)

    def write(act, c, chunk):
        return act.activation(x[:, c * CH:(c + 1) * CH], chunk, ACT.Copy)

    normalize(core, "hn", core.h[:, :], write)

    def rows(view):
        return view.rearrange("p (w e) -> p w e", e=EXPERTS)

    def spread(view):
        return view.unsqueeze(2).to_broadcast([128, wide, EXPERTS])

    def const(view):
        return view.unsqueeze(1).to_broadcast([128, wide, EXPERTS])

    part_view = parts.rearrange("p (t k u) -> p k t u", k=2, u=HALVES * EXPERTS)

    turned = [core.bank(4 + b).bitcast(F16)[0:64, :] for b in range(4)]

    with nc.Block() as block:
        @block.sync
        def _(sp):
            sp.dma_start(w_raw, ffn["wmoe"]).then_inc(S("wmoe_in"), 16)
            sp.dma_start(ffn["sel"], ffn["ffn16"]).then_inc(S("ffn16_in"), 16)
            sp.dma_start(ffn["w3"], ffn["w3_in"]).then_inc(S("w3_in"), 16)
            for i, part in enumerate((high, low)):
                sp.wait_ge(S("x_part"), i + 1)
                for q in range(HALVES):
                    dst = ffn["x"][64 * i:64 * i + 64, :].rearrange("p (g q t) -> p g q t", g=GROUPS, q=HALVES)
                    sp.dma_start(dst[:, :, q, :], part[64 * q:64 * q + 64, :].rearrange("p (g t) -> p g t", g=GROUPS))\
                      .then_inc(S("x_stacked"), 16)
            sp.wait_ge(S("x_stacked"), 64)
            sp.wait_ge(S("w3_in"), 16)

        @block.scalar
        def _(act):
            act.activation(high, x, ACT.Copy).then_inc(S("x_part"), 1)
            act.wait_ge(S("wmoe_in"), 16)
            act.activation(ffn["wh"], w_raw, ACT.Copy).then_inc(S("w_high"), 1)
            act.wait_ge(S("gap"), 1)
            act.activation(ratio, ratio, ACT.Exp).then_inc(S("ratio"), 1)
            for b in range(4):
                act.wait_ge(S("turned"), b + 1)
                act.activation(ffn["disp"][0:64, b * CH:(b + 1) * CH], turned[b], ACT.Copy).then_inc(S("disp_out"), 1)

        @block.tensor
        def _(pe):
            for t in range(tiles):
                mm = pe.matmul(core.bank(0, 2)[:, t * 32:(t + 1) * 32], x[:, t * 128:(t + 1) * 128], p("gate"),
                               start=True, stop=True)
            mm.then_inc(S("logits_mm"), 1)
            pe.wait_ge(S("parts"), 2)
            pe.wait_ge(S("ffn16_in"), 16)
            for t in range(tiles):
                mm = pe.transpose(turned[t // 8][:, (t % 8) * 128:(t % 8 + 1) * 128], parts[:, t * 64:(t + 1) * 64],
                                  ffn["ident"])
                if t % 8 == 7:
                    mm.then_inc(S("turned"), 1)

        @block.gpsimd
        def _(pool):
            pool.memset(ffn["disp"][64:128, :], 0.0).then_inc(S("disp_zero"), 1)

        @block.vector
        def _(dve):
            done = [0]

            def after():
                dve.wait_ge(S("route"), done[0])

            def mark(instruction):
                done[0] += 1
                instruction.then_inc(S("route"), 1)

            dve.wait_ge(S("x_part"), 1)
            dve.tensor_tensor(low, x, high, ALU.subtract).then_inc(S("x_part"), 1)
            dve.wait_ge(S("w_high"), 1)
            mark(dve.tensor_tensor(ffn["wl"], w_raw, ffn["wh"], ALU.subtract))
            dve.wait_ge(S("logits_mm"), 1)
            mark(dve.tensor_tensor(rows(logits), rows(core.bank(0, 2)), const(p("gate_b")), ALU.add))

            def pick_top(best, hot):
                after()
                mark(dve.tensor_reduce(best, rows(logits), AX.X, ALU.max))
                after()
                mark(dve.tensor_tensor(rows(key), rows(logits), spread(best), ALU.is_equal))
                after()
                mark(dve.tensor_tensor(rows(key), rows(key), const(p("rank")), ALU.mult))
                after()
                mark(dve.tensor_reduce(pick, rows(key), AX.X, ALU.max))
                after()
                mark(dve.tensor_tensor(rows(hot), rows(key), spread(pick), ALU.is_equal))

            pick_top(top, first)
            after()
            mark(dve.scalar_tensor_tensor(logits, first, -3e38, logits, ALU.mult, ALU.add))
            pick_top(second_top, second)
            after()
            dve.tensor_tensor(ratio, second_top, top, ALU.subtract).then_inc(S("gap"), 1)
            dve.wait_ge(S("ratio"), 1)
            mark(dve.tensor_scalar(weight, ratio, 1.0, None, ALU.add))
            after()
            mark(dve.reciprocal(weight, weight))
            after()
            mark(dve.tensor_tensor(ratio, ratio, weight, ALU.mult))
            mark(dve.tensor_tensor(rows(first), rows(first), spread(weight), ALU.mult))
            after()
            mark(dve.tensor_tensor(rows(second), rows(second), spread(ratio), ALU.mult))
            after()
            mark(dve.tensor_tensor(first, first, second, ALU.add))
            after()
            flat = first.rearrange("p (t u) -> p t u", u=HALVES * EXPERTS)
            dve.tensor_copy(part_view[:, 0], flat).then_inc(S("parts"), 1)
            dve.wait_ge(S("parts"), 1)
            dve.tensor_tensor(part_view[:, 1], flat, part_view[:, 0], ALU.subtract).then_inc(S("parts"), 1)


def experts(core, ffn, out):
    nc, S = core.nc, core.sem
    act_h = [core.take(CH) for _ in range(2)]
    hidden = [core.take(CH) for _ in range(2)]
    ps_1, ps_2, ps_d, ps_y = core.bank(0, 2), core.bank(2, 2), core.bank(4, 2), core.bank(6)

    def schedule(emit, loop):
        emit(0)
        with loop(1, GROUPS) as g:
            emit(g)

    def first_of_all(g, e, n=1):
        return isinstance(g, int) and e < n

    with nc.Block() as block:
        @block.tensor
        def _(pe):
            def tokens(g, q):
                return ffn["x"][:, bass.ds(g * GT + q * GC, GC)]

            def hidden_in(g, e, which, out_banks):
                for q in range(HALVES):
                    bank = out_banks[:, q * BANK:(q + 1) * BANK]
                    cols = slice((which * EXPERTS + e) * HID, (which * EXPERTS + e + 1) * HID)
                    pe.matmul(bank, ffn["wh"][:, cols], tokens(g, q), start=True, stop=False)
                    mm = pe.matmul(bank, ffn["wl"][:, cols], tokens(g, q), start=False, stop=True)
                return mm

            def expert_out(n, e):
                pe.wait_ge(S("hidden"), n + 1)
                for q in range(HALVES):
                    mm = pe.matmul(ps_y[64 * q:64 * q + 64, :], ffn["w3"][:, 64 * e:64 * e + 64],
                                   hidden[e % 2][:, q * BANK:(q + 1) * BANK], start=(e == 0), stop=(e == EXPERTS - 1))
                mm.then_inc(S("y_mm"), 1)

            def group(g):
                for e in range(EXPERTS):
                    n = EXPERTS * g + e
                    if not first_of_all(g, e):
                        pe.wait_ge(S("h1_act"), n)
                    hidden_in(g, e, 0, ps_1).then_inc(S("h1_mm"), 1)
                    if not first_of_all(g, e):
                        pe.wait_ge(S("h12"), n)
                    hidden_in(g, e, 1, ps_2).then_inc(S("h2_mm"), 1)
                    if not first_of_all(g, e):
                        pe.wait_ge(S("hidden"), n)
                    for q in range(HALVES):
                        at = (2 * e + q) * 128
                        mm = pe.matmul(ps_d[:, q * BANK:(q + 1) * BANK], ffn["dsel"][:, at:at + 128],
                                       ffn["disp"][:, bass.ds(g * GC, GC)], start=True, stop=True)
                    mm.then_inc(S("disp_mm"), 1)
                    if e > 0:
                        if e == 1 and not first_of_all(g, e, 2):
                            pe.wait_ge(S("y_added"), g)
                        expert_out(n - 1, e - 1)
                    elif not first_of_all(g, e):
                        expert_out(n - 1, EXPERTS - 1)

            schedule(group, pe.Fori)
            expert_out(EXPERTS * GROUPS - 1, EXPERTS - 1)

        @block.scalar
        def _(act):
            def group(g):
                for e in range(EXPERTS):
                    n = EXPERTS * g + e
                    act.wait_ge(S("h1_mm"), n + 1)
                    if not first_of_all(g, e, 2):
                        act.wait_ge(S("h12"), n - 1)
                    act.activation(act_h[e % 2], ps_1, ACT.Silu).then_inc(S("h1_act"), 1)

            act.preload_act_table_set("silu_and_others")
            schedule(group, act.Fori)

        @block.vector
        def _(dve):
            def add_out(g):
                dve.wait_ge(S("y_mm"), EXPERTS * g + EXPERTS)
                cols = core.h[:, bass.ds(g * GC, GC)]
                dve.tensor_tensor(cols, ps_y, cols, ALU.add).then_inc(S("y_added"), 1)

            def group(g):
                for e in range(EXPERTS):
                    n = EXPERTS * g + e
                    dve.wait_ge(S("h2_mm"), n + 1)
                    dve.wait_ge(S("h1_act"), n + 1)
                    if not first_of_all(g, e, 2):
                        dve.wait_ge(S("y_mm"), n - 1)
                    dve.tensor_tensor(hidden[e % 2], ps_2, act_h[e % 2], ALU.mult).then_inc(S("h12"), 1)
                    dve.wait_ge(S("disp_mm"), n + 1)
                    dve.wait_ge(S("h12"), n + 1)
                    dve.tensor_tensor(hidden[e % 2], ps_d, hidden[e % 2], ALU.mult).then_inc(S("hidden"), 1)
                    if e == 1 and not isinstance(g, int):
                        pass
                    if e == 0 and not isinstance(g, int):
                        add_out(g - 1)

            schedule(group, dve.Fori)
            add_out(GROUPS - 1)

        @block.sync
        def _(sp):
            with sp.Fori(0, GROUPS) as g:
                sp.wait_ge(S("y_added"), g + 1)
                cols = bass.ds(g * GC, GC)
                sp.dma_start(out[:, cols], core.h[:, cols]).then_inc(S("out"), 16)
            sp.wait_ge(S("out"), 16 * GROUPS)


def feed_forward(core, ffn16, wmoe, w3, out):
    sel = core.take((2 * EXPERTS + 1) * 128 // 2, F16)
    weights = EXPERTS * HID
    ffn = {"ffn16": ffn16, "wmoe": wmoe, "w3_in": w3, "sel": sel, "dsel": sel[:, 0:2 * EXPERTS * 128],
           "ident": sel[:, 2 * EXPERTS * 128:], "wh": core.take(weights, F16), "wl": core.take(weights, F16),
           "w3": core.take(EXPERTS * C), "x": core.take(GROUPS * GT // 2, F16), "disp": core.take(COLS // 2, F16)}
    kept = core.used
    route(core, ffn)
    core.used = kept
    experts(core, ffn, out)


def program(nc, xin, params, bsel, rsel, ffn16, wmoe, w3, out):
    core = Core(nc)
    with core.stage():
        setup(core, params, bsel, rsel)
    with core.stage():
        attention(core, xin)
    with core.stage():
        mix_input(core)
    with core.stage():
        mixer(core, "f")
    with core.stage():
        between_directions(core)
    with core.stage():
        mixer(core, "b")
    with core.stage():
        add_backward(core)
        feed_forward(core, ffn16, wmoe, w3, out)


def kernel(**inputs):
    import numpy as np
    import concourse.bacc as bacc
    from concourse.bass_utils import run_bass_kernel_spmd

    I = {k: np.asarray(v) for k, v in inputs.items()}
    f32 = np.float32

    def col(v):
        return np.asarray(v, f32).reshape(-1, 1)

    def both(v):
        return np.concatenate([col(v), col(v)])

    def diag(w):
        z = np.zeros_like(w)
        return np.concatenate([np.concatenate([w, z], 1), np.concatenate([z, w], 1)], 0)

    i = np.arange(128)
    same_half = (i[:, None] // 64 == i[None] // 64)
    mean = (same_half / 64).astype(f32)
    center = (np.eye(128) - same_half / 64).astype(f32)
    r = np.arange(32)
    sum_c = ((i[:, None] // 64 == (r[None] % 16) // 8) / 64).astype(f32)
    sum_d = (i[:, None] // 8 == r[None] % 16).astype(f32)
    ysel = np.concatenate([(8 * j + i[:, None] // 16 == r[None]) for j in range(4)], 1).astype(f32)
    dup = -((i % 32) // 16).astype(f32).reshape(-1, 1)
    bsel = np.concatenate([(i[:, None] // 32 == g) & (i[:, None] % 16 == i[None] // 8) for g in range(4)], 1)
    r96 = np.arange(96)
    rsel = np.concatenate([r96[:, None] % 32 == 8 * j + i[None] // 16 for j in range(4)], 1)
    r128 = np.arange(128)
    dsel = np.concatenate([np.tile(((r128[:, None] < 64) & (r128[:, None] % 32 == 16 * q + e)), (1, 128))
                           for e in range(EXPERTS) for q in range(2)], 1)
    ident = np.eye(128)

    def ph(w):
        return w.reshape((HEADS, SP) + w.shape[1:]).swapaxes(0, 1).reshape((DI,) + w.shape[1:])

    kv = I["L0_tok_Wkv"]
    pieces = {"mean": mean, "sum_c": sum_c, "sum_d": sum_d, "center": center, "ysel": ysel, "dup": dup,
              "wq": diag(I["L0_tok_Wq"].T), "wk": diag(kv[:64].T), "wv": diag(kv[64:].T),
              "proj": diag(I["L0_tok_proj_w"].T), "lnq_w": both(I["L0_tok_ln_q_w"]),
              "lnq_b": both(I["L0_tok_ln_q_b"]), "lnkv_w": both(I["L0_tok_ln_kv_w"]),
              "lnkv_b": both(I["L0_tok_ln_kv_b"]), "proj_b": both(I["L0_tok_proj_b"])}
    for d in "fb":
        a = {k[len("L0_attn_f_"):]: v for k, v in I.items() if k.startswith(f"L0_attn_{d}_")}
        xi_w, z_w = ph(a["in_proj_w"][:DI]).T, ph(a["in_proj_w"][DI:]).T
        zero = np.zeros_like(xi_w)
        top, bottom = (lambda w: np.concatenate([w, zero])), (lambda w: np.concatenate([zero, w]))
        xp, xb = a["x_proj_w"], a["x_proj_b"]
        rows = np.concatenate([ph(xp[:DI]), xp[DI:]])
        pieces |= {d + "_win": np.concatenate([top(xi_w), bottom(xi_w), top(z_w), bottom(z_w)], 1),
                   d + "_wx": ph(rows.T), d + "_wo": ph(a["out_proj_w"].T),
                   d + "_alog": a["A_log"].reshape(HEADS, SP, SN).swapaxes(1, 2).reshape(HEADS * SN, SP),
                   d + "_bxi": col(ph(a["in_proj_b"][:DI])), d + "_bz": col(ph(a["in_proj_b"][DI:])),
                   d + "_bdt": col(ph(xb[:DI])), d + "_dtb": col(ph(a["dt_bias"])),
                   d + "_bB": col(xb[DI:2 * DI]), d + "_bC": col(xb[2 * DI:]), d + "_D": col(ph(a["D_skip"])),
                   d + "_bo": both(a["out_proj_b"])}
    conv = I["L0_attn_conv_w"].reshape(C, 3)
    pieces |= {"norm_w": both(I["L0_attn_norm_w"]), "norm_b": both(I["L0_attn_norm_b"]),
               "conv_w": np.concatenate([conv, conv]), "conv_b": both(I["L0_attn_conv_b"]),
               "gate": diag(I["L0_ffn_gate_w"]), "gate_b": np.tile(I["L0_ffn_gate_b"].reshape(1, -1), (128, 1)),
               "rank": np.tile(np.arange(EXPERTS, 0, -1).astype(f32).reshape(1, -1), (128, 1))}
    params = np.concatenate([pieces[name] for name, _ in PARTS], 1).astype(f32)

    x = I["x"].reshape(GROUPS, HALVES, 2, C, T // 16, STRIDE, 16, STRIDE)
    x = x.transpose(0, 2, 1, 3, 5, 7, 4, 6).reshape(STEPS, 128, PIX)
    moe = [np.concatenate([w, w]) for w in (I["L0_ffn_w1"].transpose(1, 0, 2).reshape(C, -1),
                                            I["L0_ffn_w2"].transpose(1, 0, 2).reshape(C, -1))]
    arrays = {"xin": np.ascontiguousarray(x), "params": params,
              "bsel": bsel.astype(np.float16), "rsel": rsel.astype(mybir.dt.np(BF16)),
              "ffn16": np.concatenate([dsel, ident], 1).astype(np.float16),
              "wmoe": np.concatenate(moe, 1),
              "w3": np.ascontiguousarray(I["L0_ffn_w3"].transpose(1, 0, 2).reshape(HID, -1))}

    nc = bacc.Bacc("TRN2", target_bir_lowering=False, num_devices=1)
    aps = [nc.dram_tensor("in_" + k, v.shape, mybir.dt.from_np(v.dtype), kind="ExternalInput").ap() for k, v in arrays.items()]
    out = nc.dram_tensor("out", (128, COLS), F32, kind="ExternalOutput").ap()
    program(nc, *aps, out)
    got = run_bass_kernel_spmd(nc, [{"in_" + k: v for k, v in arrays.items()}], core_ids=[0]).results[0]["out"]
    return got.reshape(HALVES, C, GROUPS, 2, T).transpose(2, 0, 3, 4, 1).reshape(BATCH, T, C)
```

```python
from contextlib import contextmanager

import concourse.bass as bass
from concourse import mybir

F32 = mybir.dt.float32
F16 = mybir.dt.float16
BF16 = mybir.dt.bfloat16
ALU = mybir.AluOpType
ACT = mybir.ActivationFunctionType
AX = mybir.AxisListType

BATCH, C, SIDE, STRIDE, HEADS = 32, 64, 64, 4, 8
D = C // HEADS
T = (SIDE // STRIDE) ** 2
N = STRIDE * STRIDE
PIX = N * T
HALVES = 2
STEPS = BATCH // HALVES
GROUPS = STEPS // 2
COLS = STEPS * T
GC = COLS // GROUPS
GT = HALVES * GC
DI, SN = 128, 16
SP = DI // HEADS
EXPERTS, HID = 16, 128
EPS = 1e-5
BANK = 512
CH = 2 * BANK
KCH = PIX // CH
TQ = T // 4

PARTS = [("mean", 128), ("sum_c", 32), ("sum_d", 32), ("center", 128), ("ysel", 128), ("dup", 1),
         ("wq", 128), ("wk", 128), ("wv", 128), ("proj", 128),
         ("lnq_w", 1), ("lnq_b", 1), ("lnkv_w", 1), ("lnkv_b", 1), ("proj_b", 1)]
for _d in "fb":
    PARTS += [(_d + "_win", 512), (_d + "_wx", 384), (_d + "_wo", 64), (_d + "_alog", 16), (_d + "_bxi", 1),
              (_d + "_bz", 1), (_d + "_bdt", 1), (_d + "_dtb", 1), (_d + "_bB", 1), (_d + "_bC", 1),
              (_d + "_skip", 128), (_d + "_bo", 1)]
PARTS += [("norm_w", 1), ("norm_b", 1), ("conv_w", 3), ("conv_b", 1), ("gate", 32), ("gate_b", 16), ("rank", 16)]
AT, _n = {}, 0
for _name, _w in PARTS:
    AT[_name] = (_n, _w)
    _n += _w
PACKED = _n


class Core:

    def __init__(self, nc):
        self.nc = nc
        self.sems = {}
        self.pack = nc.alloc_sbuf_tensor("pack", [128, PACKED], F32)
        self.bsel = nc.alloc_sbuf_tensor("bsel", [128, 4 * 128], F16)
        self.rsel = nc.alloc_sbuf_tensor("rsel", [96, 4 * 128], BF16)
        self.wq = nc.alloc_sbuf_tensor("wq_folded", [128, 128], F32)
        self.wk = nc.alloc_sbuf_tensor("wk_folded", [128, 128], F32)
        self.wv = nc.alloc_sbuf_tensor("wv_folded", [128, 128], F32)
        self.cols = nc.alloc_sbuf_tensor("cols", [128, 16], F32)
        self.neg_a = nc.alloc_sbuf_tensor("neg_a", [128, 2 * SP], F32)
        self.h = nc.alloc_sbuf_tensor("h", [128, COLS], F32)
        self.x = nc.alloc_sbuf_tensor("x_norm", [128, COLS], F32)
        self.arena_words = 38900
        self.arena = nc.alloc_sbuf_tensor("arena", [128, self.arena_words], F32)
        self.psum = nc.alloc_psum_tensor("psum", [128, 8 * BANK], F32)
        self.used = 0

    def p(self, name, i=0, w=None):
        at, width = AT[name]
        return self.pack[:, at + i:at + i + (width if w is None else w)]

    def sem(self, name):
        if name not in self.sems:
            self.sems[name] = self.nc.alloc_semaphore(name)
        return self.sems[name]

    @contextmanager
    def stage(self):
        self.used, self.sems = 0, {}
        yield
        self.nc.all_engine_barrier()
        self.nc.clear_and_free_semaphores(list(self.sems.values()))
        self.nc.all_engine_barrier()

    def take(self, words, dtype=F32):
        at, self.used = self.used, self.used + words
        assert self.used <= self.arena_words, self.used
        view = self.arena[:, at:at + words]
        return view if dtype == F32 else view.bitcast(dtype)

    def bank(self, b, n=1):
        return self.psum[:, b * BANK:(b + n) * BANK]


def setup(core, params, bsel, rsel):
    nc, p, S = core.nc, core.p, core.sem
    t = core.take(512)
    with nc.Block() as block:
        @block.sync
        def _(sp):
            sp.dma_start(core.pack[:, :], params).then_inc(S("params_in"), 16)
            sp.dma_start(core.bsel[:, :], bsel).then_inc(S("params_in"), 16)
            sp.dma_start(core.rsel[:, :], rsel).then_inc(S("params_in"), 16)
            sp.wait_ge(S("params_in"), 48)

        @block.vector
        def _(dve):
            dve.wait_ge(S("params_in"), 48)
            dve.tensor_scalar(t[:, 0:128], p("wq"), p("lnq_w"), None, ALU.mult)
            dve.tensor_scalar(t[:, 128:256], p("wk"), p("lnkv_w"), None, ALU.mult)
            dve.tensor_scalar(t[:, 256:384], p("wv"), p("lnkv_w"), None, ALU.mult).then_inc(S("fold_scaled"), 1)
            for i, d in enumerate("fb"):
                dve.tensor_scalar(core.cols[:, 4 + 4 * i:5 + 4 * i], p(d + "_bxi"), 0.5, None, ALU.mult)
                dve.tensor_scalar(core.cols[:, 5 + 4 * i:6 + 4 * i], p(d + "_bz"), 0.5, None, ALU.mult)
                dve.tensor_tensor(core.cols[:, 6 + 4 * i:7 + 4 * i], p(d + "_bdt"), p(d + "_dtb"), ALU.add)
            dve.wait_ge(S("fold_mm"), 1)
            dve.tensor_scalar(core.wq[:, :], core.bank(0)[:, 0:128], C ** -0.5 / N, None, ALU.mult)
            dve.tensor_copy(core.wk[:, :], core.bank(0)[:, 128:256])
            dve.tensor_copy(core.wv[:, :], core.bank(0)[:, 256:384])
            dve.tensor_scalar(core.cols[:, 0:1], core.bank(1)[:, 0:1], C ** -0.5, None, ALU.mult)
            dve.tensor_copy(core.cols[:, 1:2], core.bank(1)[:, 1:2]).then_inc(S("bias_v"), 1)
            dve.wait_ge(S("bias_o_mm"), 1)
            dve.tensor_tensor(core.cols[:, 2:3], core.bank(2)[:, 0:1], p("proj_b"), ALU.add)
            dve.wait_ge(S("a_exp"), 1)
            dve.tensor_scalar(core.neg_a[:, :], core.neg_a[:, :], -1.0, None, ALU.mult)

        @block.tensor
        def _(pe):
            pe.wait_ge(S("fold_scaled"), 1)
            for i in range(3):
                pe.matmul(core.bank(0)[:, 128 * i:128 * (i + 1)], p("center"), t[:, 128 * i:128 * (i + 1)],
                          start=True, stop=True)
            pe.matmul(core.bank(1)[:, 0:1], p("wq"), p("lnq_b"), start=True, stop=True)
            pe.matmul(core.bank(1)[:, 1:2], p("wv"), p("lnkv_b"), start=True, stop=True).then_inc(S("fold_mm"), 1)
            pe.wait_ge(S("bias_v"), 1)
            pe.matmul(core.bank(2)[:, 0:1], p("proj"), core.cols[:, 1:2], start=True, stop=True)\
              .then_inc(S("bias_o_mm"), 1)

        @block.scalar
        def _(act):
            act.preload_act_table_set("natural_log_exp_and_others")
            act.wait_ge(S("params_in"), 48)
            act.activation(core.neg_a[:, 0:SP], p("f_alog"), ACT.Exp)
            act.activation(core.neg_a[:, SP:2 * SP], p("b_alog"), ACT.Exp).then_inc(S("a_exp"), 1)


def attention(core, xin):
    nc, p, S = core.nc, core.p, core.sem
    xt = [core.take(PIX) for _ in range(2)]
    xsq = core.take(PIX)
    kq = core.take(PIX)
    v = [core.take(PIX) for _ in range(2)]
    mean_t = core.take(8 * T)
    rf, rf_sq, q_musq, q_rstd, q, av_sum = (core.take(T) for _ in range(6))
    musq = core.take(CH)
    rstd = [core.take(CH) for _ in range(2)]
    prob = core.take(CH)
    gain = core.take(CH)
    hi = core.take(CH // 2, F16)
    prob16 = core.take(CH // 2, F16)
    top, den, rden = (core.take(TQ) for _ in range(3))
    slot = [core.bank(0, 2), core.bank(2, 2)]
    rows = core.bank(4, 2)
    small = core.bank(6)
    qb = core.bank(7)
    q_bias, o_bias = core.cols[:, 0:1], core.cols[:, 2:3]

    def bcast_n(view, n):
        return view.unsqueeze(1).to_broadcast([128, n, view.shape[-1]])

    def by_n(view):
        return view.rearrange("p (n t) -> p n t", n=N)

    def schedule(emit, loop):
        emit(0, 0, front=True, back=False, pre=True)
        emit(1, 1, front=True, back=True, pre=True)
        with loop(1, STEPS // 2 - 1) as k:
            emit(2 * k, 0, front=True, back=True, pre=True)
            emit(2 * k + 1, 1, front=True, back=True, pre=True)
        emit(STEPS - 2, 0, front=True, back=True, pre=True)
        emit(STEPS - 1, 1, front=True, back=True, pre=False)
        emit(STEPS, 0, front=False, back=True, pre=False)

    def later(s, n):
        return not isinstance(s, int) or s >= n

    with nc.Block() as block:
        @block.sync
        def _(sp):
            def load(s, par):
                if later(s, 2):
                    sp.wait_ge(S("v_mm"), KCH * (s - 1))
                sp.dma_start(xt[par], xin[s]).then_inc(S(f"x_in{par}"), 16)

            load(0, 0)
            load(1, 1)
            with sp.Fori(1, STEPS // 2) as k:
                load(2 * k, 0)
                load(2 * k + 1, 1)

        @block.gpsimd
        def _(pool):
            def pre(s, par):
                pool.wait_ge(S(f"x_in{par}"), 8 * (s - par) + 16)
                if later(s, 1):
                    pool.wait_ge(S("rf_sum"), s)
                x = xt[par]
                pool.tensor_tensor(mean_t, x[:, 0:8 * T], x[:, 8 * T:16 * T], ALU.add).then_inc(S("mean_part"), 1)
                for i, n in enumerate((4, 2)):
                    pool.wait_ge(S("mean_part"), 3 * s + i + 1)
                    pool.tensor_tensor(mean_t[:, 0:n * T], mean_t[:, 0:n * T], mean_t[:, n * T:2 * n * T], ALU.add)\
                        .then_inc(S("mean_part"), 1)
                pool.wait_ge(S("mean_part"), 3 * s + 3)
                if later(s, 1):
                    pool.wait_ge(S("q_mm"), s)
                    pool.wait_ge(S("h_base"), s)
                pool.tensor_tensor(rf, mean_t[:, 0:T], mean_t[:, T:2 * T], ALU.add).then_inc(S("rf_sum"), 1)

            def step(s, par, front, back, pre):
                if pre:
                    pre_(s + 1, 1 - par)
                if front:
                    pool.wait_ge(S("s_max"), s + 1)
                    pool.tensor_tensor(by_n(prob), by_n(prob), bcast_n(top, N), ALU.subtract)\
                        .then_inc(S("s_centred"), 1)
                    pool.wait_ge(S("inv_den"), s + 1)
                    pool.tensor_tensor(by_n(gain), by_n(rstd[par]), bcast_n(rden, N), ALU.mult)\
                        .then_inc(S("gain"), 1)
                    pool.wait_ge(S("gain"), s + 1)
                    pool.tensor_tensor(prob, prob, gain, ALU.mult).then_inc(S("prob"), 1)

            pre_ = pre
            pre_(0, 0)
            schedule(step, pool.Fori)

        @block.scalar
        def _(act):
            def pre_x(s, par):
                act.wait_ge(S(f"x_in{par}"), 8 * (s - par) + 16)
                if later(s, 1):
                    act.wait_ge(S("sum_x2"), s)
                act.activation(xsq, xt[par], ACT.Square).then_inc(S("x_sq"), 1)

            def pre_rf(s):
                act.wait_ge(S("rf_sum"), s + 1)
                act.activation(rf_sq, rf, ACT.Square, scale=1.0 / N).then_inc(S("rf_sq"), 1)
                act.activation(core.h[:, bass.ds(s * T, T)], rf, ACT.Identity, bias=o_bias, scale=1.0 / N)\
                   .then_inc(S("h_base"), 1)

            def pre_stats(s, par):
                act.wait_ge(S("q_stats"), s + 1)
                act.activation(q_musq, small[:, 0:T], ACT.Square, scale=1.0 / N).then_inc(S("q_musq"), 1)
                act.wait_ge(S("sum_x"), s + 1)
                act.activation(musq, rows, ACT.Square).then_inc(S("x_musq"), 1)
                act.wait_ge(S("q_var"), s + 1)
                act.activation(q_rstd, q_rstd, ACT.Ln, bias=EPS).then_inc(S("q_ln"), 1)
                act.wait_ge(S("q_ln"), s + 1)
                act.activation(q_rstd, q_rstd, ACT.Exp, scale=-0.5).then_inc(S("q_rstd"), 1)
                act.wait_ge(S("x_var"), s + 1)
                act.activation(rstd[par], rstd[par], ACT.Ln, bias=EPS).then_inc(S("x_ln"), 1)
                act.wait_ge(S("x_ln"), s + 1)
                act.activation(rstd[par], rstd[par], ACT.Exp, scale=-0.5).then_inc(S("x_rstd"), 1)

            def step(s, par, front, back, pre):
                if pre:
                    pre_x(s + 1, 1 - par)
                if front:
                    for c in range(KCH):
                        act.wait_ge(S("v_mm"), KCH * s + c + 1)
                        if c == 0 and later(s, 2):
                            act.wait_ge(S("av_sum"), s - 1)
                        act.activation(v[par][:, c * CH:(c + 1) * CH], slot[c % 2], ACT.Copy).then_inc(S("v_out"), 1)
                if pre:
                    pre_rf(s + 1)
                if front:
                    act.wait_ge(S("s_centred"), s + 1)
                    act.activation(prob, prob, ACT.Exp).then_inc(S("s_exp"), 1)
                if pre:
                    pre_stats(s + 1, 1 - par)
                if front:
                    act.wait_ge(S("prob"), s + 1)
                    act.activation(hi, prob, ACT.Copy).then_inc(S("prob_hi"), 1)

            act.preload_act_table_set("natural_log_exp_and_others")
            pre_x(0, 0)
            pre_rf(0)
            pre_stats(0, 0)
            schedule(step, act.Fori)

        @block.vector
        def _(dve):
            def pre(s, par):
                dve.wait_ge(S("q_musq"), s + 1)
                dve.tensor_tensor(q_rstd, small[:, T:2 * T], q_musq, ALU.subtract).then_inc(S("q_var"), 1)
                dve.wait_ge(S("sum_x2"), s + 1)
                dve.tensor_tensor(rstd[par], rows, musq, ALU.subtract).then_inc(S("x_var"), 1)
                dve.wait_ge(S("q_rstd"), s + 1)
                dve.tensor_tensor(q, qb[:, 0:T], q_rstd, ALU.mult).then_inc(S("q_scaled"), 1)
                dve.wait_ge(S("q_scaled"), s + 1)
                dve.tensor_scalar(q, q, q_bias, None, ALU.add).then_inc(S("q_out"), 1)

            def halve(view, n, s, i):
                dve.tensor_tensor(view[:, 0:n * T], view[:, 0:n * T], view[:, n * T:2 * n * T], ALU.add)\
                   .then_inc(S("av_part"), 1)
                dve.wait_ge(S("av_part"), 3 * (s - 1) + i + 1)

            def step(s, par, front, back, pre_next):
                for c in range(KCH):
                    if back:
                        dve.wait_ge(S("a_mm"), KCH * (s - 1) + c + 1)
                        if c == 0:
                            dve.wait_ge(S("v_out"), KCH * s)
                        quarter = by_n(v[1 - par])[:, :, c * TQ:(c + 1) * TQ]
                        dve.tensor_tensor(quarter, by_n(slot[0]), quarter, ALU.mult).then_inc(S("av"), 1)
                    if front:
                        dve.wait_ge(S("k_mm"), KCH * s + c + 1)
                        if c == 0:
                            dve.wait_ge(S("q_out"), s + 1)
                            if later(s, 1):
                                dve.wait_ge(S("scores"), s)
                        dve.tensor_tensor(kq[:, c * CH:(c + 1) * CH].rearrange("p (n t) -> p n t", t=T),
                                          slot[1].rearrange("p (n t) -> p n t", t=T), bcast_n(q, CH // T), ALU.mult)\
                           .then_inc(S("kq"), 1)
                if back:
                    dve.wait_ge(S("av"), KCH * s)
                    halve(v[1 - par], 8, s, 0)
                if front:
                    dve.wait_ge(S("scores"), s + 1)
                    dve.wait_ge(S("x_rstd"), s + 1)
                    dve.tensor_tensor(prob, rows, rstd[par], ALU.mult).then_inc(S("s_scaled"), 1)
                    dve.wait_ge(S("s_scaled"), s + 1)
                    dve.tensor_reduce(top, prob.rearrange("p (n t) -> p t n", n=N), AX.X, ALU.max)\
                       .then_inc(S("s_max"), 1)
                if back:
                    halve(v[1 - par], 4, s, 1)
                    halve(v[1 - par], 2, s, 2)
                    if later(s, 2):
                        dve.wait_ge(S("o_mm"), s - 1)
                    w = v[1 - par]
                    dve.tensor_tensor(av_sum, w[:, 0:T], w[:, T:2 * T], ALU.add).then_inc(S("av_sum"), 1)
                if front:
                    dve.wait_ge(S("s_exp"), s + 1)
                    dve.tensor_reduce(den, prob.rearrange("p (n t) -> p t n", n=N), AX.X, ALU.add)\
                       .then_inc(S("s_den"), 1)
                    dve.wait_ge(S("s_den"), s + 1)
                    dve.reciprocal(rden, den).then_inc(S("inv_den"), 1)
                if pre_next:
                    pre(s + 1, 1 - par)
                if front:
                    dve.wait_ge(S("prob_hi"), s + 1)
                    dve.scalar_tensor_tensor(prob16, hi, p("dup"), prob, ALU.mult, ALU.add).then_inc(S("prob16"), 1)
                if back:
                    dve.wait_ge(S("o_mm"), s)
                    cols = core.h[:, bass.ds((s - 1) * T, T)]
                    dve.tensor_tensor(cols, qb[:, T:2 * T], cols, ALU.add).then_inc(S("h_out"), 1)

            pre(0, 0)
            schedule(lambda s, par, front, back, pre: step(s, par, front, back, pre), dve.Fori)

        @block.tensor
        def _(pe):
            def quarters(weights, source, start_wait):
                for half in range(2):
                    for g in range(4):
                        view = by_n(source)[:, half * 8:half * 8 + 8, g * TQ:(g + 1) * TQ]
                        mm = pe.matmul(rows[32 * g:32 * g + 32, half * BANK:(half + 1) * BANK], weights, view,
                                       start=True, stop=True)
                return mm

            def pre(s, par):
                pe.wait_ge(S("rf_sq"), s + 1)
                if later(s, 1):
                    pe.wait_ge(S("q_var"), s)
                    pe.wait_ge(S("q_scaled"), s)
                pe.matmul(small[:, 0:T], p("mean"), rf, start=True, stop=True)
                pe.matmul(small[:, T:2 * T], p("mean"), rf_sq, start=True, stop=True).then_inc(S("q_stats"), 1)
                pe.matmul(qb[:, 0:T], core.wq[:, :], rf, start=True, stop=True).then_inc(S("q_mm"), 1)
                pe.wait_ge(S(f"x_in{par}"), 8 * (s - par) + 16)
                if later(s, 1):
                    pe.wait_ge(S("s_scaled"), s)
                quarters(p("sum_c"), xt[par], None).then_inc(S("sum_x"), 1)
                pe.wait_ge(S("x_sq"), s + 1)
                pe.wait_ge(S("x_musq"), s + 1)
                quarters(p("sum_c"), xsq, None).then_inc(S("sum_x2"), 1)

            def project(weights, source, dst):
                for b in range(2):
                    mm = pe.matmul(dst[:, b * BANK:(b + 1) * BANK], weights, source[:, b * BANK:(b + 1) * BANK],
                                   start=True, stop=True)
                return mm

            def step(s, par, front, back, pre_next):
                for c in range(KCH):
                    if back:
                        if c == 0:
                            pe.wait_ge(S("prob16"), s)
                            pe.wait_ge(S("v_out"), KCH * s - 1)
                        else:
                            pe.wait_ge(S("av"), KCH * (s - 1) + c)
                        project(core.bsel[:, c * 128:(c + 1) * 128], prob16, slot[0]).then_inc(S("a_mm"), 1)
                    if front:
                        if c > 0:
                            pe.wait_ge(S("kq"), KCH * s + c)
                        elif later(s, 1):
                            pe.wait_ge(S("v_out"), KCH * s)
                        project(core.wk[:, :], xt[par][:, c * CH:(c + 1) * CH], slot[1]).then_inc(S("k_mm"), 1)
                if front:
                    for c in range(KCH):
                        if c == 0 and back:
                            pe.wait_ge(S("av"), KCH * s)
                        if c == 1:
                            pe.wait_ge(S("kq"), KCH * (s + 1))
                        if c >= 2:
                            pe.wait_ge(S("v_out"), KCH * s + c - 1)
                        project(core.wv[:, :], xt[par][:, c * CH:(c + 1) * CH], slot[c % 2]).then_inc(S("v_mm"), 1)
                        if c == 0:
                            pe.wait_ge(S("kq"), KCH * (s + 1))
                            pe.wait_ge(S("x_var"), s + 1)
                            quarters(p("sum_d"), kq, None).then_inc(S("scores"), 1)
                if back:
                    pe.wait_ge(S("av_sum"), s)
                    if later(s, 2):
                        pe.wait_ge(S("h_out"), s - 1)
                    pe.matmul(qb[:, T:2 * T], p("proj"), av_sum, start=True, stop=True).then_inc(S("o_mm"), 1)
                if pre_next:
                    pre(s + 1, 1 - par)

            pre(0, 0)
            schedule(lambda s, par, front, back, pre: step(s, par, front, back, pre), pe.Fori)


def normalize(core, tag, src, write, extra=None):
    nc, p = core.nc, core.p
    S = lambda name: core.sem(f"{tag}_{name}")
    sq, musq, rstd, cen = ([core.take(CH) for _ in range(2)] for _ in range(4))
    extra = extra or {}
    chunks = COLS // CH

    with nc.Block() as block:
        @block.tensor
        def _(pe):
            for c in range(chunks):
                mean, square = core.bank(4 * (c % 2), 2), core.bank(4 * (c % 2) + 2, 2)
                if c >= 2:
                    pe.wait_ge(S("centred"), c - 1)
                    pe.wait_ge(S("var"), c - 1)
                for b in range(2):
                    cols = slice(b * BANK, (b + 1) * BANK)
                    mm = pe.matmul(mean[:, cols], p("mean"), src[:, c * CH:(c + 1) * CH][:, cols], start=True, stop=True)
                mm.then_inc(S("mean"), 1)
                pe.wait_ge(S("sq"), c + 1)
                for b in range(2):
                    cols = slice(b * BANK, (b + 1) * BANK)
                    mm = pe.matmul(square[:, cols], p("mean"), sq[c % 2][:, cols], start=True, stop=True)
                mm.then_inc(S("mean_sq"), 1)

        @block.scalar
        def _(act):
            act.preload_act_table_set("natural_log_exp_and_others")
            def square(c):
                if c >= 2:
                    act.wait_ge(S("mean_sq"), c - 1)
                act.activation(sq[c % 2], src[:, c * CH:(c + 1) * CH], ACT.Square).then_inc(S("sq"), 1)

            square(0)
            for c in range(chunks):
                if c + 1 < chunks:
                    square(c + 1)
                act.wait_ge(S("mean"), c + 1)
                if c >= 2:
                    act.wait_ge(S("var"), c - 1)
                act.activation(musq[c % 2], core.bank(4 * (c % 2), 2), ACT.Square).then_inc(S("musq"), 1)
                act.wait_ge(S("var"), c + 1)
                act.activation(rstd[c % 2], rstd[c % 2], ACT.Ln, bias=EPS).then_inc(S("ln"), 1)
                act.wait_ge(S("ln"), c + 1)
                act.activation(rstd[c % 2], rstd[c % 2], ACT.Exp, scale=-0.5).then_inc(S("rstd"), 1)
                act.wait_ge(S("scaled"), c + 1)
                write(act, c, cen[c % 2]).then_inc(S("written"), 1)
            if "act" in extra:
                extra["act"](act)

        @block.vector
        def _(dve):
            for c in range(chunks):
                if c >= 2:
                    dve.wait_ge(S("scaled"), c - 1)
                dve.wait_ge(S("mean_sq"), c + 1)
                dve.wait_ge(S("musq"), c + 1)
                dve.tensor_tensor(rstd[c % 2], core.bank(4 * (c % 2) + 2, 2), musq[c % 2], ALU.subtract)\
                   .then_inc(S("var"), 1)
                if c >= 2:
                    dve.wait_ge(S("written"), c - 1)
                dve.tensor_tensor(cen[c % 2], src[:, c * CH:(c + 1) * CH], core.bank(4 * (c % 2), 2), ALU.subtract)\
                   .then_inc(S("centred"), 1)
                dve.wait_ge(S("rstd"), c + 1)
                dve.wait_ge(S("centred"), c + 1)
                dve.tensor_tensor(cen[c % 2], cen[c % 2], rstd[c % 2], ALU.mult).then_inc(S("scaled"), 1)
            if "dve" in extra:
                extra["dve"](dve)


def by_seq(view):
    return view.rearrange("p (s t) -> p s t", t=T)


def mix_input(core):
    p, S = core.p, core.sem
    conv = core.take(COLS)
    x = core.x[:, :]

    def write(act, c, chunk):
        return act.activation(x[:, c * CH:(c + 1) * CH], chunk, ACT.Copy)

    def dve_conv(dve):
        dve.wait_ge(S("xn_written"), COLS // CH)
        dve.tensor_scalar(conv, x, p("conv_w", 1, 1), None, ALU.mult).then_inc(S("conv"), 1)
        dve.wait_ge(S("conv"), 1)
        after, before = by_seq(conv)[:, :, 1:T], by_seq(conv)[:, :, 0:T - 1]
        dve.scalar_tensor_tensor(after, by_seq(x)[:, :, 0:T - 1], p("conv_w", 0, 1), after, ALU.mult, ALU.add)\
           .then_inc(S("conv"), 1)
        dve.wait_ge(S("conv"), 2)
        dve.scalar_tensor_tensor(before, by_seq(x)[:, :, 1:T], p("conv_w", 2, 1), before, ALU.mult, ALU.add)\
           .then_inc(S("conv"), 1)
        dve.wait_ge(S("conv_gelu"), 1)
        dve.tensor_tensor(core.h[:, :], core.h[:, :], conv, ALU.add).then_inc(S("conv_added"), 1)

    def act_gelu(act):
        act.wait_ge(S("conv"), 3)
        act.activation(conv, conv, ACT.Gelu, bias=p("conv_b")).then_inc(S("conv_gelu"), 1)

    normalize(core, "xn", core.h[:, :], write, {"dve": dve_conv, "act": act_gelu})


def between_directions(core):
    p = core.p
    x = core.x[:, :]

    def write(act, c, chunk):
        return act.activation(by_seq(x[:, c * CH:(c + 1) * CH])[:, :, ::-1], by_seq(chunk), ACT.Identity,
                              bias=p("norm_b"), scale=p("norm_w"))

    normalize(core, "yn", x, write)


def add_backward(core):
    with core.nc.Block() as block:
        @block.vector
        def _(dve):
            dve.tensor_tensor(by_seq(core.h[:, :]), by_seq(core.h[:, :]), by_seq(core.x[:, :])[:, :, ::-1], ALU.add)


def mixer(core, d):
    nc, p = core.nc, core.p
    S = lambda name: core.sem(f"{d}_{name}")
    di = "fb".index(d)
    half_bxi, half_bz, b_dt = (core.cols[:, 4 + 4 * di + i:5 + 4 * di + i] for i in range(3))
    neg_a = core.neg_a[:, di * SP:(di + 1) * SP]
    decay = core.take(4 * CH)
    states = [core.take(4 * CH) for _ in range(2)]
    xi, bm, cm = ([core.take(CH) for _ in range(2)] for _ in range(3))
    zs, pre_act, sig, dt, dx, rest, gate = (core.take(CH) for _ in range(7))
    dt_part = [core.take(CH // 2, BF16) for _ in range(3)]
    dx_part = [core.take(CH // 2, BF16) for _ in range(3)]
    dt_rows = [core.take(4 * CH // 2, BF16) for _ in range(2)]
    dx_rows = [core.take(4 * CH // 2, BF16) for _ in range(2)]
    ps_dt, ps_dx, ps_y, ps_p = (core.bank(b, 2) for b in (0, 2, 4, 6))
    ps_o = ps_p[:, 0:BANK]

    def schedule(emit, loop):
        emit(0, 0, last=False)
        with loop(0, (GROUPS - 2) // 2) as k:
            emit(2 * k + 1, 1, last=False)
            emit(2 * k + 2, 0, last=False)
        emit(GROUPS - 1, 1, last=True)
        emit(GROUPS, 0, last=None)

    def wait_past(eng, name, count, g, first):
        if not isinstance(g, int) or g >= first:
            eng.wait_ge(S(name), count)

    def has_post(g):
        return not isinstance(g, int) or g >= 1

    with nc.Block() as block:
        @block.sync
        def _(sp):
            def spread(g, par, name, parts, rows):
                for i in range(3):
                    sp.wait_ge(S(f"{name}_part"), 3 * g + i + 1)
                    for m in range(4):
                        sp.dma_start(rows[par][32 * i:32 * i + 32, m * CH:(m + 1) * CH],
                                     parts[i][32 * m:32 * m + 32, :]).then_inc(S(f"{name}_rows"), 16)

            def step(g, par, last):
                if last is False:
                    spread(g + 1, 1 - par, "dt", dt_part, dt_rows)
                    spread(g + 1, 1 - par, "dx", dx_part, dx_rows)

            spread(0, 0, "dt", dt_part, dt_rows)
            spread(0, 0, "dx", dx_part, dx_rows)
            schedule(step, sp.Fori)

        @block.tensor
        def _(pe):
            def bank(view, b):
                return view[:, b * BANK:(b + 1) * BANK]

            def spread_dt(g, par, k):
                if k >= 16:
                    g, par, k = g + 1, 1 - par, k - 16
                j, m = divmod(k, 4)
                if k == 0:
                    pe.wait_ge(S("dt_rows"), 16 * 12 * (g + 1))
                if not (isinstance(g, int) and g == 0 and k == 0):
                    pe.wait_ge(S("decay"), 16 * g + k)
                for b in range(2):
                    mm = pe.matmul(bank(ps_dt, b), core.rsel[:, 128 * j:128 * j + 128],
                                   dt_rows[par][0:96, m * CH + b * BANK:m * CH + (b + 1) * BANK], start=True, stop=True)
                mm.then_inc(S("dt_mm"), 1)

            def spread_dx(g, par, k):
                j, m = divmod(k, 4)
                if k == 0:
                    pe.wait_ge(S("dx_rows"), 16 * 12 * (g + 1))
                for b in range(2):
                    if not (isinstance(g, int) and g == 0 and k == 0):
                        pe.wait_ge(S("inject"), 32 * g + 2 * k - 1 + b)
                    pe.matmul(bank(ps_dx, b), core.rsel[:, 128 * j:128 * j + 128],
                              dx_rows[par][0:96, m * CH + b * BANK:m * CH + (b + 1) * BANK], start=True, stop=True)\
                      .then_inc(S("dx_mm"), 1)

            def project_in(name, at, g, b):
                mm = pe.matmul(bank(ps_p, b), p(d + "_win", at + 128 * b, 128), core.x[:, bass.ds(g * GC, GC)],
                               start=True, stop=True)
                if b == 1:
                    mm.then_inc(S(f"{name}_mm"), 1)

            def project_xi(name, i, g, par, b):
                mm = pe.matmul(bank(ps_p, b), p(d + "_wx", 128 * i, 128), bank(xi[par], b), start=True, stop=True)
                if b == 1:
                    mm.then_inc(S(f"{name}_mm"), 1)

            def sum_states(quad, j, b, g):
                if b == 0:
                    pe.wait_ge(S("ch"), 4 * quad + 4)
                for m in range(4):
                    mm = pe.matmul(bank(ps_y, b)[32 * m:32 * m + 32, :], p("ysel", 32 * j, 32),
                                   bank(states[j % 2][:, m * CH:(m + 1) * CH], b), start=False, stop=(j == 3))
                if b == 1:
                    mm.then_inc(S("y_mm"), 1)

            def skip(g, par, b):
                if b == 0:
                    wait_past(pe, "gated", g, g, 1)
                pe.matmul(bank(ps_y, b), p(d + "_skip"), bank(xi[par], b), start=True, stop=False)

            def project_out(g):
                pe.wait_ge(S("gated"), g + 1)
                for b in range(2):
                    mm = pe.matmul(ps_o[64 * b:64 * b + 64, :], p(d + "_wo"), bank(gate, b), start=True, stop=True)
                mm.then_inc(S("o_mm"), 1)

            def step(g, par, last):
                post, more = has_post(g), last is False
                n, q = 4 * g, 1 - par
                if last is None:
                    project_in("z", 256, g - 1, 1)
                    for b in range(2):
                        sum_states(n - 1, 3, b, g)
                    pe.wait_ge(S("z_act"), g)
                    project_out(g - 1)
                    return
                for k in range(16):
                    spread_dx(g, par, k)
                    if k == 0 and post:
                        project_in("z", 256, g - 1, 1)
                    if k in (2, 3) and more:
                        if k == 2:
                            if post:
                                pe.wait_ge(S("z_act"), g)
                            else:
                                pe.wait_ge(S("c_out"), 1)
                        project_in("xi", 0, g + 1, k - 2)
                    if k in (3, 4) and post:
                        sum_states(n - 1, 3, k - 3, g)
                    if k in (5, 6):
                        skip(g, par, k - 5)
                    if k in (6, 7) and more:
                        if k == 6:
                            pe.wait_ge(S("xi"), g + 2)
                        project_xi("dtp", 0, g + 1, q, k - 6)
                    if k in (7, 8):
                        sum_states(n, 0, k - 7, g)
                    if k == 9 and post:
                        if more:
                            pe.wait_ge(S("dt_relu"), g + 2)
                        else:
                            pe.wait_ge(S("z_act"), g)
                        project_out(g - 1)
                    if k in (10, 11) and more:
                        if k == 10:
                            if post:
                                pe.wait_ge(S("o_out"), g)
                            else:
                                pe.wait_ge(S("dt_relu"), g + 2)
                        project_xi("b", 1, g + 1, q, k - 10)
                    if k in (11, 12):
                        sum_states(n + 1, 1, k - 11, g)
                    if k in (13, 14) and more:
                        if k == 13:
                            pe.wait_ge(S("b_out"), g + 2)
                        project_xi("c", 2, g + 1, q, k - 13)
                    if k in (14, 15):
                        sum_states(n + 2, 2, k - 14, g)
                    if k == 15:
                        if more:
                            pe.wait_ge(S("c_out"), g + 2)
                        else:
                            pe.wait_ge(S("o_out"), g)
                        project_in("z", 256, g, 0)
                    if more or k + 2 < 16:
                        spread_dt(g, par, k + 2)

            for b in range(2):
                project_in("xi", 0, 0, b)
            for name, i, freed in (("dtp", 0, "xi"), ("b", 1, "dt_relu"), ("c", 2, "b_out")):
                pe.wait_ge(S(freed), 1)
                for b in range(2):
                    project_xi(name, i, 0, 0, b)
            spread_dt(0, 0, 0)
            spread_dt(0, 0, 1)
            schedule(step, pe.Fori)

        @block.scalar
        def _(act):
            def silu_in(name, bias, g):
                act.wait_ge(S(f"{name}_mm"), g + 1)
                act.activation(pre_act, ps_p, ACT.Identity, bias=bias, scale=0.5).then_inc(S(f"{name}_half"), 1)
                act.preload_act_table_set("exp_and_others")
                act.activation(sig, ps_p, ACT.Tanh, bias=bias, scale=0.5).then_inc(S(f"{name}_act"), 1)

            def gate_in(g, ahead):
                act.wait_ge(S("xi"), ahead + 1)
                act.wait_ge(S("dt"), ahead + 1)
                silu_in("z", half_bz, g)

            def softplus_in(g):
                act.wait_ge(S("dtp_mm"), g + 1)
                act.wait_ge(S("xi"), g + 1)
                act.activation(sig, ps_p, ACT.Abs, bias=b_dt).then_inc(S("dt_abs"), 1)
                wait_past(act, "dt_part", 3 * g, g, 1)
                wait_past(act, "dx_part", 3 * g, g, 1)
                act.activation(dt, ps_p, ACT.Relu, bias=b_dt).then_inc(S("dt_relu"), 1)

            def softplus_log(g):
                act.wait_ge(S("dt_abs"), g + 1)
                act.activation(sig, sig, ACT.Exp, scale=-1.0).then_inc(S("dt_exp"), 1)
                act.preload_act_table_set("natural_log_exp_and_others")
                act.wait_ge(S("dt_exp"), g + 1)
                act.activation(sig, sig, ACT.Ln, bias=1.0).then_inc(S("dt_ln"), 1)

            def high(name, src, parts, g):
                act.wait_ge(S(name), g + 1)
                wait_past(act, f"{name}_rows", 16 * 12 * g, g, 1)
                act.activation(parts[0], src, ACT.Copy).then_inc(S(f"{name}_part"), 1)

            def middle(name, parts, g):
                act.wait_ge(S(f"{name}_rest"), g + 1)
                act.activation(parts[1], rest, ACT.Copy).then_inc(S(f"{name}_part"), 1)

            def plain(name, out, bias, g):
                act.wait_ge(S(f"{name}_mm"), g + 1)
                wait_past(act, "ch", 16 * (g - 1), g, 2)
                act.activation(out, ps_p, ACT.Identity, bias=bias).then_inc(S(f"{name}_out"), 1)

            def output(g):
                act.wait_ge(S("o_mm"), g + 1)
                act.activation(core.x[:, bass.ds(g * GC, GC)], ps_o, ACT.Identity, bias=p(d + "_bo"))\
                   .then_inc(S("o_out"), 1)

            def step(g, par, last):
                if last is None:
                    gate_in(g - 1, g - 1)
                    output(g - 1)
                    return
                more, q = last is False, 1 - par
                for k in range(16):
                    n = 16 * g + k
                    m = k % 4
                    act.wait_ge(S("dt_mm"), n + 1)
                    if not (isinstance(n, int) and n < 4):
                        act.wait_ge(S("scan"), n - 3)
                    ring = by_seq(decay[:, m * CH:(m + 1) * CH])[:, :, 1:T]
                    scale = neg_a[:, 4 * m + k // 4:4 * m + k // 4 + 1]
                    act.activation(ring, by_seq(ps_dt)[:, :, 1:T], ACT.Exp, scale=scale).then_inc(S("decay"), 1)
                    if k == 1 and has_post(g):
                        gate_in(g - 1, g)
                    if k == 5 and more:
                        wait_past(act, "zs", g, g, 1)
                        silu_in("xi", half_bxi, g + 1)
                    if k == 8 and more:
                        softplus_in(g + 1)
                    if k == 9 and more:
                        softplus_log(g + 1)
                    if k == 10 and has_post(g):
                        output(g - 1)
                    if k == 10 and more:
                        high("dt", dt, dt_part, g + 1)
                    if k == 11 and more:
                        middle("dt", dt_part, g + 1)
                    if k == 12 and more:
                        plain("b", bm[q], p(d + "_bB"), g + 1)
                        high("dx", dx, dx_part, g + 1)
                    if k == 13 and more:
                        middle("dx", dx_part, g + 1)
                    if k == 15 and more:
                        plain("c", cm[q], p(d + "_bC"), g + 1)

            silu_in("xi", half_bxi, 0)
            softplus_in(0)
            softplus_log(0)
            plain("b", bm[0], p(d + "_bB"), 0)
            plain("c", cm[0], p(d + "_bC"), 0)
            for name, src, parts in (("dt", dt, dt_part), ("dx", dx, dx_part)):
                high(name, src, parts, 0)
                middle(name, parts, 0)
            schedule(step, act.Fori)

        @block.gpsimd
        def _(pool):
            def add_dt(g):
                pool.wait_ge(S("dt_ln"), g + 1)
                pool.wait_ge(S("dt_relu"), g + 1)
                pool.tensor_tensor(dt, dt, sig, ALU.add).then_inc(S("dt"), 1)

            def mul_dx(g, par):
                pool.wait_ge(S("dt"), g + 1)
                pool.wait_ge(S("xi"), g + 1)
                pool.tensor_tensor(dx, dt, xi[par], ALU.mult).then_inc(S("dx"), 1)

            def step(g, par, last):
                if last is None:
                    return
                for k in range(16):
                    j, m = divmod(k, 4)
                    pool.wait_ge(S("scan"), 16 * g + k + 1)
                    if k == 0:
                        pool.wait_ge(S("c_out"), g + 1)
                    part = states[j % 2][:, m * CH:(m + 1) * CH]
                    pool.tensor_tensor(part, part, cm[par], ALU.mult).then_inc(S("ch"), 1)
                    if last is False:
                        if k == 7:
                            add_dt(g + 1)
                        if k == 8:
                            mul_dx(g + 1, 1 - par)

            add_dt(0)
            mul_dx(0, 0)
            schedule(step, pool.Fori)

        @block.vector
        def _(dve):
            def silu(name, out, g):
                dve.wait_ge(S(f"{name}_half"), g + 1)
                dve.wait_ge(S(f"{name}_act"), g + 1)
                if name == "xi":
                    wait_past(dve, "gated", g - 1, g, 2)
                else:
                    wait_past(dve, "gated", g, g, 1)
                dve.scalar_tensor_tensor(out, sig, 1.0, pre_act, ALU.add, ALU.mult)\
                   .then_inc(S("xi" if name == "xi" else "zs"), 1)

            def split_rest(name, src, parts, g):
                dve.wait_ge(S(f"{name}_part"), 3 * g + 1)
                if name == "dx":
                    dve.wait_ge(S("dt_part"), 3 * g + 3)
                else:
                    wait_past(dve, "dx_part", 3 * g, g, 1)
                dve.tensor_tensor(rest, src, parts[0], ALU.subtract).then_inc(S(f"{name}_rest"), 1)

            def split_low(name, parts, g):
                dve.wait_ge(S(f"{name}_part"), 3 * g + 2)
                dve.tensor_tensor(parts[2], rest, parts[1], ALU.subtract).then_inc(S(f"{name}_part"), 1)

            def gated(g):
                dve.wait_ge(S("y_mm"), 4 * g + 4)
                dve.wait_ge(S("zs"), g + 1)
                wait_past(dve, "o_mm", g, g, 1)
                dve.tensor_tensor(gate, ps_y, zs, ALU.mult).then_inc(S("gated"), 1)

            def step(g, par, last):
                if last is None:
                    silu("z", zs, g - 1)
                    gated(g - 1)
                    return
                for k in range(16):
                    j, m = divmod(k, 4)
                    n = 16 * g + k
                    part = states[j % 2][:, m * CH:(m + 1) * CH]
                    if k == 0:
                        dve.wait_ge(S("b_out"), g + 1)
                    if m == 0 and not (isinstance(g, int) and 4 * g + j < 2):
                        dve.wait_ge(S("y_mm"), 4 * g + j - 1)
                    for b in range(2):
                        half = slice(b * BANK, (b + 1) * BANK)
                        dve.wait_ge(S("dx_mm"), 2 * n + 1 + b)
                        dve.tensor_tensor(part[:, half], ps_dx[:, half], bm[par][:, half], ALU.mult)\
                           .then_inc(S("inject"), 1)
                    dve.wait_ge(S("decay"), n + 1)
                    dve.wait_ge(S("inject"), 2 * n + 2)
                    dve.tensor_tensor_scan(part, decay[:, m * CH:(m + 1) * CH], part, 0.0, ALU.mult, ALU.add)\
                       .then_inc(S("scan"), 1)
                    if k == 4 and has_post(g):
                        gated(g - 1)
                    if k == 2 and has_post(g):
                        silu("z", zs, g - 1)
                    if last is False:
                        if k == 5:
                            silu("xi", xi[1 - par], g + 1)
                        if k == 10:
                            split_rest("dt", dt, dt_part, g + 1)
                        if k == 11:
                            split_low("dt", dt_part, g + 1)
                        if k == 12:
                            split_rest("dx", dx, dx_part, g + 1)
                        if k == 13:
                            split_low("dx", dx_part, g + 1)

            dve.memset(by_seq(decay)[:, :, 0:1], 0.0).then_inc(S("starts"), 1)
            silu("xi", xi[0], 0)
            for name, src, parts in (("dt", dt, dt_part), ("dx", dx, dx_part)):
                split_rest(name, src, parts, 0)
                split_low(name, parts, 0)
            schedule(step, dve.Fori)


def route(core, ffn):
    nc, p, S = core.nc, core.p, core.sem
    x, tiles = core.x[:, :], COLS // 128
    wide = tiles * HALVES
    high, low = core.take(COLS // 2, F16), core.take(COLS // 2, F16)
    logits, first, second, key = (core.take(wide * EXPERTS) for _ in range(4))
    top, pick, second_top, ratio, weight = (core.take(wide) for _ in range(5))
    parts = core.take(wide * EXPERTS, F16)
    w_raw = core.take(2 * EXPERTS * HID)

    def write(act, c, chunk):
        return act.activation(x[:, c * CH:(c + 1) * CH], chunk, ACT.Copy)

    normalize(core, "hn", core.h[:, :], write)

    def rows(view):
        return view.rearrange("p (w e) -> p w e", e=EXPERTS)

    def spread(view):
        return view.unsqueeze(2).to_broadcast([128, wide, EXPERTS])

    def const(view):
        return view.unsqueeze(1).to_broadcast([128, wide, EXPERTS])

    part_view = parts.rearrange("p (t k u) -> p k t u", k=2, u=HALVES * EXPERTS)

    turned = [core.bank(4 + b).bitcast(F16)[0:64, :] for b in range(4)]

    with nc.Block() as block:
        @block.sync
        def _(sp):
            sp.dma_start(w_raw, ffn["wmoe"]).then_inc(S("wmoe_in"), 16)
            sp.dma_start(ffn["sel"], ffn["ffn16"]).then_inc(S("ffn16_in"), 16)
            sp.dma_start(ffn["w3"], ffn["w3_in"]).then_inc(S("w3_in"), 16)
            for i, part in enumerate((high, low)):
                sp.wait_ge(S("x_part"), i + 1)
                for q in range(HALVES):
                    dst = ffn["x"][64 * i:64 * i + 64, :].rearrange("p (g q t) -> p g q t", g=GROUPS, q=HALVES)
                    sp.dma_start(dst[:, :, q, :], part[64 * q:64 * q + 64, :].rearrange("p (g t) -> p g t", g=GROUPS))\
                      .then_inc(S("x_stacked"), 16)
            sp.wait_ge(S("x_stacked"), 64)
            sp.wait_ge(S("w3_in"), 16)

        @block.scalar
        def _(act):
            act.activation(high, x, ACT.Copy).then_inc(S("x_part"), 1)
            act.wait_ge(S("wmoe_in"), 16)
            act.activation(ffn["wh"], w_raw, ACT.Copy).then_inc(S("w_high"), 1)
            act.wait_ge(S("gap"), 1)
            act.activation(ratio, ratio, ACT.Exp).then_inc(S("ratio"), 1)
            for b in range(4):
                act.wait_ge(S("turned"), b + 1)
                act.activation(ffn["disp"][0:64, b * CH:(b + 1) * CH], turned[b], ACT.Copy).then_inc(S("disp_out"), 1)

        @block.tensor
        def _(pe):
            for t in range(tiles):
                mm = pe.matmul(core.bank(0, 2)[:, t * 32:(t + 1) * 32], x[:, t * 128:(t + 1) * 128], p("gate"),
                               start=True, stop=True)
            mm.then_inc(S("logits_mm"), 1)
            pe.wait_ge(S("parts"), 2)
            pe.wait_ge(S("ffn16_in"), 16)
            for t in range(tiles):
                mm = pe.transpose(turned[t // 8][:, (t % 8) * 128:(t % 8 + 1) * 128], parts[:, t * 64:(t + 1) * 64],
                                  ffn["ident"])
                if t % 8 == 7:
                    mm.then_inc(S("turned"), 1)

        @block.gpsimd
        def _(pool):
            pool.memset(ffn["disp"][64:128, :], 0.0).then_inc(S("disp_zero"), 1)

        @block.vector
        def _(dve):
            done = [0]

            def after():
                dve.wait_ge(S("route"), done[0])

            def mark(instruction):
                done[0] += 1
                instruction.then_inc(S("route"), 1)

            dve.wait_ge(S("x_part"), 1)
            dve.tensor_tensor(low, x, high, ALU.subtract).then_inc(S("x_part"), 1)
            dve.wait_ge(S("w_high"), 1)
            mark(dve.tensor_tensor(ffn["wl"], w_raw, ffn["wh"], ALU.subtract))
            dve.wait_ge(S("logits_mm"), 1)
            mark(dve.tensor_tensor(rows(logits), rows(core.bank(0, 2)), const(p("gate_b")), ALU.add))

            def pick_top(best, hot):
                after()
                mark(dve.tensor_reduce(best, rows(logits), AX.X, ALU.max))
                after()
                mark(dve.tensor_tensor(rows(key), rows(logits), spread(best), ALU.is_equal))
                after()
                mark(dve.tensor_tensor(rows(key), rows(key), const(p("rank")), ALU.mult))
                after()
                mark(dve.tensor_reduce(pick, rows(key), AX.X, ALU.max))
                after()
                mark(dve.tensor_tensor(rows(hot), rows(key), spread(pick), ALU.is_equal))

            pick_top(top, first)
            after()
            mark(dve.scalar_tensor_tensor(logits, first, -3e38, logits, ALU.mult, ALU.add))
            pick_top(second_top, second)
            after()
            dve.tensor_tensor(ratio, second_top, top, ALU.subtract).then_inc(S("gap"), 1)
            dve.wait_ge(S("ratio"), 1)
            mark(dve.tensor_scalar(weight, ratio, 1.0, None, ALU.add))
            after()
            mark(dve.reciprocal(weight, weight))
            after()
            mark(dve.tensor_tensor(ratio, ratio, weight, ALU.mult))
            mark(dve.tensor_tensor(rows(first), rows(first), spread(weight), ALU.mult))
            after()
            mark(dve.tensor_tensor(rows(second), rows(second), spread(ratio), ALU.mult))
            after()
            mark(dve.tensor_tensor(first, first, second, ALU.add))
            after()
            flat = first.rearrange("p (t u) -> p t u", u=HALVES * EXPERTS)
            dve.tensor_copy(part_view[:, 0], flat).then_inc(S("parts"), 1)
            dve.wait_ge(S("parts"), 1)
            dve.tensor_tensor(part_view[:, 1], flat, part_view[:, 0], ALU.subtract).then_inc(S("parts"), 1)


def experts(core, ffn, out):
    nc, S = core.nc, core.sem
    act_h = [core.take(CH) for _ in range(2)]
    hidden = [core.take(CH) for _ in range(2)]
    ps_1, ps_2, ps_d, ps_y = core.bank(0, 2), core.bank(2, 2), core.bank(4, 2), core.bank(6)

    def schedule(emit, loop):
        emit(0)
        with loop(1, GROUPS) as g:
            emit(g)

    def first_of_all(g, e, n=1):
        return isinstance(g, int) and e < n

    with nc.Block() as block:
        @block.tensor
        def _(pe):
            def tokens(g, q):
                return ffn["x"][:, bass.ds(g * GT + q * GC, GC)]

            def hidden_in(g, e, which, out_banks):
                for q in range(HALVES):
                    bank = out_banks[:, q * BANK:(q + 1) * BANK]
                    cols = slice((which * EXPERTS + e) * HID, (which * EXPERTS + e + 1) * HID)
                    pe.matmul(bank, ffn["wh"][:, cols], tokens(g, q), start=True, stop=False)
                    mm = pe.matmul(bank, ffn["wl"][:, cols], tokens(g, q), start=False, stop=True)
                return mm

            def expert_out(n, e):
                pe.wait_ge(S("hidden"), n + 1)
                for q in range(HALVES):
                    mm = pe.matmul(ps_y[64 * q:64 * q + 64, :], ffn["w3"][:, 64 * e:64 * e + 64],
                                   hidden[e % 2][:, q * BANK:(q + 1) * BANK], start=(e == 0), stop=(e == EXPERTS - 1))
                mm.then_inc(S("y_mm"), 1)

            def group(g):
                for e in range(EXPERTS):
                    n = EXPERTS * g + e
                    if not first_of_all(g, e):
                        pe.wait_ge(S("h1_act"), n)
                    hidden_in(g, e, 0, ps_1).then_inc(S("h1_mm"), 1)
                    if not first_of_all(g, e):
                        pe.wait_ge(S("h12"), n)
                    hidden_in(g, e, 1, ps_2).then_inc(S("h2_mm"), 1)
                    if not first_of_all(g, e):
                        pe.wait_ge(S("hidden"), n)
                    for q in range(HALVES):
                        at = (2 * e + q) * 128
                        mm = pe.matmul(ps_d[:, q * BANK:(q + 1) * BANK], ffn["dsel"][:, at:at + 128],
                                       ffn["disp"][:, bass.ds(g * GC, GC)], start=True, stop=True)
                    mm.then_inc(S("disp_mm"), 1)
                    if e > 0:
                        if e == 1 and not first_of_all(g, e, 2):
                            pe.wait_ge(S("y_added"), g)
                        expert_out(n - 1, e - 1)
                    elif not first_of_all(g, e):
                        expert_out(n - 1, EXPERTS - 1)

            schedule(group, pe.Fori)
            expert_out(EXPERTS * GROUPS - 1, EXPERTS - 1)

        @block.scalar
        def _(act):
            def group(g):
                for e in range(EXPERTS):
                    n = EXPERTS * g + e
                    act.wait_ge(S("h1_mm"), n + 1)
                    if not first_of_all(g, e, 2):
                        act.wait_ge(S("h12"), n - 1)
                    act.activation(act_h[e % 2], ps_1, ACT.Silu).then_inc(S("h1_act"), 1)

            act.preload_act_table_set("silu_and_others")
            schedule(group, act.Fori)

        @block.vector
        def _(dve):
            def add_out(g):
                dve.wait_ge(S("y_mm"), EXPERTS * g + EXPERTS)
                cols = core.h[:, bass.ds(g * GC, GC)]
                dve.tensor_tensor(cols, ps_y, cols, ALU.add).then_inc(S("y_added"), 1)

            def group(g):
                for e in range(EXPERTS):
                    n = EXPERTS * g + e
                    dve.wait_ge(S("h2_mm"), n + 1)
                    dve.wait_ge(S("h1_act"), n + 1)
                    if not first_of_all(g, e, 2):
                        dve.wait_ge(S("y_mm"), n - 1)
                    dve.tensor_tensor(hidden[e % 2], ps_2, act_h[e % 2], ALU.mult).then_inc(S("h12"), 1)
                    dve.wait_ge(S("disp_mm"), n + 1)
                    dve.wait_ge(S("h12"), n + 1)
                    dve.tensor_tensor(hidden[e % 2], ps_d, hidden[e % 2], ALU.mult).then_inc(S("hidden"), 1)
                    if e == 1 and not isinstance(g, int):
                        pass
                    if e == 0 and not isinstance(g, int):
                        add_out(g - 1)

            schedule(group, dve.Fori)
            add_out(GROUPS - 1)

        @block.sync
        def _(sp):
            with sp.Fori(0, GROUPS) as g:
                sp.wait_ge(S("y_added"), g + 1)
                cols = bass.ds(g * GC, GC)
                sp.dma_start(out[:, cols], core.h[:, cols]).then_inc(S("out"), 16)
            sp.wait_ge(S("out"), 16 * GROUPS)


def feed_forward(core, ffn16, wmoe, w3, out):
    sel = core.take((2 * EXPERTS + 1) * 128 // 2, F16)
    weights = EXPERTS * HID
    ffn = {"ffn16": ffn16, "wmoe": wmoe, "w3_in": w3, "sel": sel, "dsel": sel[:, 0:2 * EXPERTS * 128],
           "ident": sel[:, 2 * EXPERTS * 128:], "wh": core.take(weights, F16), "wl": core.take(weights, F16),
           "w3": core.take(EXPERTS * C), "x": core.take(GROUPS * GT // 2, F16), "disp": core.take(COLS // 2, F16)}
    kept = core.used
    route(core, ffn)
    core.used = kept
    experts(core, ffn, out)


def program(nc, xin, params, bsel, rsel, ffn16, wmoe, w3, out):
    core = Core(nc)
    with core.stage():
        setup(core, params, bsel, rsel)
    with core.stage():
        attention(core, xin)
    with core.stage():
        mix_input(core)
    with core.stage():
        mixer(core, "f")
    with core.stage():
        between_directions(core)
    with core.stage():
        mixer(core, "b")
    with core.stage():
        add_backward(core)
        feed_forward(core, ffn16, wmoe, w3, out)


def kernel(**inputs):
    import numpy as np
    import concourse.bacc as bacc
    from concourse.bass_utils import run_bass_kernel_spmd

    I = {k: np.asarray(v) for k, v in inputs.items()}
    f32 = np.float32

    def col(v):
        return np.asarray(v, f32).reshape(-1, 1)

    def both(v):
        return np.concatenate([col(v), col(v)])

    def diag(w):
        z = np.zeros_like(w)
        return np.concatenate([np.concatenate([w, z], 1), np.concatenate([z, w], 1)], 0)

    i = np.arange(128)
    same_half = (i[:, None] // 64 == i[None] // 64)
    mean = (same_half / 64).astype(f32)
    center = (np.eye(128) - same_half / 64).astype(f32)
    r = np.arange(32)
    sum_c = ((i[:, None] // 64 == (r[None] % 16) // 8) / 64).astype(f32)
    sum_d = (i[:, None] // 8 == r[None] % 16).astype(f32)
    ysel = np.concatenate([(8 * j + i[:, None] // 16 == r[None]) for j in range(4)], 1).astype(f32)
    dup = -((i % 32) // 16).astype(f32).reshape(-1, 1)
    bsel = np.concatenate([(i[:, None] // 32 == g) & (i[:, None] % 16 == i[None] // 8) for g in range(4)], 1)
    r96 = np.arange(96)
    rsel = np.concatenate([r96[:, None] % 32 == 8 * j + i[None] // 16 for j in range(4)], 1)
    r128 = np.arange(128)
    dsel = np.concatenate([np.tile(((r128[:, None] < 64) & (r128[:, None] % 32 == 16 * q + e)), (1, 128))
                           for e in range(EXPERTS) for q in range(2)], 1)
    ident = np.eye(128)

    def ph(w):
        return w.reshape((HEADS, SP) + w.shape[1:]).swapaxes(0, 1).reshape((DI,) + w.shape[1:])

    kv = I["L0_tok_Wkv"]
    pieces = {"mean": mean, "sum_c": sum_c, "sum_d": sum_d, "center": center, "ysel": ysel, "dup": dup,
              "wq": diag(I["L0_tok_Wq"].T), "wk": diag(kv[:64].T), "wv": diag(kv[64:].T),
              "proj": diag(I["L0_tok_proj_w"].T), "lnq_w": both(I["L0_tok_ln_q_w"]),
              "lnq_b": both(I["L0_tok_ln_q_b"]), "lnkv_w": both(I["L0_tok_ln_kv_w"]),
              "lnkv_b": both(I["L0_tok_ln_kv_b"]), "proj_b": both(I["L0_tok_proj_b"])}
    for d in "fb":
        a = {k[len("L0_attn_f_"):]: v for k, v in I.items() if k.startswith(f"L0_attn_{d}_")}
        xi_w, z_w = ph(a["in_proj_w"][:DI]).T, ph(a["in_proj_w"][DI:]).T
        zero = np.zeros_like(xi_w)
        top, bottom = (lambda w: np.concatenate([w, zero])), (lambda w: np.concatenate([zero, w]))
        xp, xb = a["x_proj_w"], a["x_proj_b"]
        rows = np.concatenate([ph(xp[:DI]), xp[DI:]])
        pieces |= {d + "_win": np.concatenate([top(xi_w), bottom(xi_w), top(z_w), bottom(z_w)], 1),
                   d + "_wx": ph(rows.T), d + "_wo": ph(a["out_proj_w"].T),
                   d + "_alog": a["A_log"].reshape(HEADS, SP, SN).swapaxes(1, 2).reshape(HEADS * SN, SP),
                   d + "_bxi": col(ph(a["in_proj_b"][:DI])), d + "_bz": col(ph(a["in_proj_b"][DI:])),
                   d + "_bdt": col(ph(xb[:DI])), d + "_dtb": col(ph(a["dt_bias"])),
                   d + "_bB": col(xb[DI:2 * DI]), d + "_bC": col(xb[2 * DI:]), d + "_skip": np.diag(ph(a["D_skip"])),
                   d + "_bo": both(a["out_proj_b"])}
    conv = I["L0_attn_conv_w"].reshape(C, 3)
    pieces |= {"norm_w": both(I["L0_attn_norm_w"]), "norm_b": both(I["L0_attn_norm_b"]),
               "conv_w": np.concatenate([conv, conv]), "conv_b": both(I["L0_attn_conv_b"]),
               "gate": diag(I["L0_ffn_gate_w"]), "gate_b": np.tile(I["L0_ffn_gate_b"].reshape(1, -1), (128, 1)),
               "rank": np.tile(np.arange(EXPERTS, 0, -1).astype(f32).reshape(1, -1), (128, 1))}
    params = np.concatenate([pieces[name] for name, _ in PARTS], 1).astype(f32)

    x = I["x"].reshape(GROUPS, HALVES, 2, C, T // 16, STRIDE, 16, STRIDE)
    x = x.transpose(0, 2, 1, 3, 5, 7, 4, 6).reshape(STEPS, 128, PIX)
    moe = [np.concatenate([w, w]) for w in (I["L0_ffn_w1"].transpose(1, 0, 2).reshape(C, -1),
                                            I["L0_ffn_w2"].transpose(1, 0, 2).reshape(C, -1))]
    arrays = {"xin": np.ascontiguousarray(x), "params": params,
              "bsel": bsel.astype(np.float16), "rsel": rsel.astype(mybir.dt.np(BF16)),
              "ffn16": np.concatenate([dsel, ident], 1).astype(np.float16),
              "wmoe": np.concatenate(moe, 1),
              "w3": np.ascontiguousarray(I["L0_ffn_w3"].transpose(1, 0, 2).reshape(HID, -1))}

    nc = bacc.Bacc("TRN2", target_bir_lowering=False, num_devices=1)
    aps = [nc.dram_tensor("in_" + k, v.shape, mybir.dt.from_np(v.dtype), kind="ExternalInput").ap() for k, v in arrays.items()]
    out = nc.dram_tensor("out", (128, COLS), F32, kind="ExternalOutput").ap()
    program(nc, *aps, out)
    got = run_bass_kernel_spmd(nc, [{"in_" + k: v for k, v in arrays.items()}], core_ids=[0]).results[0]["out"]
    return got.reshape(HALVES, C, GROUPS, 2, T).transpose(2, 0, 3, 4, 1).reshape(BATCH, T, C)
```

```python
from contextlib import contextmanager

import concourse.bass as bass
from concourse import mybir

F32 = mybir.dt.float32
F16 = mybir.dt.float16
BF16 = mybir.dt.bfloat16
ALU = mybir.AluOpType
ACT = mybir.ActivationFunctionType
AX = mybir.AxisListType

BATCH, C, SIDE, STRIDE, HEADS = 32, 64, 64, 4, 8
D = C // HEADS
T = (SIDE // STRIDE) ** 2
N = STRIDE * STRIDE
PIX = N * T
HALVES = 2
STEPS = BATCH // HALVES
GROUPS = STEPS // 2
COLS = STEPS * T
GC = COLS // GROUPS
GT = HALVES * GC
DI, SN = 128, 16
SP = DI // HEADS
EXPERTS, HID = 16, 128
EPS = 1e-5
BANK = 512
CH = 2 * BANK
KCH = PIX // CH
TQ = T // 4

PARTS = [("mean", 128), ("sum_c", 32), ("sum_d", 32), ("center", 128), ("ysel", 128), ("dup", 1),
         ("wq", 128), ("wk", 128), ("wv", 128), ("proj", 128),
         ("lnq_w", 1), ("lnq_b", 1), ("lnkv_w", 1), ("lnkv_b", 1), ("proj_b", 1)]
for _d in "fb":
    PARTS += [(_d + "_win", 512), (_d + "_wx", 384), (_d + "_wo", 64), (_d + "_alog", 16), (_d + "_bxi", 1),
              (_d + "_bz", 1), (_d + "_bdt", 1), (_d + "_dtb", 1), (_d + "_bB", 1), (_d + "_bC", 1),
              (_d + "_skip", 128), (_d + "_bo", 1)]
PARTS += [("norm_w", 1), ("norm_b", 1), ("conv_w", 3), ("conv_b", 1), ("gate", 32), ("gate_b", 16), ("rank", 16)]
AT, _n = {}, 0
for _name, _w in PARTS:
    AT[_name] = (_n, _w)
    _n += _w
PACKED = _n


class Core:

    def __init__(self, nc):
        self.nc = nc
        self.sems = {}
        self.pack = nc.alloc_sbuf_tensor("pack", [128, PACKED], F32)
        self.bsel = nc.alloc_sbuf_tensor("bsel", [128, 4 * 128], F16)
        self.rsel = nc.alloc_sbuf_tensor("rsel", [96, 4 * 128], BF16)
        self.wq = nc.alloc_sbuf_tensor("wq_folded", [128, 128], F32)
        self.wk = nc.alloc_sbuf_tensor("wk_folded", [128, 128], F32)
        self.wv = nc.alloc_sbuf_tensor("wv_folded", [128, 128], F32)
        self.cols = nc.alloc_sbuf_tensor("cols", [128, 16], F32)
        self.neg_a = nc.alloc_sbuf_tensor("neg_a", [128, 2 * SP], F32)
        self.h = nc.alloc_sbuf_tensor("h", [128, COLS], F32)
        self.x = nc.alloc_sbuf_tensor("x_norm", [128, COLS], F32)
        self.arena_words = 38900
        self.arena = nc.alloc_sbuf_tensor("arena", [128, self.arena_words], F32)
        self.psum = nc.alloc_psum_tensor("psum", [128, 8 * BANK], F32)
        self.used = 0

    def p(self, name, i=0, w=None):
        at, width = AT[name]
        return self.pack[:, at + i:at + i + (width if w is None else w)]

    def sem(self, name):
        if name not in self.sems:
            self.sems[name] = self.nc.alloc_semaphore(name)
        return self.sems[name]

    @contextmanager
    def stage(self):
        self.used, self.sems = 0, {}
        yield
        self.nc.all_engine_barrier()
        self.nc.clear_and_free_semaphores(list(self.sems.values()))
        self.nc.all_engine_barrier()

    def take(self, words, dtype=F32):
        at, self.used = self.used, self.used + words
        assert self.used <= self.arena_words, self.used
        view = self.arena[:, at:at + words]
        return view if dtype == F32 else view.bitcast(dtype)

    def bank(self, b, n=1):
        return self.psum[:, b * BANK:(b + n) * BANK]


def load_pixels(sp, core, xin, xt, s, par, freed=None):
    for c in range(KCH):
        if freed:
            freed(c)
        chunk = slice(c * CH, (c + 1) * CH)
        sp.dma_start(xt[par][:, chunk], xin[s][:, chunk]).then_inc(core.sem(f"x_in{par}"), 16)


def setup(core, params, bsel, rsel, xin, xt):
    nc, p, S = core.nc, core.p, core.sem
    t = core.take(512)
    with nc.Block() as block:
        @block.sync
        def _(sp):
            sp.dma_start(core.pack[:, :], params).then_inc(S("params_in"), 16)
            sp.dma_start(core.bsel[:, :], bsel).then_inc(S("params_in"), 16)
            sp.dma_start(core.rsel[:, :], rsel).then_inc(S("params_in"), 16)
            load_pixels(sp, core, xin, xt, 0, 0)
            sp.wait_ge(S("params_in"), 48)

        @block.vector
        def _(dve):
            dve.wait_ge(S("params_in"), 48)
            dve.tensor_scalar(t[:, 0:128], p("wq"), p("lnq_w"), None, ALU.mult)
            dve.tensor_scalar(t[:, 128:256], p("wk"), p("lnkv_w"), None, ALU.mult)
            dve.tensor_scalar(t[:, 256:384], p("wv"), p("lnkv_w"), None, ALU.mult).then_inc(S("fold_scaled"), 1)
            for i, d in enumerate("fb"):
                dve.tensor_tensor(core.cols[:, 3 + i:4 + i], p(d + "_bdt"), p(d + "_dtb"), ALU.add)
            dve.wait_ge(S("fold_mm"), 1)
            dve.tensor_scalar(core.wq[:, :], core.bank(0)[:, 0:128], C ** -0.5 / N, None, ALU.mult)
            dve.tensor_copy(core.wk[:, :], core.bank(0)[:, 128:256])
            dve.tensor_copy(core.wv[:, :], core.bank(0)[:, 256:384])
            dve.tensor_scalar(core.cols[:, 0:1], core.bank(1)[:, 0:1], C ** -0.5, None, ALU.mult)
            dve.tensor_copy(core.cols[:, 1:2], core.bank(1)[:, 1:2]).then_inc(S("bias_v"), 1)
            dve.wait_ge(S("bias_o_mm"), 1)
            dve.tensor_tensor(core.cols[:, 2:3], core.bank(2)[:, 0:1], p("proj_b"), ALU.add)
            dve.wait_ge(S("a_exp"), 1)
            dve.tensor_scalar(core.neg_a[:, :], core.neg_a[:, :], -1.0, None, ALU.mult)

        @block.tensor
        def _(pe):
            pe.wait_ge(S("fold_scaled"), 1)
            for i in range(3):
                pe.matmul(core.bank(0)[:, 128 * i:128 * (i + 1)], p("center"), t[:, 128 * i:128 * (i + 1)],
                          start=True, stop=True)
            pe.matmul(core.bank(1)[:, 0:1], p("wq"), p("lnq_b"), start=True, stop=True)
            pe.matmul(core.bank(1)[:, 1:2], p("wv"), p("lnkv_b"), start=True, stop=True).then_inc(S("fold_mm"), 1)
            pe.wait_ge(S("bias_v"), 1)
            pe.matmul(core.bank(2)[:, 0:1], p("proj"), core.cols[:, 1:2], start=True, stop=True)\
              .then_inc(S("bias_o_mm"), 1)

        @block.scalar
        def _(act):
            act.preload_act_table_set("natural_log_exp_and_others")
            act.wait_ge(S("params_in"), 48)
            act.activation(core.neg_a[:, 0:SP], p("f_alog"), ACT.Exp)
            act.activation(core.neg_a[:, SP:2 * SP], p("b_alog"), ACT.Exp).then_inc(S("a_exp"), 1)


def attention(core, xin, xt):
    nc, p, S = core.nc, core.p, core.sem
    xsq = core.take(PIX)
    kq = core.take(PIX)
    v = [core.take(PIX) for _ in range(2)]
    mean_t = core.take(8 * T)
    rf, rf_sq, q_musq, q_rstd, q, av_sum = (core.take(T) for _ in range(6))
    musq = core.take(CH)
    rstd = [core.take(CH) for _ in range(2)]
    prob = core.take(CH)
    gain = core.take(CH)
    hi = core.take(CH // 2, F16)
    prob16 = core.take(CH // 2, F16)
    top, den, rden = (core.take(TQ) for _ in range(3))
    slot = [core.bank(0, 2), core.bank(2, 2)]
    rows = core.bank(4, 2)
    small = core.bank(6)
    qb = core.bank(7)
    q_bias, o_bias = core.cols[:, 0:1], core.cols[:, 2:3]

    def bcast_n(view, n):
        return view.unsqueeze(1).to_broadcast([128, n, view.shape[-1]])

    def by_n(view):
        return view.rearrange("p (n t) -> p n t", n=N)

    def schedule(emit, loop):
        emit(0, 0, front=True, back=False, pre=True)
        emit(1, 1, front=True, back=True, pre=True)
        with loop(1, STEPS // 2 - 1) as k:
            emit(2 * k, 0, front=True, back=True, pre=True)
            emit(2 * k + 1, 1, front=True, back=True, pre=True)
        emit(STEPS - 2, 0, front=True, back=True, pre=True)
        emit(STEPS - 1, 1, front=True, back=True, pre=False)
        emit(STEPS, 0, front=False, back=True, pre=False)
        emit(STEPS + 1, 1, front=False, back=False, pre=False)

    def later(s, n):
        return not isinstance(s, int) or s >= n

    def x_loaded(s, par):
        return 16 * KCH // 2 * (s - par) + 16 * KCH

    with nc.Block() as block:
        @block.sync
        def _(sp):
            def load(s, par):
                load_pixels(sp, core, xin, xt, s, par, lambda c: sp.wait_ge(S("v_mm"), KCH * (s - 2) + c + 1))

            load_pixels(sp, core, xin, xt, 1, 1)
            with sp.Fori(1, STEPS // 2) as k:
                load(2 * k, 0)
                load(2 * k + 1, 1)

        @block.gpsimd
        def _(pool):
            def pre(s, par):
                pool.wait_ge(S(f"x_in{par}"), x_loaded(s, par))
                if later(s, 1):
                    pool.wait_ge(S("rf_sum"), s)
                x = xt[par]
                pool.tensor_tensor(mean_t, x[:, 0:8 * T], x[:, 8 * T:16 * T], ALU.add).then_inc(S("mean_part"), 1)
                for i, n in enumerate((4, 2)):
                    pool.wait_ge(S("mean_part"), 3 * s + i + 1)
                    pool.tensor_tensor(mean_t[:, 0:n * T], mean_t[:, 0:n * T], mean_t[:, n * T:2 * n * T], ALU.add)\
                        .then_inc(S("mean_part"), 1)
                pool.wait_ge(S("mean_part"), 3 * s + 3)
                if later(s, 1):
                    pool.wait_ge(S("q_mm"), s)
                    pool.wait_ge(S("h_base"), s)
                pool.tensor_tensor(rf, mean_t[:, 0:T], mean_t[:, T:2 * T], ALU.add).then_inc(S("rf_sum"), 1)

            def step(s, par, front, back, pre):
                if pre:
                    pre_(s + 1, 1 - par)
                if front:
                    pool.wait_ge(S("s_max"), s + 1)
                    pool.tensor_tensor(by_n(prob), by_n(prob), bcast_n(top, N), ALU.subtract)\
                        .then_inc(S("s_centred"), 1)
                    pool.wait_ge(S("inv_den"), s + 1)
                    pool.tensor_tensor(by_n(gain), by_n(rstd[par]), bcast_n(rden, N), ALU.mult)\
                        .then_inc(S("gain"), 1)
                    pool.wait_ge(S("gain"), s + 1)
                    pool.tensor_tensor(prob, prob, gain, ALU.mult).then_inc(S("prob"), 1)

            pre_ = pre
            pre_(0, 0)
            schedule(step, pool.Fori)

        @block.scalar
        def _(act):
            def pre_x(s, par):
                act.wait_ge(S(f"x_in{par}"), x_loaded(s, par))
                if later(s, 1):
                    act.wait_ge(S("sum_x2"), s)
                act.activation(xsq, xt[par], ACT.Square).then_inc(S("x_sq"), 1)

            def pre_rf(s):
                act.wait_ge(S("rf_sum"), s + 1)
                act.activation(rf_sq, rf, ACT.Square, scale=1.0 / N).then_inc(S("rf_sq"), 1)
                act.activation(core.h[:, bass.ds(s * T, T)], rf, ACT.Identity, bias=o_bias, scale=1.0 / N)\
                   .then_inc(S("h_base"), 1)

            def pre_q_square(s):
                act.wait_ge(S("q_stats"), s + 1)
                act.activation(q_musq, small[:, 0:T], ACT.Square, scale=1.0 / N).then_inc(S("q_musq"), 1)

            def pre_q_rstd(s):
                act.wait_ge(S("q_var"), s + 1)
                act.activation(q_rstd, q_rstd, ACT.Ln, bias=EPS).then_inc(S("q_ln"), 1)
                act.wait_ge(S("q_ln"), s + 1)
                act.activation(q_rstd, q_rstd, ACT.Exp, scale=-0.5).then_inc(S("q_rstd"), 1)

            def pre_x_square(s):
                act.wait_ge(S("sum_x"), s + 1)
                if later(s, 1):
                    act.wait_ge(S("x_var"), s)
                act.activation(musq, rows, ACT.Square).then_inc(S("x_musq"), 1)

            def pre_x_rstd(s, par):
                act.wait_ge(S("x_var"), s + 1)
                act.activation(rstd[par], rstd[par], ACT.Ln, bias=EPS).then_inc(S("x_ln"), 1)
                act.wait_ge(S("x_ln"), s + 1)
                act.activation(rstd[par], rstd[par], ACT.Exp, scale=-0.5).then_inc(S("x_rstd"), 1)

            def v_out(s, par, c):
                act.wait_ge(S("v_mm"), KCH * s + c + 1)
                if c == 0 and later(s, 2):
                    act.wait_ge(S("av_sum"), s - 1)
                act.activation(v[par][:, c * CH:(c + 1) * CH], slot[0], ACT.Copy).then_inc(S("v_out"), 1)

            def step(s, par, front, back, pre):
                if pre:
                    pre_x(s + 1, 1 - par)
                if front:
                    v_out(s, par, 0)
                if pre:
                    pre_rf(s + 1)
                if front:
                    v_out(s, par, 1)
                if front:
                    v_out(s, par, 2)
                    act.wait_ge(S("s_centred"), s + 1)
                    act.activation(prob, prob, ACT.Exp).then_inc(S("s_exp"), 1)
                if pre:
                    pre_q_square(s + 1)
                    pre_q_rstd(s + 1)
                if pre:
                    pre_x_square(s + 1)
                if front:
                    v_out(s, par, 3)
                if pre:
                    pre_x_rstd(s + 1, 1 - par)
                if front:
                    act.wait_ge(S("prob"), s + 1)
                    act.activation(hi, prob, ACT.Copy).then_inc(S("prob_hi"), 1)

            act.preload_act_table_set("natural_log_exp_and_others")
            pre_x(0, 0)
            pre_rf(0)
            pre_q_square(0)
            pre_q_rstd(0)
            pre_x_square(0)
            pre_x_rstd(0, 0)
            schedule(step, act.Fori)

        @block.vector
        def _(dve):
            def pre_q_var(s):
                dve.wait_ge(S("q_musq"), s + 1)
                dve.tensor_tensor(q_rstd, small[:, T:2 * T], q_musq, ALU.subtract).then_inc(S("q_var"), 1)

            def pre_q(s):
                dve.wait_ge(S("q_rstd"), s + 1)
                dve.wait_ge(S("q_mm"), s + 1)
                dve.tensor_tensor(q, qb[:, 0:T], q_rstd, ALU.mult).then_inc(S("q_scaled"), 1)
                dve.wait_ge(S("q_scaled"), s + 1)
                dve.tensor_scalar(q, q, q_bias, None, ALU.add).then_inc(S("q_out"), 1)

            def pre_x(s, par):
                dve.wait_ge(S("sum_x2"), s + 1)
                dve.wait_ge(S("x_musq"), s + 1)
                dve.tensor_tensor(rstd[par], rows, musq, ALU.subtract).then_inc(S("x_var"), 1)

            def weigh_k(s, c):
                dve.wait_ge(S("k_mm"), KCH * s + c + 1)
                if c == 0:
                    dve.wait_ge(S("q_out"), s + 1)
                    if later(s, 1):
                        dve.wait_ge(S("scores"), s)
                dve.tensor_tensor(kq[:, c * CH:(c + 1) * CH].rearrange("p (n t) -> p n t", t=T),
                                  slot[c % 2].rearrange("p (n t) -> p n t", t=T), bcast_n(q, CH // T), ALU.mult)\
                   .then_inc(S("kq"), 1)

            def split_prob(s):
                dve.wait_ge(S("prob_hi"), s + 1)
                if later(s, 1):
                    dve.wait_ge(S("a_mm"), KCH * s)
                dve.scalar_tensor_tensor(prob16, hi, p("dup"), prob, ALU.mult, ALU.add).then_inc(S("prob16"), 1)

            def weigh_v(s, par, c):
                dve.wait_ge(S("a_mm"), KCH * s + c + 1)
                if c == 0:
                    dve.wait_ge(S("v_out"), KCH * (s + 1))
                quarter = by_n(v[par])[:, :, c * TQ:(c + 1) * TQ]
                dve.tensor_tensor(quarter, by_n(slot[1]), quarter, ALU.mult).then_inc(S("av"), 1)

            def halve_v(s, w, i):
                dve.wait_ge(*((S("av"), KCH * (s + 1)) if i == 0 else (S("av_part"), 3 * s + i)))
                n = 8 * T >> i
                if i == 3 and later(s, 1):
                    dve.wait_ge(S("o_mm"), s)
                dve.tensor_tensor(av_sum if i == 3 else w[:, 0:n], w[:, 0:n], w[:, n:2 * n], ALU.add)\
                   .then_inc(S("av_sum" if i == 3 else "av_part"), 1)

            def finish(s):
                dve.wait_ge(S("o_mm"), s + 1)
                dve.wait_ge(S("h_base"), s + 1)
                cols = core.h[:, bass.ds(s * T, T)]
                dve.tensor_tensor(cols, qb[:, T:2 * T], cols, ALU.add).then_inc(S("h_out"), 1)

            def step(s, par, front, back, pre):
                if front:
                    weigh_k(s, 0)
                    weigh_k(s, 1)
                if later(s, 2):
                    halve_v(s - 2, v[par], 1)
                if front:
                    weigh_k(s, 2)
                    weigh_k(s, 3)
                if back:
                    split_prob(s - 1)
                if later(s, 2):
                    halve_v(s - 2, v[par], 2)
                    halve_v(s - 2, v[par], 3)
                if back:
                    weigh_v(s - 1, 1 - par, 0)
                if front:
                    dve.wait_ge(S("scores"), s + 1)
                    dve.wait_ge(S("x_rstd"), s + 1)
                    if back:
                        dve.wait_ge(S("prob16"), s)
                    dve.tensor_tensor(prob, rows, rstd[par], ALU.mult).then_inc(S("s_scaled"), 1)
                    dve.wait_ge(S("s_scaled"), s + 1)
                    dve.tensor_reduce(top, prob.rearrange("p (n t) -> p t n", n=N), AX.X, ALU.max)\
                       .then_inc(S("s_max"), 1)
                if back:
                    weigh_v(s - 1, 1 - par, 1)
                if later(s, 2):
                    finish(s - 2)
                if back:
                    weigh_v(s - 1, 1 - par, 2)
                if pre:
                    pre_q_var(s + 1)
                if front:
                    dve.wait_ge(S("s_exp"), s + 1)
                    dve.tensor_reduce(den, prob.rearrange("p (n t) -> p t n", n=N), AX.X, ALU.add)\
                       .then_inc(S("s_den"), 1)
                    dve.wait_ge(S("s_den"), s + 1)
                    dve.reciprocal(rden, den).then_inc(S("inv_den"), 1)
                if back:
                    weigh_v(s - 1, 1 - par, 3)
                if pre:
                    pre_q(s + 1)
                if back:
                    halve_v(s - 1, v[1 - par], 0)
                if pre:
                    pre_x(s + 1, 1 - par)

            pre_q_var(0)
            pre_q(0)
            pre_x(0, 0)
            schedule(step, dve.Fori)

        @block.tensor
        def _(pe):
            def quarters(weights, source):
                for half in range(2):
                    for g in range(4):
                        view = by_n(source)[:, half * 8:half * 8 + 8, g * TQ:(g + 1) * TQ]
                        mm = pe.matmul(rows[32 * g:32 * g + 32, half * BANK:(half + 1) * BANK], weights, view,
                                       start=True, stop=True)
                return mm

            def pre_q(s):
                pe.wait_ge(S("rf_sq"), s + 1)
                if later(s, 1):
                    pe.wait_ge(S("q_var"), s)
                    pe.wait_ge(S("q_scaled"), s)
                if later(s, 3):
                    pe.wait_ge(S("h_out"), s - 2)
                pe.matmul(small[:, 0:T], p("mean"), rf, start=True, stop=True)
                pe.matmul(small[:, T:2 * T], p("mean"), rf_sq, start=True, stop=True).then_inc(S("q_stats"), 1)
                pe.matmul(qb[:, 0:T], core.wq[:, :], rf, start=True, stop=True).then_inc(S("q_mm"), 1)

            def pre_sum(s, par):
                pe.wait_ge(S(f"x_in{par}"), x_loaded(s, par))
                if later(s, 1):
                    pe.wait_ge(S("s_scaled"), s)
                quarters(p("sum_c"), xt[par]).then_inc(S("sum_x"), 1)

            def pre_sum_squares(s):
                pe.wait_ge(S("x_sq"), s + 1)
                pe.wait_ge(S("x_musq"), s + 1)
                quarters(p("sum_c"), xsq).then_inc(S("sum_x2"), 1)

            def project(weights, source, dst):
                for b in range(2):
                    mm = pe.matmul(dst[:, b * BANK:(b + 1) * BANK], weights, source[:, b * BANK:(b + 1) * BANK],
                                   start=True, stop=True)
                return mm

            def project_k(s, par, c):
                if c == 0 and later(s, 1):
                    pe.wait_ge(S("v_out"), KCH * s)
                if c == 1 and later(s, 1):
                    pe.wait_ge(S("kq"), KCH * s)
                    if later(s, 2):
                        pe.wait_ge(S("av"), KCH * (s - 1))
                if c >= 2:
                    pe.wait_ge(S("kq"), KCH * s + c - 1)
                project(core.wk[:, :], xt[par][:, c * CH:(c + 1) * CH], slot[c % 2]).then_inc(S("k_mm"), 1)

            def project_v(s, par, c):
                if c > 0:
                    pe.wait_ge(S("v_out"), KCH * s + c)
                else:
                    pe.wait_ge(S("kq"), KCH * s + 3)
                project(core.wv[:, :], xt[par][:, c * CH:(c + 1) * CH], slot[0]).then_inc(S("v_mm"), 1)

            def spread_prob(s, c):
                if c == 0:
                    pe.wait_ge(S("prob16"), s + 1)
                    if not isinstance(s, int) or s + 1 < STEPS:
                        pe.wait_ge(S("kq"), KCH * (s + 2))
                if c > 0 or later(s, 1):
                    pe.wait_ge(S("av"), KCH * s + c)
                project(core.bsel[:, c * 128:(c + 1) * 128], prob16, slot[1]).then_inc(S("a_mm"), 1)

            def finish(s):
                pe.wait_ge(S("av_sum"), s + 1)
                if later(s, 1):
                    pe.wait_ge(S("h_out"), s)
                pe.matmul(qb[:, T:2 * T], p("proj"), av_sum, start=True, stop=True).then_inc(S("o_mm"), 1)

            def step(s, par, front, back, pre):
                if front:
                    for c in range(KCH):
                        project_k(s, par, c)
                    project_v(s, par, 0)
                if front:
                    pe.wait_ge(S("kq"), KCH * (s + 1))
                    pe.wait_ge(S("x_var"), s + 1)
                    quarters(p("sum_d"), kq).then_inc(S("scores"), 1)
                if back:
                    spread_prob(s - 1, 0)
                if later(s, 2):
                    finish(s - 2)
                if front:
                    project_v(s, par, 1)
                if back:
                    spread_prob(s - 1, 1)
                if front:
                    project_v(s, par, 2)
                if back:
                    spread_prob(s - 1, 2)
                if pre:
                    pre_q(s + 1)
                if back:
                    spread_prob(s - 1, 3)
                if pre:
                    pre_sum(s + 1, 1 - par)
                if front:
                    project_v(s, par, 3)
                if pre:
                    pre_sum_squares(s + 1)

            pre_q(0)
            pre_sum(0, 0)
            pre_sum_squares(0)
            schedule(step, pe.Fori)


def normalize(core, tag, src, dst=None, write=None, extra=None):
    nc, p = core.nc, core.p
    S = lambda name: core.sem(f"{tag}_{name}")
    ring, chunks = 4, COLS // BANK
    sq, musq, rstd, cen = ([core.take(BANK) for _ in range(ring)] for _ in range(4))
    extra = extra or {}

    def mean(c):
        return core.bank(c % ring)

    def square(c):
        return core.bank(ring + c % ring)

    def part(view, c):
        return view[:, c * BANK:(c + 1) * BANK]

    with nc.Block() as block:
        @block.tensor
        def _(pe):
            for c in range(chunks):
                if c >= ring:
                    pe.wait_ge(S("centred"), c - ring + 1)
                    pe.wait_ge(S("musq"), c - ring + 1)
                pe.matmul(mean(c), p("mean"), part(src, c), start=True, stop=True).then_inc(S("mean"), 1)
                pe.wait_ge(S("sq"), c + 1)
                if c >= ring:
                    pe.wait_ge(S("var"), c - ring + 1)
                pe.matmul(square(c), p("mean"), sq[c % ring], start=True, stop=True).then_inc(S("mean_sq"), 1)
            if "pe" in extra:
                extra["pe"](pe)

        @block.scalar
        def _(act):
            def squares(c):
                if c < chunks:
                    if c >= ring:
                        act.wait_ge(S("mean_sq"), c - ring + 1)
                    act.activation(sq[c % ring], part(src, c), ACT.Square).then_inc(S("sq"), 1)

            def mean_squared(c):
                if c < chunks:
                    act.wait_ge(S("mean"), c + 1)
                    if c >= ring:
                        act.wait_ge(S("var"), c - ring + 1)
                    act.activation(musq[c % ring], mean(c), ACT.Square).then_inc(S("musq"), 1)

            def written(c):
                if write and c >= 0:
                    act.wait_ge(S("scaled"), c + 1)
                    write(act, c, cen[c % ring]).then_inc(S("written"), 1)

            act.preload_act_table_set("natural_log_exp_and_others")
            squares(0)
            squares(1)
            mean_squared(0)
            for c in range(chunks):
                squares(c + 2)
                mean_squared(c + 1)
                act.wait_ge(S("var"), c + 1)
                act.activation(rstd[c % ring], rstd[c % ring], ACT.Ln, bias=EPS).then_inc(S("ln"), 1)
                written(c - 1)
                act.wait_ge(S("ln"), c + 1)
                act.activation(rstd[c % ring], rstd[c % ring], ACT.Exp, scale=-0.5).then_inc(S("rstd"), 1)
            written(chunks - 1)
            if "act" in extra:
                extra["act"](act)

        @block.vector
        def _(dve):
            def scale(c):
                if c >= 0:
                    dve.wait_ge(S("rstd"), c + 1)
                    dve.wait_ge(S("centred"), c + 1)
                    dve.tensor_tensor(part(dst, c) if dst is not None else cen[c % ring], cen[c % ring],
                                      rstd[c % ring], ALU.mult).then_inc(S("scaled"), 1)

            for c in range(chunks):
                dve.wait_ge(S("mean_sq"), c + 1)
                dve.wait_ge(S("musq"), c + 1)
                if c >= ring:
                    dve.wait_ge(S("scaled"), c - ring + 1)
                    if write:
                        dve.wait_ge(S("written"), c - ring + 1)
                dve.tensor_tensor(rstd[c % ring], square(c), musq[c % ring], ALU.subtract).then_inc(S("var"), 1)
                dve.tensor_tensor(cen[c % ring], part(src, c), mean(c), ALU.subtract).then_inc(S("centred"), 1)
                scale(c - 1)
            scale(chunks - 1)
            if "dve" in extra:
                extra["dve"](dve)

        if "sync" in extra:
            @block.sync
            def _(sp):
                extra["sync"](sp)


def by_seq(view):
    return view.rearrange("p (s t) -> p s t", t=T)


def mix_input(core):
    normalize(core, "xn", core.h[:, :], dst=core.x[:, :])


def local_branch(core, conv):
    p, S = core.p, core.sem
    x = core.x[:, :]

    def convolve(dve):
        dve.tensor_scalar(conv, x, p("conv_w", 1, 1), None, ALU.mult).then_inc(S("conv"), 1)
        dve.wait_ge(S("conv"), 1)
        after, before = by_seq(conv)[:, :, 1:T], by_seq(conv)[:, :, 0:T - 1]
        dve.scalar_tensor_tensor(after, by_seq(x)[:, :, 0:T - 1], p("conv_w", 0, 1), after, ALU.mult, ALU.add)\
           .then_inc(S("conv"), 1)
        dve.wait_ge(S("conv"), 2)
        dve.scalar_tensor_tensor(before, by_seq(x)[:, :, 1:T], p("conv_w", 2, 1), before, ALU.mult, ALU.add)\
           .then_inc(S("conv"), 1)

    def gelu(act):
        act.wait_ge(S("conv"), 3)
        act.activation(conv, conv, ACT.Gelu, bias=p("conv_b")).then_inc(S("conv_gelu"), 1)

    def add(dve):
        dve.wait_ge(S("conv_gelu"), 1)
        dve.tensor_tensor(core.h[:, :], core.h[:, :], conv, ALU.add).then_inc(S("conv_added"), 1)

    return convolve, gelu, add


def between_directions(core):
    p = core.p
    x = core.x[:, :]

    def write(act, c, chunk):
        return act.activation(by_seq(x[:, c * BANK:(c + 1) * BANK])[:, :, ::-1], by_seq(chunk), ACT.Identity,
                              bias=p("norm_b"), scale=p("norm_w"))

    normalize(core, "yn", x, write=write)


def add_backward(core):
    with core.nc.Block() as block:
        @block.vector
        def _(dve):
            dve.tensor_tensor(by_seq(core.h[:, :]), by_seq(core.h[:, :]), by_seq(core.x[:, :])[:, :, ::-1], ALU.add)


def mixer(core, d, beside=None):
    nc, p = core.nc, core.p
    S = lambda name: core.sem(f"{d}_{name}")
    di = "fb".index(d)
    b_dt = core.cols[:, 3 + di:4 + di]
    neg_a = core.neg_a[:, di * SP:(di + 1) * SP]
    decay = core.take(4 * CH)
    states = [core.take(4 * CH) for _ in range(2)]
    xi, bm, cm = ([core.take(CH) for _ in range(2)] for _ in range(3))
    zs, soft, dt, dx, rest, gate = (core.take(CH) for _ in range(6))
    dt_part = [core.take(CH // 2, BF16) for _ in range(3)]
    dx_part = [core.take(CH // 2, BF16) for _ in range(3)]
    dt_rows = [core.take(4 * CH // 2, BF16) for _ in range(2)]
    dx_rows = [core.take(4 * CH // 2, BF16) for _ in range(2)]
    ps_dt, ps_dx, ps_y, ps_p = (core.bank(b, 2) for b in (0, 2, 4, 6))
    ps_o = ps_p[:, 0:BANK]
    convolve, gelu, add_local = beside(core, states[1]) if beside else (None,) * 3

    def schedule(emit, loop):
        emit(0, 0, last=False)
        with loop(0, (GROUPS - 2) // 2) as k:
            emit(2 * k + 1, 1, last=False)
            emit(2 * k + 2, 0, last=False)
        emit(GROUPS - 1, 1, last=True)
        emit(GROUPS, 0, last=None)

    def wait_past(eng, name, count, g, first):
        if not isinstance(g, int) or g >= first:
            eng.wait_ge(S(name), count)

    def has_post(g):
        return not isinstance(g, int) or g >= 1

    with nc.Block() as block:
        @block.sync
        def _(sp):
            def spread(g, par, name, parts, rows):
                for i in range(3):
                    sp.wait_ge(S(f"{name}_part"), 3 * g + i + 1)
                    for m in range(4):
                        sp.dma_start(rows[par][32 * i:32 * i + 32, m * CH:(m + 1) * CH],
                                     parts[i][32 * m:32 * m + 32, :]).then_inc(S(f"{name}_rows"), 16)

            def step(g, par, last):
                if last is False:
                    spread(g + 1, 1 - par, "dt", dt_part, dt_rows)
                    spread(g + 1, 1 - par, "dx", dx_part, dx_rows)

            spread(0, 0, "dt", dt_part, dt_rows)
            spread(0, 0, "dx", dx_part, dx_rows)
            schedule(step, sp.Fori)

        @block.tensor
        def _(pe):
            def bank(view, b):
                return view[:, b * BANK:(b + 1) * BANK]

            def spread_dt(g, par, k):
                if k >= 16:
                    g, par, k = g + 1, 1 - par, k - 16
                j, m = divmod(k, 4)
                if k == 0:
                    pe.wait_ge(S("dt_rows"), 16 * 12 * (g + 1))
                if not (isinstance(g, int) and g == 0 and k == 0):
                    pe.wait_ge(S("decay"), 16 * g + k)
                for b in range(2):
                    mm = pe.matmul(bank(ps_dt, b), core.rsel[:, 128 * j:128 * j + 128],
                                   dt_rows[par][0:96, m * CH + b * BANK:m * CH + (b + 1) * BANK], start=True, stop=True)
                mm.then_inc(S("dt_mm"), 1)

            def spread_dx(g, par, k):
                j, m = divmod(k, 4)
                if k == 0:
                    pe.wait_ge(S("dx_rows"), 16 * 12 * (g + 1))
                for b in range(2):
                    if not (isinstance(g, int) and g == 0 and k == 0):
                        pe.wait_ge(S("inject"), 32 * g + 2 * k - 1 + b)
                    pe.matmul(bank(ps_dx, b), core.rsel[:, 128 * j:128 * j + 128],
                              dx_rows[par][0:96, m * CH + b * BANK:m * CH + (b + 1) * BANK], start=True, stop=True)\
                      .then_inc(S("dx_mm"), 1)

            def project_in(name, at, g, b):
                mm = pe.matmul(bank(ps_p, b), p(d + "_win", at + 128 * b, 128), core.x[:, bass.ds(g * GC, GC)],
                               start=True, stop=True)
                if b == 1:
                    mm.then_inc(S(f"{name}_mm"), 1)

            def project_xi(name, i, par, b):
                mm = pe.matmul(bank(ps_p, b), p(d + "_wx", 128 * i, 128), bank(xi[par], b), start=True, stop=True)
                if b == 1:
                    mm.then_inc(S(f"{name}_mm"), 1)

            def sum_states(quad, j, b, g):
                if b == 0:
                    pe.wait_ge(S("ch"), 4 * quad + 4)
                for m in range(4):
                    mm = pe.matmul(bank(ps_y, b)[32 * m:32 * m + 32, :], p("ysel", 32 * j, 32),
                                   bank(states[j % 2][:, m * CH:(m + 1) * CH], b), start=False, stop=(j == 3))
                if b == 1:
                    mm.then_inc(S("y_mm"), 1)

            def skip(g, par, b):
                if b == 0:
                    wait_past(pe, "gated", g, g, 1)
                pe.matmul(bank(ps_y, b), p(d + "_skip"), bank(xi[par], b), start=True, stop=False)

            def project_out(g):
                pe.wait_ge(S("gated"), g + 1)
                for b in range(2):
                    mm = pe.matmul(ps_o[64 * b:64 * b + 64, :], p(d + "_wo"), bank(gate, b), start=True, stop=True)
                mm.then_inc(S("o_mm"), 1)

            def step(g, par, last):
                post, more = has_post(g), last is False
                n, q = 4 * g, 1 - par
                if last is None:
                    project_in("z", 256, g - 1, 1)
                    for b in range(2):
                        sum_states(n - 1, 3, b, g)
                    pe.wait_ge(S("z"), g)
                    project_out(g - 1)
                    return
                for k in range(16):
                    spread_dx(g, par, k)
                    if k == 0 and post:
                        project_in("z", 256, g - 1, 1)
                    if k in (2, 3) and more:
                        if k == 2:
                            if post:
                                pe.wait_ge(S("z"), g)
                            else:
                                pe.wait_ge(S("c_out"), 1)
                        project_in("xi", 0, g + 1, k - 2)
                    if k in (2, 3) and post:
                        sum_states(n - 1, 3, k - 2, g)
                    if k in (4, 5):
                        skip(g, par, k - 4)
                    if k in (6, 7) and more:
                        if k == 6:
                            pe.wait_ge(S("xi"), g + 2)
                        project_xi("dtp", 0, q, k - 6)
                    if k in (7, 8):
                        sum_states(n, 0, k - 7, g)
                    if k == 8 and post:
                        if more:
                            pe.wait_ge(S("dt_relu"), g + 2)
                        else:
                            pe.wait_ge(S("z"), g)
                        project_out(g - 1)
                    if k in (10, 11) and more:
                        if k == 10:
                            if post:
                                pe.wait_ge(S("o_out"), g)
                            else:
                                pe.wait_ge(S("dt_relu"), g + 2)
                        project_xi("b", 1, q, k - 10)
                    if k in (10, 11):
                        sum_states(n + 1, 1, k - 10, g)
                    if k in (13, 14) and more:
                        if k == 13:
                            pe.wait_ge(S("b_out"), g + 2)
                        project_xi("c", 2, q, k - 13)
                    if k in (14, 15):
                        sum_states(n + 2, 2, k - 14, g)
                    if k == 15:
                        if more:
                            pe.wait_ge(S("c_out"), g + 2)
                        else:
                            pe.wait_ge(S("o_out"), g)
                        project_in("z", 256, g, 0)
                    if more or k + 2 < 16:
                        spread_dt(g, par, k + 2)

            for b in range(2):
                project_in("xi", 0, 0, b)
            for name, i, freed in (("dtp", 0, "xi"), ("b", 1, "dt_relu"), ("c", 2, "b_out")):
                pe.wait_ge(S(freed), 1)
                for b in range(2):
                    project_xi(name, i, 0, b)
            spread_dt(0, 0, 0)
            spread_dt(0, 0, 1)
            schedule(step, pe.Fori)

        @block.scalar
        def _(act):
            def silu(name, out, g):
                act.preload_act_table_set("silu_and_others")
                act.wait_ge(S(f"{name}_mm"), g + 1)
                if name == "xi":
                    wait_past(act, "y_mm", 4 * (g - 2) + 1, g, 2)
                else:
                    wait_past(act, "gated", g, g, 1)
                act.activation(out, ps_p, ACT.Silu, bias=p(f"{d}_b{name}")).then_inc(S(name), 1)
                act.preload_act_table_set("natural_log_exp_and_others")

            def softplus_in(g):
                act.wait_ge(S("dtp_mm"), g + 1)
                wait_past(act, "dt", g, g, 1)
                act.activation(soft, ps_p, ACT.Abs, bias=b_dt).then_inc(S("dt_abs"), 1)
                wait_past(act, "dt_part", 3 * g, g, 1)
                wait_past(act, "dx_part", 3 * g, g, 1)
                act.activation(dt, ps_p, ACT.Relu, bias=b_dt).then_inc(S("dt_relu"), 1)

            def softplus_log(g):
                act.wait_ge(S("dt_abs"), g + 1)
                act.activation(soft, soft, ACT.Exp, scale=-1.0).then_inc(S("dt_exp"), 1)
                act.wait_ge(S("dt_exp"), g + 1)
                act.activation(soft, soft, ACT.Ln, bias=1.0).then_inc(S("dt_ln"), 1)

            def high(name, src, parts, g):
                act.wait_ge(S(name), g + 1)
                wait_past(act, f"{name}_rows", 16 * 12 * g, g, 1)
                act.activation(parts[0], src, ACT.Copy).then_inc(S(f"{name}_part"), 1)

            def middle(name, parts, g):
                act.wait_ge(S(f"{name}_rest"), g + 1)
                act.activation(parts[1], rest, ACT.Copy).then_inc(S(f"{name}_part"), 1)

            def plain(name, out, bias, g):
                act.wait_ge(S(f"{name}_mm"), g + 1)
                wait_past(act, "ch", 16 * (g - 1), g, 2)
                act.activation(out, ps_p, ACT.Identity, bias=bias).then_inc(S(f"{name}_out"), 1)

            def output(g):
                act.wait_ge(S("o_mm"), g + 1)
                act.activation(core.x[:, bass.ds(g * GC, GC)], ps_o, ACT.Identity, bias=p(d + "_bo"))\
                   .then_inc(S("o_out"), 1)

            def step(g, par, last):
                if last is None:
                    silu("z", zs, g - 1)
                    output(g - 1)
                    return
                more, q = last is False, 1 - par
                for k in range(16):
                    n = 16 * g + k
                    m = k % 4
                    act.wait_ge(S("dt_mm"), n + 1)
                    if not (isinstance(n, int) and n < 4):
                        act.wait_ge(S("scan"), n - 3)
                    ring = by_seq(decay[:, m * CH:(m + 1) * CH])[:, :, 1:T]
                    scale = neg_a[:, 4 * m + k // 4:4 * m + k // 4 + 1]
                    act.activation(ring, by_seq(ps_dt)[:, :, 1:T], ACT.Exp, scale=scale).then_inc(S("decay"), 1)
                    if k == 2 and has_post(g):
                        silu("z", zs, g - 1)
                    if k == 4 and more:
                        silu("xi", xi[q], g + 1)
                    if k == 8 and more:
                        softplus_in(g + 1)
                    if k == 9 and more:
                        softplus_log(g + 1)
                    if k == 10 and has_post(g):
                        output(g - 1)
                    if k == 10 and more:
                        high("dt", dt, dt_part, g + 1)
                    if k == 11 and more:
                        middle("dt", dt_part, g + 1)
                        plain("b", bm[q], p(d + "_bB"), g + 1)
                        high("dx", dx, dx_part, g + 1)
                    if k == 13 and more:
                        middle("dx", dx_part, g + 1)
                    if k == 15 and more:
                        plain("c", cm[q], p(d + "_bC"), g + 1)

            silu("xi", xi[0], 0)
            softplus_in(0)
            softplus_log(0)
            plain("b", bm[0], p(d + "_bB"), 0)
            for name, src, parts in (("dt", dt, dt_part), ("dx", dx, dx_part)):
                high(name, src, parts, 0)
                middle(name, parts, 0)
            plain("c", cm[0], p(d + "_bC"), 0)
            if beside:
                gelu(act)
            schedule(step, act.Fori)

        @block.gpsimd
        def _(pool):
            def add_dt(g):
                pool.wait_ge(S("dt_ln"), g + 1)
                pool.wait_ge(S("dt_relu"), g + 1)
                pool.tensor_tensor(dt, dt, soft, ALU.add).then_inc(S("dt"), 1)

            def mul_dx(g, par):
                pool.wait_ge(S("dt"), g + 1)
                pool.wait_ge(S("xi"), g + 1)
                pool.tensor_tensor(dx, dt, xi[par], ALU.mult).then_inc(S("dx"), 1)

            def step(g, par, last):
                if last is None:
                    return
                for k in range(16):
                    j, m = divmod(k, 4)
                    pool.wait_ge(S("scan"), 16 * g + k + 1)
                    if k == 0:
                        pool.wait_ge(S("c_out"), g + 1)
                    part = states[j % 2][:, m * CH:(m + 1) * CH]
                    pool.tensor_tensor(part, part, cm[par], ALU.mult).then_inc(S("ch"), 1)
                    if last is False:
                        if k == 7:
                            add_dt(g + 1)
                        if k == 8:
                            mul_dx(g + 1, 1 - par)

            add_dt(0)
            mul_dx(0, 0)
            schedule(step, pool.Fori)

        @block.vector
        def _(dve):
            def split_rest(name, src, parts, g):
                dve.wait_ge(S(f"{name}_part"), 3 * g + 1)
                if name == "dx":
                    dve.wait_ge(S("dt_part"), 3 * g + 3)
                else:
                    wait_past(dve, "dx_part", 3 * g, g, 1)
                dve.tensor_tensor(rest, src, parts[0], ALU.subtract).then_inc(S(f"{name}_rest"), 1)

            def split_low(name, parts, g):
                dve.wait_ge(S(f"{name}_part"), 3 * g + 2)
                dve.tensor_tensor(parts[2], rest, parts[1], ALU.subtract).then_inc(S(f"{name}_part"), 1)

            def gated(g):
                dve.wait_ge(S("y_mm"), 4 * g + 4)
                dve.wait_ge(S("z"), g + 1)
                wait_past(dve, "o_mm", g, g, 1)
                dve.tensor_tensor(gate, ps_y, zs, ALU.mult).then_inc(S("gated"), 1)

            def step(g, par, last):
                if last is None:
                    gated(g - 1)
                    return
                for k in range(16):
                    j, m = divmod(k, 4)
                    n = 16 * g + k
                    part = states[j % 2][:, m * CH:(m + 1) * CH]
                    if k == 0:
                        dve.wait_ge(S("b_out"), g + 1)
                    if m == 0 and not (isinstance(g, int) and 4 * g + j < 2):
                        dve.wait_ge(S("y_mm"), 4 * g + j - 1)
                    for b in range(2):
                        half = slice(b * BANK, (b + 1) * BANK)
                        dve.wait_ge(S("dx_mm"), 2 * n + 1 + b)
                        dve.tensor_tensor(part[:, half], ps_dx[:, half], bm[par][:, half], ALU.mult)\
                           .then_inc(S("inject"), 1)
                    dve.wait_ge(S("decay"), n + 1)
                    dve.wait_ge(S("inject"), 2 * n + 2)
                    dve.tensor_tensor_scan(part, decay[:, m * CH:(m + 1) * CH], part, 0.0, ALU.mult, ALU.add)\
                       .then_inc(S("scan"), 1)
                    if k == 3 and has_post(g):
                        gated(g - 1)
                    if last is False:
                        if k == 10:
                            split_rest("dt", dt, dt_part, g + 1)
                        if k == 11:
                            split_low("dt", dt_part, g + 1)
                            split_rest("dx", dx, dx_part, g + 1)
                        if k == 13:
                            split_low("dx", dx_part, g + 1)

            dve.memset(by_seq(decay)[:, :, 0:1], 0.0).then_inc(S("starts"), 1)
            if beside:
                convolve(dve)
            for name, src, parts in (("dt", dt, dt_part), ("dx", dx, dx_part)):
                split_rest(name, src, parts, 0)
                split_low(name, parts, 0)
            if beside:
                add_local(dve)
                dve.wait_ge(core.sem("conv_added"), 1)
            schedule(step, dve.Fori)


def route(core, ffn):
    nc, p, S = core.nc, core.p, core.sem
    x, tiles = core.x[:, :], COLS // 128
    wide = tiles * HALVES
    high, low = core.take(COLS // 2, F16), core.take(COLS // 2, F16)
    logits, first, second, key = (core.take(wide * EXPERTS) for _ in range(4))
    top, pick, second_top, ratio, weight = (core.take(wide) for _ in range(5))
    parts = core.take(wide * EXPERTS, F16)
    w_raw = core.take(2 * EXPERTS * HID)

    def gate(pe):
        pe.wait_ge(S("hn_centred"), COLS // BANK - 2)
        pe.wait_ge(S("hn_musq"), COLS // BANK - 2)
        for t in range(tiles):
            if t % 4 == 0:
                pe.wait_ge(S("hn_scaled"), t // 4 + 1)
            mm = pe.matmul(core.bank(0, 2)[:, t * 32:(t + 1) * 32], x[:, t * 128:(t + 1) * 128], p("gate"),
                           start=True, stop=True)
        mm.then_inc(S("logits_mm"), 1)

    def load(sp):
        sp.dma_start(w_raw, ffn["wmoe"]).then_inc(S("wmoe_in"), 16)
        sp.dma_start(ffn["sel"], ffn["ffn16"]).then_inc(S("ffn16_in"), 16)
        sp.dma_start(ffn["w3"], ffn["w3_in"]).then_inc(S("w3_in"), 16)

    def split_weights(act):
        act.wait_ge(S("wmoe_in"), 16)
        act.activation(ffn["wh"], w_raw, ACT.Copy).then_inc(S("w_high"), 1)

    normalize(core, "hn", core.h[:, :], dst=x, extra={"pe": gate, "sync": load, "act": split_weights})

    def rows(view):
        return view.rearrange("p (w e) -> p w e", e=EXPERTS)

    def spread(view):
        return view.unsqueeze(2).to_broadcast([128, wide, EXPERTS])

    def const(view):
        return view.unsqueeze(1).to_broadcast([128, wide, EXPERTS])

    part_view = parts.rearrange("p (t k u) -> p k t u", k=2, u=HALVES * EXPERTS)

    turned = [core.bank(4 + b).bitcast(F16)[0:64, :] for b in range(4)]

    with nc.Block() as block:
        @block.sync
        def _(sp):
            for i, part in enumerate((high, low)):
                sp.wait_ge(S("x_part"), i + 1)
                for q in range(HALVES):
                    dst = ffn["x"][64 * i:64 * i + 64, :].rearrange("p (g q t) -> p g q t", g=GROUPS, q=HALVES)
                    sp.dma_start(dst[:, :, q, :], part[64 * q:64 * q + 64, :].rearrange("p (g t) -> p g t", g=GROUPS))\
                      .then_inc(S("x_stacked"), 16)
            sp.wait_ge(S("x_stacked"), 64)
            sp.wait_ge(S("w3_in"), 16)

        @block.scalar
        def _(act):
            act.activation(high, x, ACT.Copy).then_inc(S("x_part"), 1)
            act.wait_ge(S("gap"), 1)
            act.activation(ratio, ratio, ACT.Exp).then_inc(S("ratio"), 1)
            for b in range(4):
                act.wait_ge(S("turned"), b + 1)
                act.activation(ffn["disp"][0:64, b * CH:(b + 1) * CH], turned[b], ACT.Copy).then_inc(S("disp_out"), 1)

        @block.tensor
        def _(pe):
            pe.wait_ge(S("parts"), 2)
            pe.wait_ge(S("ffn16_in"), 16)
            for t in range(tiles):
                mm = pe.transpose(turned[t // 8][:, (t % 8) * 128:(t % 8 + 1) * 128], parts[:, t * 64:(t + 1) * 64],
                                  ffn["ident"])
                if t % 8 == 7:
                    mm.then_inc(S("turned"), 1)

        @block.gpsimd
        def _(pool):
            pool.memset(ffn["disp"][64:128, :], 0.0).then_inc(S("disp_zero"), 1)
            pool.wait_ge(S("disp_zero"), 1)
            pool.wait_ge(S("x_part"), 1)
            pool.tensor_tensor(low, x, high, ALU.subtract).then_inc(S("x_part"), 1)
            pool.wait_ge(S("x_part"), 2)
            pool.wait_ge(S("w_high"), 1)
            pool.tensor_tensor(ffn["wl"], w_raw, ffn["wh"], ALU.subtract).then_inc(S("w_low"), 1)

        @block.vector
        def _(dve):
            done = [0]

            def after():
                dve.wait_ge(S("route"), done[0])

            def mark(instruction):
                done[0] += 1
                instruction.then_inc(S("route"), 1)

            dve.wait_ge(S("logits_mm"), 1)
            mark(dve.tensor_tensor(rows(logits), rows(core.bank(0, 2)), const(p("gate_b")), ALU.add))

            def pick_top(best, hot):
                after()
                mark(dve.tensor_reduce(best, rows(logits), AX.X, ALU.max))
                after()
                mark(dve.tensor_tensor(rows(key), rows(logits), spread(best), ALU.is_equal))
                after()
                mark(dve.tensor_tensor(rows(key), rows(key), const(p("rank")), ALU.mult))
                after()
                mark(dve.tensor_reduce(pick, rows(key), AX.X, ALU.max))
                after()
                mark(dve.tensor_tensor(rows(hot), rows(key), spread(pick), ALU.is_equal))

            pick_top(top, first)
            after()
            mark(dve.scalar_tensor_tensor(logits, first, -3e38, logits, ALU.mult, ALU.add))
            pick_top(second_top, second)
            after()
            dve.tensor_tensor(ratio, second_top, top, ALU.subtract).then_inc(S("gap"), 1)
            dve.wait_ge(S("ratio"), 1)
            mark(dve.tensor_scalar(weight, ratio, 1.0, None, ALU.add))
            after()
            mark(dve.reciprocal(weight, weight))
            after()
            mark(dve.tensor_tensor(ratio, ratio, weight, ALU.mult))
            mark(dve.tensor_tensor(rows(first), rows(first), spread(weight), ALU.mult))
            after()
            mark(dve.tensor_tensor(rows(second), rows(second), spread(ratio), ALU.mult))
            after()
            mark(dve.tensor_tensor(first, first, second, ALU.add))
            after()
            flat = first.rearrange("p (t u) -> p t u", u=HALVES * EXPERTS)
            dve.tensor_copy(part_view[:, 0], flat).then_inc(S("parts"), 1)
            dve.wait_ge(S("parts"), 1)
            dve.tensor_tensor(part_view[:, 1], flat, part_view[:, 0], ALU.subtract).then_inc(S("parts"), 1)


def experts(core, ffn, out):
    nc, S = core.nc, core.sem
    act_h = [core.take(CH) for _ in range(2)]
    hidden = [core.take(CH) for _ in range(2)]
    ps_1, ps_2, ps_d, ps_y = core.bank(0, 2), core.bank(2, 2), core.bank(4, 2), core.bank(6)

    def schedule(emit, loop):
        emit(0)
        with loop(1, GROUPS) as g:
            emit(g)

    def first_of_all(g, e, n=1):
        return isinstance(g, int) and e < n

    with nc.Block() as block:
        @block.tensor
        def _(pe):
            def tokens(g, q):
                return ffn["x"][:, bass.ds(g * GT + q * GC, GC)]

            def hidden_in(g, e, which, out_banks):
                for q in range(HALVES):
                    bank = out_banks[:, q * BANK:(q + 1) * BANK]
                    cols = slice((which * EXPERTS + e) * HID, (which * EXPERTS + e + 1) * HID)
                    pe.matmul(bank, ffn["wh"][:, cols], tokens(g, q), start=True, stop=False)
                    mm = pe.matmul(bank, ffn["wl"][:, cols], tokens(g, q), start=False, stop=True)
                return mm

            def expert_out(n, e):
                pe.wait_ge(S("hidden"), n + 1)
                for q in range(HALVES):
                    mm = pe.matmul(ps_y[64 * q:64 * q + 64, :], ffn["w3"][:, 64 * e:64 * e + 64],
                                   hidden[e % 2][:, q * BANK:(q + 1) * BANK], start=(e == 0), stop=(e == EXPERTS - 1))
                mm.then_inc(S("y_mm"), 1)

            def group(g):
                for e in range(EXPERTS):
                    n = EXPERTS * g + e
                    if not first_of_all(g, e):
                        pe.wait_ge(S("h1_act"), n)
                    hidden_in(g, e, 0, ps_1).then_inc(S("h1_mm"), 1)
                    if not first_of_all(g, e):
                        pe.wait_ge(S("h12"), n)
                    hidden_in(g, e, 1, ps_2).then_inc(S("h2_mm"), 1)
                    if not first_of_all(g, e):
                        pe.wait_ge(S("hidden"), n)
                    for q in range(HALVES):
                        at = (2 * e + q) * 128
                        mm = pe.matmul(ps_d[:, q * BANK:(q + 1) * BANK], ffn["dsel"][:, at:at + 128],
                                       ffn["disp"][:, bass.ds(g * GC, GC)], start=True, stop=True)
                    mm.then_inc(S("disp_mm"), 1)
                    if e > 0:
                        if e == 1 and not first_of_all(g, e, 2):
                            pe.wait_ge(S("y_added"), g)
                        expert_out(n - 1, e - 1)
                    elif not first_of_all(g, e):
                        expert_out(n - 1, EXPERTS - 1)

            schedule(group, pe.Fori)
            expert_out(EXPERTS * GROUPS - 1, EXPERTS - 1)

        @block.scalar
        def _(act):
            def group(g):
                for e in range(EXPERTS):
                    n = EXPERTS * g + e
                    act.wait_ge(S("h1_mm"), n + 1)
                    if not first_of_all(g, e, 2):
                        act.wait_ge(S("h12"), n - 1)
                    act.activation(act_h[e % 2], ps_1, ACT.Silu).then_inc(S("h1_act"), 1)

            act.preload_act_table_set("silu_and_others")
            schedule(group, act.Fori)

        @block.vector
        def _(dve):
            def add_out(g):
                dve.wait_ge(S("y_mm"), EXPERTS * g + EXPERTS)
                cols = core.h[:, bass.ds(g * GC, GC)]
                dve.tensor_tensor(cols, ps_y, cols, ALU.add).then_inc(S("y_added"), 1)

            def group(g):
                for e in range(EXPERTS):
                    n = EXPERTS * g + e
                    dve.wait_ge(S("h2_mm"), n + 1)
                    dve.wait_ge(S("h1_act"), n + 1)
                    if not first_of_all(g, e, 2):
                        dve.wait_ge(S("y_mm"), n - 1)
                    dve.tensor_tensor(hidden[e % 2], ps_2, act_h[e % 2], ALU.mult).then_inc(S("h12"), 1)
                    dve.wait_ge(S("disp_mm"), n + 1)
                    dve.wait_ge(S("h12"), n + 1)
                    dve.tensor_tensor(hidden[e % 2], ps_d, hidden[e % 2], ALU.mult).then_inc(S("hidden"), 1)
                    if e == 0 and not isinstance(g, int):
                        add_out(g - 1)

            schedule(group, dve.Fori)
            add_out(GROUPS - 1)

        @block.sync
        def _(sp):
            with sp.Fori(0, GROUPS) as g:
                sp.wait_ge(S("y_added"), g + 1)
                cols = bass.ds(g * GC, GC)
                sp.dma_start(out[:, cols], core.h[:, cols]).then_inc(S("out"), 16)
            sp.wait_ge(S("out"), 16 * GROUPS)


def feed_forward(core, ffn16, wmoe, w3, out):
    sel = core.take((2 * EXPERTS + 1) * 128 // 2, F16)
    weights = EXPERTS * HID
    ffn = {"ffn16": ffn16, "wmoe": wmoe, "w3_in": w3, "sel": sel, "dsel": sel[:, 0:2 * EXPERTS * 128],
           "ident": sel[:, 2 * EXPERTS * 128:], "wh": core.take(weights, F16), "wl": core.take(weights, F16),
           "w3": core.take(EXPERTS * C), "x": core.take(GROUPS * GT // 2, F16), "disp": core.take(COLS // 2, F16)}
    kept = core.used
    route(core, ffn)
    core.used = kept
    experts(core, ffn, out)


def program(nc, xin, params, bsel, rsel, ffn16, wmoe, w3, out):
    core = Core(nc)
    with core.stage():
        xt = [core.take(PIX) for _ in range(2)]
        setup(core, params, bsel, rsel, xin, xt)
        attention(core, xin, xt)
    with core.stage():
        mix_input(core)
    with core.stage():
        mixer(core, "f", beside=local_branch)
    with core.stage():
        between_directions(core)
    with core.stage():
        mixer(core, "b")
    with core.stage():
        add_backward(core)
        feed_forward(core, ffn16, wmoe, w3, out)


def kernel(**inputs):
    import numpy as np
    import concourse.bacc as bacc
    from concourse.bass_utils import run_bass_kernel_spmd

    I = {k: np.asarray(v) for k, v in inputs.items()}
    f32 = np.float32

    def col(v):
        return np.asarray(v, f32).reshape(-1, 1)

    def both(v):
        return np.concatenate([col(v), col(v)])

    def diag(w):
        z = np.zeros_like(w)
        return np.concatenate([np.concatenate([w, z], 1), np.concatenate([z, w], 1)], 0)

    i = np.arange(128)
    same_half = (i[:, None] // 64 == i[None] // 64)
    mean = (same_half / 64).astype(f32)
    center = (np.eye(128) - same_half / 64).astype(f32)
    r = np.arange(32)
    sum_c = ((i[:, None] // 64 == (r[None] % 16) // 8) / 64).astype(f32)
    sum_d = (i[:, None] // 8 == r[None] % 16).astype(f32)
    ysel = np.concatenate([(8 * j + i[:, None] // 16 == r[None]) for j in range(4)], 1).astype(f32)
    dup = -((i % 32) // 16).astype(f32).reshape(-1, 1)
    bsel = np.concatenate([(i[:, None] // 32 == g) & (i[:, None] % 16 == i[None] // 8) for g in range(4)], 1)
    r96 = np.arange(96)
    rsel = np.concatenate([r96[:, None] % 32 == 8 * j + i[None] // 16 for j in range(4)], 1)
    r128 = np.arange(128)
    dsel = np.concatenate([np.tile(((r128[:, None] < 64) & (r128[:, None] % 32 == 16 * q + e)), (1, 128))
                           for e in range(EXPERTS) for q in range(2)], 1)
    ident = np.eye(128)

    def ph(w):
        return w.reshape((HEADS, SP) + w.shape[1:]).swapaxes(0, 1).reshape((DI,) + w.shape[1:])

    kv = I["L0_tok_Wkv"]
    pieces = {"mean": mean, "sum_c": sum_c, "sum_d": sum_d, "center": center, "ysel": ysel, "dup": dup,
              "wq": diag(I["L0_tok_Wq"].T), "wk": diag(kv[:64].T), "wv": diag(kv[64:].T),
              "proj": diag(I["L0_tok_proj_w"].T), "lnq_w": both(I["L0_tok_ln_q_w"]),
              "lnq_b": both(I["L0_tok_ln_q_b"]), "lnkv_w": both(I["L0_tok_ln_kv_w"]),
              "lnkv_b": both(I["L0_tok_ln_kv_b"]), "proj_b": both(I["L0_tok_proj_b"])}
    for d in "fb":
        a = {k[len("L0_attn_f_"):]: v for k, v in I.items() if k.startswith(f"L0_attn_{d}_")}
        xi_w, z_w = ph(a["in_proj_w"][:DI]).T, ph(a["in_proj_w"][DI:]).T
        zero = np.zeros_like(xi_w)
        top, bottom = (lambda w: np.concatenate([w, zero])), (lambda w: np.concatenate([zero, w]))
        xp, xb = a["x_proj_w"], a["x_proj_b"]
        rows = np.concatenate([ph(xp[:DI]), xp[DI:]])
        pieces |= {d + "_win": np.concatenate([top(xi_w), bottom(xi_w), top(z_w), bottom(z_w)], 1),
                   d + "_wx": ph(rows.T), d + "_wo": ph(a["out_proj_w"].T),
                   d + "_alog": a["A_log"].reshape(HEADS, SP, SN).swapaxes(1, 2).reshape(HEADS * SN, SP),
                   d + "_bxi": col(ph(a["in_proj_b"][:DI])), d + "_bz": col(ph(a["in_proj_b"][DI:])),
                   d + "_bdt": col(ph(xb[:DI])), d + "_dtb": col(ph(a["dt_bias"])),
                   d + "_bB": col(xb[DI:2 * DI]), d + "_bC": col(xb[2 * DI:]), d + "_skip": np.diag(ph(a["D_skip"])),
                   d + "_bo": both(a["out_proj_b"])}
    conv = I["L0_attn_conv_w"].reshape(C, 3)
    pieces |= {"norm_w": both(I["L0_attn_norm_w"]), "norm_b": both(I["L0_attn_norm_b"]),
               "conv_w": np.concatenate([conv, conv]), "conv_b": both(I["L0_attn_conv_b"]),
               "gate": diag(I["L0_ffn_gate_w"]), "gate_b": np.tile(I["L0_ffn_gate_b"].reshape(1, -1), (128, 1)),
               "rank": np.tile(np.arange(EXPERTS, 0, -1).astype(f32).reshape(1, -1), (128, 1))}
    params = np.concatenate([pieces[name] for name, _ in PARTS], 1).astype(f32)

    x = I["x"].reshape(GROUPS, HALVES, 2, C, T // 16, STRIDE, 16, STRIDE)
    x = x.transpose(0, 2, 1, 3, 5, 7, 4, 6).reshape(STEPS, 128, PIX)
    moe = [np.concatenate([w, w]) for w in (I["L0_ffn_w1"].transpose(1, 0, 2).reshape(C, -1),
                                            I["L0_ffn_w2"].transpose(1, 0, 2).reshape(C, -1))]
    arrays = {"xin": np.ascontiguousarray(x), "params": params,
              "bsel": bsel.astype(np.float16), "rsel": rsel.astype(mybir.dt.np(BF16)),
              "ffn16": np.concatenate([dsel, ident], 1).astype(np.float16),
              "wmoe": np.concatenate(moe, 1),
              "w3": np.ascontiguousarray(I["L0_ffn_w3"].transpose(1, 0, 2).reshape(HID, -1))}

    nc = bacc.Bacc("TRN2", target_bir_lowering=False, num_devices=1)
    aps = [nc.dram_tensor("in_" + k, v.shape, mybir.dt.from_np(v.dtype), kind="ExternalInput").ap() for k, v in arrays.items()]
    out = nc.dram_tensor("out", (128, COLS), F32, kind="ExternalOutput").ap()
    program(nc, *aps, out)
    got = run_bass_kernel_spmd(nc, [{"in_" + k: v for k, v in arrays.items()}], core_ids=[0]).results[0]["out"]
    return got.reshape(HALVES, C, GROUPS, 2, T).transpose(2, 0, 3, 4, 1).reshape(BATCH, T, C)
```
